# Optimizing a Trainium2 kernel written in Bass

```python
import numpy as np
import jax
import jax.numpy as jnp

def _softmax(x, axis=-1):
    return jax.nn.softmax(x, axis=axis)

def _gelu(x):
    return jax.nn.gelu(x, approximate=True)

def _silu(x):
    return jax.nn.silu(x)

def _sigmoid(x):
    return jax.nn.sigmoid(x)

def _layernorm(x, axis=-1, eps=1e-05):
    m = jnp.mean(x, axis=axis, keepdims=True)
    v = jnp.var(x, axis=axis, keepdims=True)
    return (x - m) / jnp.sqrt(v + eps)

def _scatter_add(tgt, idx, src, axis=0):
    return tgt.at[idx].add(src)

def _segment_sum(src, seg, n):
    return jax.ops.segment_sum(src, seg, n)
kernel_name = 'mk_xattn_ffn_d2_seqx_r4_dc2b4e'

def setup_inputs(seed: int=0):
    np.random.seed(seed)
    _w = jnp.asarray

    def _rec_inputs():
        import jax
        import jax.numpy as jnp
        _rk = jax.random.key(seed)
        x = -0.0002928 + 1 * jax.random.normal(jax.random.fold_in(_rk, 1), (8, 256, 256), jnp.float32)
        _lenS = 256 - jax.random.randint(jax.random.fold_in(_rk, 7), (8,), 0, max(1, 256 // 4) + 1, jnp.int32)
        _lenS2 = 256 - jax.random.randint(jax.random.fold_in(_rk, 8), (8,), 0, max(1, 256 // 4) + 1, jnp.int32)
        _ctx_1024P = jax.random.normal(jax.random.fold_in(_rk, 11), (8, 16, 256), jnp.float32)
        _ctx_1024c = jax.random.dirichlet(jax.random.fold_in(_rk, 511), 0.3 * jnp.ones((16,), jnp.float32), (8, 256))
        _ctx_1024t = jnp.einsum('bsk,bkd->bsd', _ctx_1024c, _ctx_1024P)
        _ctx_1024t = _ctx_1024t * jax.lax.rsqrt(jnp.mean(jnp.square(_ctx_1024t)) + 1e-12) * 0.953939
        ctx_1024 = -1.39393e-06 + 0.999914 * (_ctx_1024t + 0.3 * jax.random.normal(jax.random.fold_in(_rk, 611), (8, 256, 256), jnp.float32))
        return (x, ctx_1024)
    x, ctx_1024 = _rec_inputs()

    def _L0_xattn_setup():
        import jax, jax.numpy as jnp
        import numpy as np
        D_MODEL = 256
        HEADS = 16
        HEAD_DIM = D_MODEL // HEADS
        key = jax.random.key(seed)
        ks = jax.random.split(key, 11)
        B, S = (2, 512)
        scale = 1.0 / np.sqrt(D_MODEL)
        inp = {'q': jax.random.normal(ks[0], (B, S, D_MODEL), jnp.float32), 'k': jax.random.normal(ks[1], (B, S, D_MODEL), jnp.float32), 'v': jax.random.normal(ks[2], (B, S, D_MODEL), jnp.float32), 'Wq': jax.random.normal(ks[3], (D_MODEL, D_MODEL), jnp.float32) * scale, 'bq': jax.random.normal(ks[4], (D_MODEL,), jnp.float32) * scale, 'Wk': jax.random.normal(ks[5], (D_MODEL, D_MODEL), jnp.float32) * scale, 'bk': jax.random.normal(ks[6], (D_MODEL,), jnp.float32) * scale, 'Wv': jax.random.normal(ks[7], (D_MODEL, D_MODEL), jnp.float32) * scale, 'bv': jax.random.normal(ks[8], (D_MODEL,), jnp.float32) * scale, 'Wo': jax.random.normal(ks[9], (D_MODEL, D_MODEL), jnp.float32) * scale, 'bo': jax.random.normal(ks[10], (D_MODEL,), jnp.float32) * scale}
        return inp
    _L0_xattn_all = _L0_xattn_setup()
    _L0_xattn_in = {k: v for k, v in _L0_xattn_all.items() if k in ('Wq', 'bq', 'Wk', 'bk', 'Wv', 'bv', 'Wo', 'bo')}
    del _L0_xattn_all

    def _L0_ffn_setup():
        import jax, jax.numpy as jnp
        import numpy as np
        E = 8
        H = 256
        I = 256
        TOPK = 2
        key = jax.random.key(seed)
        k1, k2, k3, k4 = jax.random.split(key, 4)
        hidden_states = jax.random.normal(k1, (2, 256, H), dtype=jnp.float32)
        router_weight = jax.random.normal(k2, (E, H), dtype=jnp.float32) * 0.02
        w1 = jax.random.normal(k3, (E, 2 * I, H), dtype=jnp.float32) * 0.02
        w2 = jax.random.normal(k4, (E, H, I), dtype=jnp.float32) * 0.02
        return {'hidden_states': hidden_states, 'router_weight': router_weight, 'w1': w1, 'w2': w2}
    _L0_ffn_all = _L0_ffn_setup()
    _L0_ffn_in = {k: v for k, v in _L0_ffn_all.items() if k in ('router_weight', 'w1', 'w2')}
    del _L0_ffn_all

    def _L1_xattn_setup():
        import jax, jax.numpy as jnp
        import numpy as np
        B, SQ, SK, HID, NH = (4, 512, 512, 256, 16)
        HD = HID // NH

        def _heads(x):
            b, s, _ = x.shape
            return x.reshape(b, s, NH, HD).transpose(0, 2, 1, 3)
        key = jax.random.key(seed)
        ks = jax.random.split(key, 8)
        s = 1.0 / np.sqrt(HID)
        return {'hidden_states': jax.random.normal(ks[0], (B, SQ, HID), jnp.float32), 'context': jax.random.normal(ks[1], (B, SK, HID), jnp.float32), 'Wq': jax.random.normal(ks[2], (HID, HID), jnp.float32) * s, 'bq': jnp.zeros((HID,), jnp.float32), 'Wk': jax.random.normal(ks[3], (HID, HID), jnp.float32) * s, 'bk': jnp.zeros((HID,), jnp.float32), 'Wv': jax.random.normal(ks[4], (HID, HID), jnp.float32) * s, 'bv': jnp.zeros((HID,), jnp.float32)}
    _L1_xattn_all = _L1_xattn_setup()
    _L1_xattn_in = {k: v for k, v in _L1_xattn_all.items() if k in ('Wq', 'bq', 'Wk', 'bk', 'Wv', 'bv')}
    del _L1_xattn_all

    def _L1_ffn_setup():
        import jax, jax.numpy as jnp
        import numpy as np
        B, S, H, E, I, MAX_K, A_HID = (2, 512, 256, 8, 672, 6, 50)
        key = jax.random.key(seed)
        ks = jax.random.split(key, 10)
        sc = 0.02
        return {'hidden_states': jax.random.normal(ks[0], (B, S, H), dtype=jnp.float32), 'router_w': jax.random.normal(ks[1], (E, H), dtype=jnp.float32) * sc, 'actor_w1': jax.random.normal(ks[2], (A_HID, H), dtype=jnp.float32) * sc, 'actor_b1': jnp.zeros((A_HID,), dtype=jnp.float32), 'actor_w2': jax.random.normal(ks[3], (MAX_K, A_HID), dtype=jnp.float32) * sc, 'actor_b2': jnp.zeros((MAX_K,), dtype=jnp.float32), 'gate_w': jax.random.normal(ks[4], (E, I, H), dtype=jnp.float32) * sc, 'up_w': jax.random.normal(ks[5], (E, I, H), dtype=jnp.float32) * sc, 'down_w': jax.random.normal(ks[6], (E, H, I), dtype=jnp.float32) * sc}
    _L1_ffn_all = _L1_ffn_setup()
    _L1_ffn_in = {k: v for k, v in _L1_ffn_all.items() if k in ('router_w', 'actor_w1', 'actor_b1', 'actor_w2', 'actor_b2', 'gate_w', 'up_w', 'down_w')}
    del _L1_ffn_all
    return {'x': x, 'ctx_1024': ctx_1024, 'L0_xattn_Wq': _L0_xattn_in['Wq'], 'L0_xattn_bq': _L0_xattn_in['bq'], 'L0_xattn_Wk': _L0_xattn_in['Wk'], 'L0_xattn_bk': _L0_xattn_in['bk'], 'L0_xattn_Wv': _L0_xattn_in['Wv'], 'L0_xattn_bv': _L0_xattn_in['bv'], 'L0_xattn_Wo': _L0_xattn_in['Wo'], 'L0_xattn_bo': _L0_xattn_in['bo'], 'L0_ffn_router_weight': _L0_ffn_in['router_weight'], 'L0_ffn_w1': _L0_ffn_in['w1'], 'L0_ffn_w2': _L0_ffn_in['w2'], 'L1_xattn_Wq': _L1_xattn_in['Wq'], 'L1_xattn_bq': _L1_xattn_in['bq'], 'L1_xattn_Wk': _L1_xattn_in['Wk'], 'L1_xattn_bk': _L1_xattn_in['bk'], 'L1_xattn_Wv': _L1_xattn_in['Wv'], 'L1_xattn_bv': _L1_xattn_in['bv'], 'L1_ffn_router_w': _L1_ffn_in['router_w'], 'L1_ffn_actor_w1': _L1_ffn_in['actor_w1'], 'L1_ffn_actor_b1': _L1_ffn_in['actor_b1'], 'L1_ffn_actor_w2': _L1_ffn_in['actor_w2'], 'L1_ffn_actor_b2': _L1_ffn_in['actor_b2'], 'L1_ffn_gate_w': _L1_ffn_in['gate_w'], 'L1_ffn_up_w': _L1_ffn_in['up_w'], 'L1_ffn_down_w': _L1_ffn_in['down_w']}

def reference(x, ctx_1024, L0_xattn_Wq, L0_xattn_bq, L0_xattn_Wk, L0_xattn_bk, L0_xattn_Wv, L0_xattn_bv, L0_xattn_Wo, L0_xattn_bo, L0_ffn_router_weight, L0_ffn_w1, L0_ffn_w2, L1_xattn_Wq, L1_xattn_bq, L1_xattn_Wk, L1_xattn_bk, L1_xattn_Wv, L1_xattn_bv, L1_ffn_router_w, L1_ffn_actor_w1, L1_ffn_actor_b1, L1_ffn_actor_w2, L1_ffn_actor_b2, L1_ffn_gate_w, L1_ffn_up_w, L1_ffn_down_w):
    import jax
    import jax.numpy as jnp

    def _L0_xattn_ref(q, k, v, Wq, bq, Wk, bk, Wv, bv, Wo, bo):
        import jax, jax.numpy as jnp
        import numpy as np
        D_MODEL = 256
        HEADS = 16
        HEAD_DIM = D_MODEL // HEADS
        B, S, _ = q.shape
        inv_sqrt_d = 1.0 / np.sqrt(HEAD_DIM).astype(np.float32)

        def split_heads(x):
            return x.reshape(B, S, HEADS, HEAD_DIM).transpose(0, 2, 1, 3)
        qw = split_heads(q @ Wq + bq)
        kw = split_heads(k @ Wk + bk)
        vw = split_heads(v @ Wv + bv)
        scores = jnp.einsum('bhqd,bhkd->bhqk', qw, kw) * inv_sqrt_d
        weights = jax.nn.softmax(scores, axis=-1)
        ctx = jnp.einsum('bhqk,bhkd->bhqd', weights, vw)
        ctx = ctx.transpose(0, 2, 1, 3).reshape(B, S, D_MODEL)
        return ctx @ Wo + bo

    def _L0_ffn_ref(hidden_states, router_weight, w1, w2):
        import jax, jax.numpy as jnp
        import numpy as np
        E = 8
        H = 256
        I = 256
        TOPK = 2
        orig_shape = hidden_states.shape
        h = hidden_states.reshape(-1, H)
        T = h.shape[0]
        logits = h @ router_weight.T
        top_logits, top_idx = jax.lax.top_k(logits, TOPK)
        scores = jax.nn.softmax(top_logits.astype(jnp.float32), axis=-1)
        combine = jnp.zeros((T, E), dtype=jnp.float32)
        combine = combine.at[jnp.arange(T)[:, None], top_idx].add(scores)
        out = jnp.zeros((T, H), dtype=h.dtype)
        for e in range(E):
            gu = h @ w1[e].T
            gate, up = (gu[:, :I], gu[:, I:])
            inter = jax.nn.silu(gate) * up
            out = out + combine[:, e:e + 1] * (inter @ w2[e].T)
        return out.reshape(orig_shape)

    def _L1_xattn_ref(hidden_states, context, Wq, bq, Wk, bk, Wv, bv):
        import jax, jax.numpy as jnp
        import numpy as np
        B, SQ, SK, HID, NH = (4, 512, 512, 256, 16)
        HD = HID // NH

        def _heads(x):
            b, s, _ = x.shape
            return x.reshape(b, s, NH, HD).transpose(0, 2, 1, 3)
        q = _heads(hidden_states @ Wq + bq)
        k = _heads(context @ Wk + bk)
        v = _heads(context @ Wv + bv)
        scores = jnp.einsum('bhqd,bhkd->bhqk', q, k) / jnp.sqrt(jnp.float32(HD))
        probs = jax.nn.softmax(scores, axis=-1)
        ctx = jnp.einsum('bhqk,bhkd->bhqd', probs, v)
        return ctx.transpose(0, 2, 1, 3).reshape(hidden_states.shape[0], -1, NH * HD)

    def _L1_ffn_ref(hidden_states, router_w, actor_w1, actor_b1, actor_w2, actor_b2, gate_w, up_w, down_w):
        import jax, jax.numpy as jnp
        import numpy as np
        B, S, H, E, I, MAX_K, A_HID = (2, 512, 256, 8, 672, 6, 50)
        probs = jax.nn.softmax(jnp.einsum('bsh,eh->bse', hidden_states, router_w).astype(jnp.float32), axis=-1)
        a_h = jax.nn.gelu(jnp.einsum('bsh,ah->bsa', hidden_states, actor_w1) + actor_b1)
        actor_logits = jnp.clip(jnp.einsum('bsa,ka->bsk', a_h, actor_w2) + actor_b2, -30.0, 30.0)
        sampled_k = jnp.argmax(actor_logits, axis=-1) + 1
        order = jnp.argsort(-probs, axis=-1)
        rank = jnp.argsort(order, axis=-1)
        mask = rank < sampled_k[..., None]
        scores = jnp.where(mask, probs, 0.0).astype(hidden_states.dtype)
        out = jnp.zeros_like(hidden_states)
        for e in range(E):
            g = jnp.einsum('bsh,ih->bsi', hidden_states, gate_w[e])
            u = jnp.einsum('bsh,ih->bsi', hidden_states, up_w[e])
            y = jnp.einsum('bsi,hi->bsh', jax.nn.silu(g) * u, down_w[e])
            out = out + scores[..., e:e + 1] * y
        return out
    x = x + _L0_xattn_ref(_layernorm(x, axis=-1), ctx_1024, ctx_1024, L0_xattn_Wq, L0_xattn_bq, L0_xattn_Wk, L0_xattn_bk, L0_xattn_Wv, L0_xattn_bv, L0_xattn_Wo, L0_xattn_bo)
    x = x + _L0_ffn_ref(_layernorm(x, axis=-1), L0_ffn_router_weight, L0_ffn_w1, L0_ffn_w2)
    x = x + _L1_xattn_ref(_layernorm(x, axis=-1), ctx_1024, L1_xattn_Wq, L1_xattn_bq, L1_xattn_Wk, L1_xattn_bk, L1_xattn_Wv, L1_xattn_bv)
    x = x + _L1_ffn_ref(_layernorm(x, axis=-1), L1_ffn_router_w, L1_ffn_actor_w1, L1_ffn_actor_b1, L1_ffn_actor_w2, L1_ffn_actor_b2, L1_ffn_gate_w, L1_ffn_up_w, L1_ffn_down_w)
    return x

_drawn_inputs = setup_inputs


def setup_inputs(seed=0):
    import zlib

    import numpy as np

    out = dict(_drawn_inputs(seed))
    spreads = {'L1_xattn_bq': (0.0, 0.474),
     'L1_xattn_bk': (0.0, 0.8),
     'L1_xattn_bv': (0.0, 0.1),
     'L1_ffn_actor_b1': (0.0, 0.1),
     'L1_ffn_actor_b2': (0.0, 0.8)}
    factors = {'L0_xattn_bq': 5.271,
     'L0_xattn_bk': 8.0,
     'L0_ffn_router_weight': 6.666,
     'L0_ffn_w1': 5.807,
     'L0_ffn_w2': 5.821,
     'L1_ffn_router_w': 8.0,
     'L1_ffn_gate_w': 8.0,
     'L1_ffn_up_w': 8.0,
     'L1_ffn_down_w': 8.0}
    for name, (base, spread) in spreads.items():
        noise = np.random.default_rng([zlib.crc32(name.encode()), seed]).standard_normal(out[name].shape)
        drawn = base * np.exp(spread * noise) if base else spread * noise
        out[name] = jnp.asarray(drawn.astype(out[name].dtype))
    for name, factor in factors.items():
        out[name] = (out[name] * factor).astype(out[name].dtype)
    return out
```

```python
import concourse.bass as bass
from concourse import mybir
from contextlib import ExitStack

F32 = mybir.dt.float32
F32R = mybir.dt.float32r
I32 = mybir.dt.int32
ALU = mybir.AluOpType
ACT = mybir.ActivationFunctionType
AXX = mybir.AxisListType.X

P = 128
B, S, D = 8, 256, 256
T = B * S
NT = T // P
TB = S // P
FC = D // P
NH, HD = 16, 16
NP = NH // 2
KR = 3 * HD
VW = 32
EPS = 1e-5
SCORE_SCALE = 0.25
NBUF = 4
LEAD = 12


class Mem:

    held = []

    def __init__(self, nc, tag):
        self.nc, self.tag, self.stack = nc, tag, ExitStack()

    def __enter__(self):
        return self

    def __exit__(self, *a):
        self.stack.close()

    def sb(self, name, shape, dt=F32):
        return self.stack.enter_context(self.nc.sbuf_tensor(f"{self.tag}_{name}", shape, dt))

    def ps(self, name, shape, dt=F32):
        return self.stack.enter_context(self.nc.psum_tensor(f"{self.tag}_{name}", shape, dt))

    def sem(self, name):
        Mem.held.append(self.nc.alloc_semaphore(f"{self.tag}_{name}"))
        return Mem.held[-1]

    @staticmethod
    def release(nc):
        nc.clear_and_free_semaphores(Mem.held)
        Mem.held = []
        nc.all_engine_barrier()

    def sems(self, name, n=2):
        return [self.sem(f"{name}{i}") for i in range(n)]


class Chain:

    def __init__(self, eng, sem):
        self.eng, self.sem, self.n = eng, sem, 0

    def step(self, ins):
        self.n += 1
        ins.then_inc(self.sem, 1)

    def wait(self):
        self.eng.wait_ge(self.sem, self.n)


def loop(eng, n, body):
    body(0)
    with eng.Fori(1, n) as i:
        body(i)


def wait(eng, sem, value):
    if not (isinstance(value, int) and value <= 0):
        eng.wait_ge(sem, value)


class Norm:

    def __init__(self, m):
        self.st = m.sb("st", [P, NT, 6])
        self.mv = m.sb("mv", [P, NT, 2])
        self.ve = m.sb("ve", [P, NT])
        self.root_sb = m.sb("root", [P, NT])
        self.y = m.sb("y", [P, NT])
        self.z = m.sb("z", [P, NT])
        self.rstd = m.sb("rstd", [P, NT])
        self.stats, self.aggr, self.steps, self.rooted = (m.sem(n) for n in ("stats", "aggr", "steps", "rooted"))

    def statistics(self, dve, x_sb):
        with dve.Fori(0, NT) as t:
            dve.bn_stats(self.st[:, bass.ds(t, 1), :].rearrange("p a s -> p (a s)"),
                         x_sb[:, bass.ds(t, 1), :].rearrange("p a d -> p (a d)")).then_inc(self.stats, 1)
        dve.wait_ge(self.stats, NT)
        for t in range(NT):
            dve.bn_aggr(self.mv[:, t, :], self.st[:, t, :]).then_inc(self.aggr, 1)
        dve.wait_ge(self.aggr, NT)
        dve.tensor_scalar(self.ve[:], self.mv[:, :, 1], EPS, None, ALU.add).then_inc(self.steps, 1)
        dve.wait_ge(self.rooted, 1)
        dve.reciprocal(self.y[:], self.root_sb[:]).then_inc(self.steps, 1)
        dve.wait_ge(self.steps, 2)
        dve.tensor_tensor(self.z[:], self.y[:], self.y[:], ALU.mult).then_inc(self.steps, 1)
        dve.wait_ge(self.steps, 3)
        dve.tensor_tensor(self.z[:], self.z[:], self.ve[:], ALU.mult).then_inc(self.steps, 1)
        dve.wait_ge(self.steps, 4)
        dve.tensor_scalar(self.z[:], self.z[:], -0.5, 1.5, ALU.mult, ALU.add).then_inc(self.steps, 1)
        dve.wait_ge(self.steps, 5)
        dve.tensor_tensor(self.rstd[:], self.z[:], self.y[:], ALU.mult).then_inc(self.steps, 1)
        dve.wait_ge(self.steps, 6)

    def root(self, act):
        act.wait_ge(self.steps, 1)
        act.activation(self.root_sb[:], self.ve[:], ACT.Sqrt).then_inc(self.rooted, 1)


def constants(nc, ident, x_sb, c_sb, va, x_in, ctx_t):
    with Mem(nc, "init") as m:
        loaded, zeroed, va_zeroed = m.sem("loaded"), m.sem("zeroed"), m.sem("va_zeroed")
        with nc.Block() as block:
            @block.sync
            def _(sp):
                sp.dma_start(x_sb[:], x_in.rearrange("(n p) d -> p n d", p=P)).then_inc(loaded, 16)
                sp.dma_start(c_sb[:], ctx_t.rearrange("(c p) t -> p c t", p=P)).then_inc(loaded, 16)
                sp.wait_ge(loaded, 32)

            @block.gpsimd
            def _(pool):
                pool.memset(ident[:], 0.0).then_inc(zeroed, 1)
                pool.wait_ge(zeroed, 1)
                pool.affine_select(out=ident[:], in_=ident[:], compare_op=ALU.not_equal, fill=1.0, base=0,
                                   pattern=[[-1, P]], channel_multiplier=1)

            @block.vector
            def _(dve):
                dve.memset(va[:], 0.0).then_inc(va_zeroed, 1)
                dve.wait_ge(va_zeroed, 1)
                dve.memset(va[:, :, :, HD:HD + 1], 1.0)


def split_weights(nc, tag, raws, his, los, srcs):
    with Mem(nc, tag) as m:
        loaded = m.sems("loaded", len(srcs))
        rounded = m.sem("rounded")
        with nc.Block() as block:
            @block.sync
            def _(sp):
                for raw, src, done in zip(raws, srcs, loaded):
                    sp.dma_start(raw, src).then_inc(done, 16)

            @block.vector
            def _(dve):
                for n, (raw, hi, lo) in enumerate(zip(raws, his, los)):
                    dve.wait_ge(loaded[n], 16)
                    dve.tensor_copy(hi, raw).then_inc(rounded, 1)
                    dve.wait_ge(rounded, n + 1)
                    dve.tensor_tensor(lo, raw, hi, ALU.subtract)


def three_products(pe, out, lhs, rhs, terms, start, stop):
    n = len(terms)
    for a, t in enumerate(terms):
        lh, ll = lhs[0](t), lhs[1](t)
        rh, rl = rhs[0](t), rhs[1](t)
        pe.matmul(out, lh, rh, start=start and a == 0, stop=False)
        pe.matmul(out, ll, rh, start=False, stop=False)
        last = pe.matmul(out, lh, rl, start=False, stop=stop and a == n - 1)
    return last


def project(nc, tag, x_sb, c_sb, va, ident, w, bqk, bv, parts):
    with Mem(nc, tag) as m:
        wqh, wql, wkh, wkl, wvh, wvl = w
        bvb = m.sb("bvb", [P, D])
        bqk_sb = m.sb("bqk", [P, 4])
        xn = [m.sb(f"xn{u}", [P, TB, D]) for u in range(2)]
        norm = Norm(m)
        xh = [m.sb(f"xh{u}", [P, FC, S], F32R) for u in range(2)]
        xl = [m.sb(f"xl{u}", [P, FC, S], F32R) for u in range(2)]
        ch = [m.sb(f"ch{u}", [P, FC, S], F32R) for u in range(2)]
        cl = [m.sb(f"cl{u}", [P, FC, S], F32R) for u in range(2)]
        qkh = [[m.sb(f"{n}h{u}", [P, 2, S], F32R) for u in range(2)] for n in "qk"]
        qkl = [[m.sb(f"{n}l{u}", [P, 2, S], F32R) for u in range(2)] for n in "qk"]
        pt = [m.ps(f"pt{u}", [P, FC, S]) for u in range(2)]
        pq = [[m.ps(f"p{n}{u}", [P, 2, S]) for u in range(2)] for n in "qk"]
        pv = [m.ps(f"pv{u}", [P, TB, D]) for u in range(2)]

        biases = m.sem("biases")
        ln = m.sem("ln")
        xn_ready, xt_ready = m.sems("xn_ready"), m.sems("xt_ready")
        xh_ready, xl_ready = m.sems("xh_ready"), m.sems("xl_ready")
        ch_ready, cl_ready = m.sems("ch_ready"), m.sems("cl_ready")
        mm_ready = [m.sems("q_mm"), m.sems("k_mm")]
        v_mm = m.sems("v_mm")
        hi_ready = [m.sems("qh_ready"), m.sems("kh_ready")]
        lo_ready = [m.sems("ql_ready"), m.sems("kl_ready")]
        v_ready = m.sems("v_ready")
        stored = [m.sems("q_stored"), m.sems("k_stored")]

        with nc.Block() as block:
            @block.sync
            def _(sp):
                sp.dma_start(bvb[:], bv.partition_broadcast(P)).then_inc(biases, 16)
                sp.dma_start(bqk_sb[:], bqk).then_inc(biases, 16)
                def batches(i):
                    for u in range(2):
                        for n in (1, 0):
                            for src, dst, ready in ((qkh[n][u], parts[2 * n], hi_ready[n][u]),
                                                    (qkl[n][u], parts[2 * n + 1], lo_ready[n][u])):
                                sp.wait_ge(ready, 2 * i + 2)
                                sp.dma_start(dst[bass.ds(2 * i + u, 1)].rearrange("a j r s -> r (a j) s"),
                                             src[:].bitcast(F32)).then_inc(stored[n][u], 16)
                loop(sp, B // 2, batches)
                for n in range(2):
                    for u in range(2):
                        sp.wait_ge(stored[n][u], 32 * (B // 2))

            @block.gpsimd
            def _(pool):
                for b in range(B):
                    u, i = b % 2, b // 2
                    wait(pool, v_mm[u], i)
                    c = c_sb[:, :, b * S:(b + 1) * S]
                    pool.tensor_copy(ch[u][:], c).then_inc(ch_ready[u], 1)
                    pool.wait_ge(ch_ready[u], i + 1)
                    pool.tensor_tensor(cl[u][:], c, ch[u][:], ALU.subtract).then_inc(cl_ready[u], 1)

            @block.vector
            def _(dve):
                norm.statistics(dve, x_sb)
                dve.wait_ge(biases, 32)

                def normalise(i, u):
                    wait(dve, xt_ready[u], i)
                    for t in range(TB):
                        tile = 2 * (2 * i + u) + t
                        dve.tensor_scalar(xn[u][:, t, :], x_sb[:, bass.ds(tile, 1), :].rearrange("p a d -> p (a d)"),
                                          norm.mv[:, bass.ds(tile, 1), 0], norm.rstd[:, bass.ds(tile, 1)],
                                          ALU.subtract, ALU.mult).then_inc(xn_ready[u], 1)

                def low(i, u, n):
                    for j in range(2):
                        dve.wait_ge(hi_ready[n][u], 2 * i + 2)
                        if j == 0:
                            wait(dve, stored[n][u], 32 * i)
                        dve.scalar_tensor_tensor(out=qkl[n][u][:, j, :], in0=pq[n][u][:, j, :],
                                                 scalar=bqk_sb[:, 2 * n + j:2 * n + j + 1], in1=qkh[n][u][:, j, :],
                                                 op0=ALU.add, op1=ALU.subtract).then_inc(lo_ready[n][u], 1)

                def batches(i):
                    for u in range(2):
                        normalise(i, u)
                        dve.wait_ge(xh_ready[u], i + 1)
                        dve.tensor_tensor(xl[u][:], pt[u][:], xh[u][:], ALU.subtract).then_inc(xl_ready[u], 1)
                        low(i, u, 1)
                        dve.wait_ge(v_mm[u], i + 1)
                        for t in range(TB):
                            dve.tensor_tensor(
                                va[:, bass.ds(2 * (2 * i + u) + t, 1), :, 0:HD].rearrange("p a h d -> p (a h) d"),
                                pv[u][:, t, :].rearrange("p (h d) -> p h d", h=NH),
                                bvb[:].rearrange("p (h d) -> p h d", h=NH), ALU.add).then_inc(v_ready[u], 1)
                        low(i, u, 0)

                loop(dve, B // 2, batches)

            @block.scalar
            def _(act):
                norm.root(act)
                act.wait_ge(biases, 32)
                def batches(i):
                    for u in range(2):
                        act.wait_ge(xt_ready[u], i + 1)
                        wait(act, mm_ready[0][u], i)
                        act.activation(xh[u][:], pt[u][:], ACT.Copy).then_inc(xh_ready[u], 1)
                        for n in (1, 0):
                            act.wait_ge(mm_ready[n][u], i + 1)
                            wait(act, stored[n][u], 32 * i)
                            for j in range(2):
                                act.activation(qkh[n][u][:, j, :], pq[n][u][:, j, :], ACT.Identity,
                                               bias=bqk_sb[:, 2 * n + j:2 * n + j + 1]).then_inc(hi_ready[n][u], 1)

                loop(act, B // 2, batches)

            @block.tensor
            def _(pe):
                def batches(i):
                    for u in range(2):
                        pe.wait_ge(xn_ready[u], 2 * i + 2)
                        wait(pe, xl_ready[u], i)
                        for t in range(TB):
                            for c in range(FC):
                                last = pe.transpose(pt[u][:, c, t * P:(t + 1) * P], xn[u][:, t, c * P:(c + 1) * P], ident[:])
                        last.then_inc(xt_ready[u], 1)
                        pe.wait_ge(cl_ready[u], i + 1)

                        def qk(n, wh, wl, ah, al):
                            wait(pe, lo_ready[n][u], 2 * i)
                            for j in range(2):
                                last = three_products(
                                    pe, pq[n][u][:, j, :],
                                    (lambda c: wh[:, c, j * P:(j + 1) * P], lambda c: wl[:, c, j * P:(j + 1) * P]),
                                    (lambda c: ah[:, c, :], lambda c: al[:, c, :]), range(FC), True, True)
                            last.then_inc(mm_ready[n][u], 1)

                        qk(1, wkh, wkl, ch[u], cl[u])
                        wait(pe, v_ready[u], 2 * i)
                        for t in range(TB):
                            last = three_products(
                                pe, pv[u][:, t, :],
                                (lambda c: ch[u][:, c, t * P:(t + 1) * P], lambda c: cl[u][:, c, t * P:(t + 1) * P]),
                                (lambda c: wvh[:, c, :], lambda c: wvl[:, c, :]), range(FC), True, True)
                        last.then_inc(v_mm[u], 1)
                        pe.wait_ge(xl_ready[u], i + 1)
                        qk(0, wqh, wql, xh[u], xl[u])

                loop(pe, B // 2, batches)


def attend(nc, tag, x_sb, ctx_sb, va, ident, parts, bias=None):
    SLOTS = B * NP
    with Mem(nc, tag) as m:
        qs = [m.sb(f"qs{n}", [P, NP, S], F32R) for n in range(NBUF)]
        ks = [m.sb(f"ks{n}", [P, NP, S], F32R) for n in range(NBUF)]
        pT = [m.sb(f"pT{n}", [P, 2, TB, S]) for n in range(4)]
        mx = [m.sb(f"mx{n}", [P, TB, NH]) for n in range(2)]
        nm = [m.sb(f"nm{n}", [NH, S], F32R) for n in range(2)]
        oT = [m.sb(f"oT{n}", [P, 2, 2 * S]) for n in range(2)]
        rs = m.sb("rs", [P, TB, NH])
        sc = [m.ps(f"sc{n}", [P, TB, S]) for n in range(2)]
        sT = [m.ps(f"sT{n}", [P, 2, 2 * S]) for n in range(2)]
        po = m.ps("po", [P, 2, S])
        pf = m.ps("pf", [P, 512])

        ones = m.sem("ones")
        q_in, k_in = m.sems("q_in", NBUF), m.sems("k_in", NBUF)
        sc_mm, sc_max = m.sem("sc_mm"), m.sem("sc_max")
        mT_mm, nm_made, m_in = m.sem("mT_mm"), m.sem("nm_made"), m.sems("m_in", NBUF)
        sT_mm, exped = m.sem("sT_mm"), m.sem("exped")
        pv_mm, o_out = m.sem("pv_mm"), m.sem("o_out")
        oT_mm, recip, normed = m.sem("oT_mm"), m.sem("recip"), m.sem("normed")
        bias_in, added = m.sem("bias_in"), m.sem("added")
        bias_sb = m.sb("bias", [P, D]) if bias is not None else None

        with nc.Block() as block:
            @block.sync
            def _(sp):
                if bias is not None:
                    sp.dma_start(bias_sb[:], bias.partition_broadcast(P)).then_inc(bias_in, 16)
                sp.wait_ge(ones, 2 * NBUF)

                def load(b):
                    n = b % NBUF
                    if b >= NBUF:
                        sp.wait_ge(sT_mm, NP * (b - NBUF + 1))
                    for dst, hi, lo, kinds, done in ((qs[n], parts[0], parts[1], (0, 0, 1), q_in[n]),
                                                     (ks[n], parts[2], parts[3], (0, 1, 0), k_in[n])):
                        for j in range(2):
                            for r, kind in enumerate(kinds):
                                src = (hi, lo)[kind][b, j].rearrange("(p d) s -> d p s", d=HD)
                                row = 64 * j + HD * r
                                sp.dma_start(dst[row:row + HD, :, :].bitcast(F32), src).then_inc(done, 16)

                def maxima(b):
                    n = b % NBUF
                    sp.wait_ge(nm_made, b + 1)
                    for j in range(2):
                        row = 64 * j + KR
                        sp.dma_start(qs[n][row:row + 1, :, :].bitcast(F32), nm[b % 2][NP * j:NP * j + NP, :].bitcast(F32)).then_inc(m_in[n], 16)

                load(0)
                load(1)
                for b in range(B):
                    if b + 2 < B:
                        load(b + 2)
                    maxima(b)

            @block.gpsimd
            def _(pool):
                for n in range(NBUF):
                    for j in range(2):
                        pool.memset(ks[n][64 * j + 32:64 * j + 64, :, :].bitcast(F32), 1.0).then_inc(ones, 1)
                pool.wait_ge(ones, 2 * NBUF)
                if bias is not None:
                    pool.wait_ge(bias_in, 16)
                for k in range(NT):
                    if bias is None:
                        pool.wait_ge(normed, k + 1)
                    pool.tensor_tensor(x_sb[:, k, :], x_sb[:, k, :],
                                       ctx_sb[:, k, :] if bias is None else bias_sb[:], ALU.add)

            @block.tensor
            def _(pe):
                def scores(n):
                    b, p = divmod(n, NP)
                    if p == 0:
                        pe.wait_ge(q_in[b % NBUF], 96 * (b // NBUF + 1))
                        pe.wait_ge(k_in[b % NBUF], 96 * (b // NBUF + 1))
                    for j in range(2):
                        rows = slice(64 * j, 64 * j + KR)
                        if n >= 1:
                            pe.wait_ge(sc_max, 2 * (n - 1) + j + 1)
                        for qt in range(TB):
                            last = pe.matmul(sc[j][:, qt, :], qs[b % NBUF][rows, p, qt * P:(qt + 1) * P],
                                             ks[b % NBUF][rows, p, :], start=True, stop=True)
                        last.then_inc(sc_mm, 1)

                def maxima_T(b):
                    pe.wait_ge(sc_max, 2 * NP * (b + 1))
                    for qt in range(TB):
                        last = pe.transpose(pf[0:NH, qt * P:(qt + 1) * P], mx[b % 2][:, qt, :], ident[:])
                    last.then_inc(mT_mm, 1)

                def scores_T(t):
                    b, p = divmod(t, NP)
                    if p == 0:
                        pe.wait_ge(m_in[b % NBUF], 32 * (b // NBUF + 1))
                    if t >= 2:
                        pe.wait_ge(exped, t - 1)
                    for j in range(2):
                        rows = slice(64 * j, 64 * j + KR + 1)
                        for kt in range(TB):
                            last = pe.matmul(sT[t % 2][:, j, kt * S:(kt + 1) * S],
                                             ks[b % NBUF][rows, p, kt * P:(kt + 1) * P],
                                             qs[b % NBUF][rows, p, :], start=True, stop=True)
                    last.then_inc(sT_mm, 1)

                def values(g):
                    b, gb = divmod(g, NP // 2)
                    pe.wait_ge(exped, 2 * g + 2)
                    if g % 2 == 0 and g >= 2:
                        pe.wait_ge(o_out, g // 2)
                    for kt in range(TB):
                        for c in range(4):
                            last = pe.matmul(po[32 * c:32 * c + VW, g % 2, :], va[:, TB * b + kt, 4 * gb + c, :],
                                             pT[(2 * g + c // 2) % 4][:, c % 2, kt, :],
                                             start=(kt == 0), stop=(kt == TB - 1))
                    last.then_inc(pv_mm, 1)

                def outputs_T(b, qt):
                    pe.wait_ge(o_out, 2 * b + 2)
                    for g in range(4):
                        last = pe.transpose(pf[:, g * P:(g + 1) * P],
                                            oT[b % 2][:, g // 2, (g % 2) * S + qt * P:(g % 2) * S + (qt + 1) * P], ident[:])
                    last.then_inc(oT_mm, 1)

                shared = None
                for what, k in pe_order(SLOTS):
                    if what in ("mT", "oT"):
                        if shared is not None:
                            pe.wait_ge(nm_made if shared[0] == "mT" else normed, shared[1] + 1)
                        shared = what, k
                    if what == "sT":
                        scores_T(k)
                    elif what == "sc":
                        scores(k)
                    elif what == "mT":
                        maxima_T(k)
                    elif what == "pv":
                        values(k)
                    else:
                        outputs_T(k // TB, k % TB)

            @block.vector
            def _(dve):
                for n in range(SLOTS + LEAD + 6):
                    if n < SLOTS:
                        b, p = divmod(n, NP)
                        for j in range(2):
                            dve.wait_ge(sc_mm, 2 * n + j + 1)
                            if p == 0 and j == 0 and b >= 2:
                                dve.wait_ge(mT_mm, b - 1)
                            dve.tensor_reduce(mx[b % 2][:, :, NP * j + p], sc[j][:], AXX, ALU.max).then_inc(sc_max, 1)
                    if n >= 9 and (n - 9) % NP == 0 and (n - 9) // NP < B:
                        b = (n - 9) // NP
                        dve.wait_ge(mT_mm, b + 1)
                        if b >= 2:
                            dve.wait_ge(m_in[(b - 2) % NBUF], 32 * ((b - 2) // NBUF + 1))
                        dve.tensor_scalar(nm[b % 2][:], pf[0:NH, 0:S], -1.0, None, ALU.mult).then_inc(nm_made, 1)
                    t = n - LEAD
                    for qt in range(TB):
                        if t >= NP + 3 + qt and (t - NP - 3 - qt) % NP == 0 and (t - NP - 3 - qt) // NP < B:
                            k = TB * ((t - NP - 3 - qt) // NP) + qt
                            o = pf[:].rearrange("p (h w) -> p h w", w=VW)
                            dve.wait_ge(oT_mm, k + 1)
                            if k >= 1:
                                dve.wait_ge(normed, k)
                            dve.reciprocal(rs[:, k % 2, :], o[:, :, HD]).then_inc(recip, 1)
                            dve.wait_ge(recip, k + 1)
                            dve.tensor_tensor(ctx_sb[:, k, :].rearrange("p (h d) -> p h d", h=NH), o[:, :, 0:HD],
                                              rs[:, k % 2, :].unsqueeze(2).to_broadcast([P, NH, HD]),
                                              ALU.mult).then_inc(normed, 1)

            @block.scalar
            def _(act):
                for t in range(SLOTS + 2):
                    if t < SLOTS:
                        act.wait_ge(sT_mm, t + 1)
                        if t >= 4:
                            act.wait_ge(pv_mm, (t - 4) // 2 + 1)
                        act.activation(pT[t % 4][:].rearrange("p a b s -> p a (b s)"), sT[t % 2][:], ACT.Exp,
                                       scale=SCORE_SCALE).then_inc(exped, 1)
                    if t >= 5 and (t - 5) % 4 == 0 and (t - 5) // 4 < 2 * B:
                        h = (t - 5) // 4
                        act.wait_ge(pv_mm, 2 * h + 2)
                        if h >= 4 and h % 2 == 0:
                            act.wait_ge(oT_mm, TB * (h // 2 - 1))
                        act.activation(oT[(h // 2) % 2][:, h % 2, :], po[:].rearrange("p g s -> p (g s)"),
                                       ACT.Copy).then_inc(o_out, 1)


def pe_order(slots):
    order = []
    for n in range(slots + LEAD + 6):
        t = n - LEAD
        if 0 <= t < slots:
            order.append(("sT", t))
        if n < slots:
            order.append(("sc", n))
        if n >= 9 and (n - 9) % NP == 0 and (n - 9) // NP < B:
            order.append(("mT", (n - 9) // NP))
        if t >= 3 and (t - 3) % 2 == 0 and (t - 3) // 2 < slots // 2:
            order.append(("pv", (t - 3) // 2))
        for qt in range(TB):
            k = t - NP - 3 - qt
            if k >= 0 and k % NP == 0 and k // NP < B:
                order.append(("oT", TB * (k // NP) + qt))
    return order


def project_out(nc, tag, x_sb, ctx_sb, ident, w):
    with Mem(nc, tag) as m:
        wh, wl = w
        ch = [m.sb(f"ch{u}", [P, FC, S], F32R) for u in range(2)]
        cl = [m.sb(f"cl{u}", [P, FC, S], F32R) for u in range(2)]
        pt = [m.ps(f"pt{u}", [P, FC, S]) for u in range(2)]
        po = [m.ps(f"po{u}", [P, TB, D]) for u in range(2)]
        t_mm, h_ready, l_ready = m.sems("t_mm"), m.sems("h_ready"), m.sems("l_ready")
        o_mm, added = m.sems("o_mm"), m.sems("added")
        with nc.Block() as block:
            @block.tensor
            def _(pe):
                for b in range(B + 1):
                    if b < B:
                        u, i = b % 2, b // 2
                        wait(pe, l_ready[u], i)
                        for t in range(TB):
                            for c in range(FC):
                                last = pe.transpose(pt[u][:, c, t * P:(t + 1) * P],
                                                    ctx_sb[:, TB * b + t, c * P:(c + 1) * P], ident[:])
                        last.then_inc(t_mm[u], 1)
                    if b >= 1:
                        u, i = (b - 1) % 2, (b - 1) // 2
                        pe.wait_ge(l_ready[u], i + 1)
                        wait(pe, added[u], i)
                        for t in range(TB):
                            last = three_products(
                                pe, po[u][:, t, :],
                                (lambda c: ch[u][:, c, t * P:(t + 1) * P], lambda c: cl[u][:, c, t * P:(t + 1) * P]),
                                (lambda c: wh[:, c, :], lambda c: wl[:, c, :]), range(FC), True, True)
                        last.then_inc(o_mm[u], 1)

            @block.scalar
            def _(act):
                for b in range(B):
                    u, i = b % 2, b // 2
                    act.wait_ge(t_mm[u], i + 1)
                    wait(act, o_mm[u], i)
                    act.activation(ch[u][:], pt[u][:], ACT.Copy).then_inc(h_ready[u], 1)

            @block.vector
            def _(dve):
                for b in range(B + 1):
                    if b < B:
                        u, i = b % 2, b // 2
                        dve.wait_ge(h_ready[u], i + 1)
                        dve.tensor_tensor(cl[u][:], pt[u][:], ch[u][:], ALU.subtract).then_inc(l_ready[u], 1)
                    if b >= 1:
                        u, i = (b - 1) % 2, (b - 1) // 2
                        dve.wait_ge(o_mm[u], i + 1)
                        x = x_sb[:, TB * (b - 1):TB * b, :]
                        dve.tensor_tensor(x, po[u][:], x, ALU.add).then_inc(added[u], 1)


NE = 8
PAIR = 2 * P
HI = T // P
COLS = 2 * NE * (T // PAIR)
PAD_COLS = COLS + HI
AK = 6
I0, I1, A1 = 256, 672, 50


class Tables:

    def __init__(self, m):
        self.gather = m.sb("gather_rows", [P, PAD_COLS], I32)
        self.scatter = m.sb("scatter_rows", [P, PAD_COLS], I32)
        self.weight = m.sb("slot_weight", [P, PAD_COLS])
        self.pairs = m.sb("pairs", [P, 2, NE], I32)


def route(nc, tag, x_sb, ident, tables, rows, acc, router, actor=None):
    A = actor["w1n"] if actor else 0
    R = NE + A
    with Mem(nc, tag) as m:
        norm = Norm(m)
        xn = m.sb("xn", [P, NT, D])
        xt = [m.sb(f"xt{u}", [P, FC, P]) for u in range(2)]
        rw = m.sb("rw", [P, FC, R])
        lg = m.sb("lg", [P, NT, R])
        big = [m.sb(f"big{n}", [P, NT, NE, NE]) for n in range(2)]
        V = m.sb("value", [P, NT, NE])
        W = m.sb("w", [P, NT, NE])
        M = m.sb("mask", [P, NT, NE])
        rank = m.sb("rank", [P, NT, NE])
        top = m.sb("top", [P, NT])
        tot = m.sb("tot", [P, NT])
        cum = [m.sb(f"cum{n}", [P, NT, NE]) for n in range(2)]
        slot = m.sb("slot", [P, NT, NE])
        sloti = m.sb("sloti", [P, NT, NE], I32)
        parti = m.sb("parti", [P, 2, NT, NE], I32)
        part = m.sb("part", [P, 2, NT, NE])
        cnt = m.sb("cnt", [P, NE])
        before = m.sb("before", [P, NE, NE])
        tril = m.sb("tril", [P, P])
        allone = m.sb("allone", [P, P])
        lanes = m.sb("lanes", [P, P])
        token = m.sb("token", [P, NT])
        spare = m.sb("spare", [P, 1])
        hot_lo = [m.sb(f"hot_lo{u}", [P, NE, P]) for u in range(2)]
        hot_hi = m.sb("hot_hi", [P, NT, NE, HI])
        kind = [m.sb(f"kind{u}", [P, NE, 2, HI]) for u in range(2)]
        packed = m.sb("packed", [P, 2, PAD_COLS])
        rowf = m.sb("rowf", [P, PAD_COLS])
        pt = [m.ps(f"pt{u}", [P, 512]) for u in range(2)]
        pl = [m.ps(f"pl{u}", [P, 512]) for u in range(2)]
        pcount = m.ps("pcount", [P, 2, NT, NE])
        ptab = m.ps("ptab", [P, NE, 2, HI])
        if actor:
            b1 = m.sb("b1", [P, A])
            b2 = m.sb("b2", [P, AK])
            w2 = m.sb("w2", [A, AK])
            ah = m.sb("ah", [P, NT, A])
            ag = m.sb("ag", [P, NT, A])
            at = m.sb("at", [A, NT, P])
            al = m.sb("al", [P, NT, AK])
            number = m.sb("number", [P, AK])
            pa = [m.ps(f"pa{u}", [P, 4, P]) for u in range(2)]

        zeros = m.sb("zeros", [P, NT + 1, D])
        zeroed = m.sem("zeroed")
        w_in = m.sem("w_in")
        consts, lanes_made = m.sem("consts"), m.sem("lanes_made")
        xn_made, rows_out, acc_out = m.sem("xn_made"), m.sem("rows_out"), m.sem("acc_out")
        t_mm, xt_out, l_mm, lg_out = m.sems("t_mm"), m.sems("xt_out"), m.sems("l_mm"), m.sems("lg_out")
        a_in, a_act, a_mm, a_out, a2_mm = (m.sem(n) for n in ("a_in", "a_act", "a_mm", "a_out", "a2_mm"))
        step, to_exp, from_exp = m.sem("step"), m.sem("to_exp"), m.sem("from_exp")
        masked, counted = m.sem("masked"), m.sem("counted")
        parts_ready, lo_made, kind_made, tab_mm = m.sem("parts_ready"), m.sems("lo_made"), m.sems("kind_made"), m.sems("tab_mm")


        def bc(ap, shape):
            return ap.to_broadcast(shape)

        with nc.Block() as block:
            @block.sync
            def _(sp):
                sp.dma_start(rw[:], router.rearrange("(c p) n -> p c n", p=P)).then_inc(w_in, 16)
                n_in = 16
                if actor:
                    sp.dma_start(b1[:], actor["b1"].partition_broadcast(P)).then_inc(w_in, 16)
                    sp.dma_start(b2[:], actor["b2"].partition_broadcast(P)).then_inc(w_in, 16)
                    sp.dma_start(w2[:], actor["w2"]).then_inc(w_in, 16)
                    n_in = 64
                sp.dma_start(acc[0][0:T, :].rearrange("(n p) d -> p n d", p=P), x_sb[:]).then_inc(acc_out, 16)
                sp.dma_start(acc[0][T:T + P, :], x_sb[:, 0, :]).then_inc(acc_out, 16)
                sp.wait_ge(zeroed, 1)
                sp.dma_start(acc[1].rearrange("(n p) d -> p n d", p=P), zeros[:]).then_inc(acc_out, 16)
                sp.wait_ge(xn_made, NT)
                sp.dma_start(rows.rearrange("(n p) d -> p n d", p=P), xn[:]).then_inc(rows_out, 16)
                sp.wait_ge(acc_out, 48)
                sp.wait_ge(rows_out, 16)
                sp.wait_ge(w_in, n_in)

            @block.gpsimd
            def _(pool):
                pool.memset(zeros[:], 0.0).then_inc(zeroed, 1)
                pool.memset(tril[:], 0.0).then_inc(consts, 1)
                pool.memset(allone[:], 1.0).then_inc(consts, 1)
                pool.memset(before[:], 0.0).then_inc(consts, 1)
                pool.iota(lanes[:], [[1, P]], base=0, channel_multiplier=0, allow_small_or_imprecise_dtypes=True).then_inc(consts, 1)
                pool.iota(token[:], [[P, NT]], base=1, channel_multiplier=1, allow_small_or_imprecise_dtypes=True).then_inc(consts, 1)
                pool.iota(spare[:], [[0, 1]], base=T + 1, channel_multiplier=1, allow_small_or_imprecise_dtypes=True).then_inc(consts, 1)
                if actor:
                    pool.iota(number[:], [[1, AK]], base=-AK, channel_multiplier=0, allow_small_or_imprecise_dtypes=True).then_inc(lanes_made, 1)
                pool.wait_ge(consts, 6)
                pool.affine_select(out=tril[:], in_=tril[:], compare_op=ALU.is_ge, fill=1.0, base=0,
                                   pattern=[[-1, P]], channel_multiplier=1).then_inc(consts, 1)
                pool.affine_select(out=before[:], in_=before[:], compare_op=ALU.is_ge, fill=1.0, base=0,
                                   pattern=[[-1, NE], [1, NE]], channel_multiplier=0).then_inc(consts, 1)
                pool.wait_ge(consts, 8)
                pool.wait_ge(parts_ready, 2)
                for t in range(NT):
                    u, i = t % 2, t // 2
                    wait(pool, tab_mm[u], i)
                    pool.tensor_scalar(kind[u][:, :, 0, :], hot_hi[:, t], token[:, t:t + 1], None, ALU.mult).then_inc(kind_made[u], 1)
                    pool.tensor_tensor(kind[u][:, :, 1, :], hot_hi[:, t], bc(W[:, t, :].unsqueeze(2), [P, NE, HI]),
                                       ALU.mult).then_inc(kind_made[u], 1)

            @block.scalar
            def _(act):
                norm.root(act)

                def tiles(i):
                    for u in range(2):
                        act.wait_ge(t_mm[u], i + 1)
                        wait(act, l_mm[u], i)
                        act.activation(xt[u][:].rearrange("p c t -> p (c t)"), pt[u][:, 0:FC * P], ACT.Copy).then_inc(xt_out[u], 1)
                        act.wait_ge(l_mm[u], i + 1)
                        act.activation(lg[:, bass.ds(2 * i + u, 1), :].rearrange("p a r -> p (a r)"), pl[u][:, 0:R],
                                       ACT.Copy).then_inc(lg_out[u], 1)

                loop(act, NT // 2, tiles)
                if actor:
                    act.wait_ge(a_in, 1)
                    act.activation(ag[:], ah[:], ACT.Gelu_apprx_tanh).then_inc(a_act, 1)
                    for g in range(4):
                        act.wait_ge(a_mm, g + 1)
                        act.activation(at[:, 4 * g:4 * g + 4, :], pa[g % 2][0:A], ACT.Copy).then_inc(a_out, 1)
                act.wait_ge(to_exp, 1)
                act.activation(V[:], V[:], ACT.Exp).then_inc(from_exp, 1)

            @block.tensor
            def _(pe):
                pe.wait_ge(w_in, 64 if actor else 16)

                def tiles(i):
                    for u in range(2):
                        pe.wait_ge(xn_made, 2 * i + u + 1)
                        wait(pe, xt_out[u], i)
                        for c in range(FC):
                            last = pe.transpose(pt[u][:, c * P:(c + 1) * P], xt_src(u, i, c), ident[:])
                        last.then_inc(t_mm[u], 1)
                        pe.wait_ge(xt_out[u], i + 1)
                        wait(pe, lg_out[u], i)
                        for c in range(FC):
                            last = pe.matmul(pl[u][:, 0:R], xt[u][:, c, :], rw[:, c, :], start=(c == 0), stop=(c == FC - 1))
                        last.then_inc(l_mm[u], 1)

                def xt_src(u, i, c):
                    return xn[:, 2 * i + u, c * P:(c + 1) * P]

                for i in range(NT // 2):
                    tiles(i)
                if actor:
                    pe.wait_ge(a_act, 1)
                    for g in range(4):
                        if g >= 2:
                            pe.wait_ge(a_out, g - 1)
                        for t in range(4):
                            last = pe.transpose(pa[g % 2][0:A, t, :], ag[:, 4 * g + t, :], ident[:])
                        last.then_inc(a_mm, 1)
                    pe.wait_ge(a_out, 4)
                    for t in range(NT):
                        last = pe.matmul(pl[0][:, AK * t:AK * t + AK], at[:, t, :], w2[:], start=True, stop=True)
                    last.then_inc(a2_mm, 1)
                pe.wait_ge(masked, 1)
                pe.wait_ge(consts, 8)
                pe.matmul(pcount[:, 0, :, :], tril[:], M[:], start=True, stop=True)
                pe.matmul(pcount[:, 1, :, :], allone[:], M[:], start=True, stop=True).then_inc(counted, 1)
                for t in range(NT):
                    u, i = t % 2, t // 2
                    pe.wait_ge(lo_made[u], i + 1)
                    pe.wait_ge(kind_made[u], 2 * i + 2)
                    for e in range(NE):
                        last = pe.matmul(ptab[:, e, :, :], hot_lo[u][:, e, :], kind[u][:, e, :, :],
                                         start=(t == 0 and e == 0), stop=(t == NT - 1 and e == NE - 1), skip_group_check=True)
                    last.then_inc(tab_mm[u], 1)

            @block.vector
            def _(dve):
                chain = Chain(dve, step)

                def do(ins):
                    chain.step(ins)
                    chain.wait()

                norm.statistics(dve, x_sb)
                with dve.Fori(0, NT) as t:
                    dve.tensor_scalar(xn[:, bass.ds(t, 1), :].rearrange("p a d -> p (a d)"),
                                      x_sb[:, bass.ds(t, 1), :].rearrange("p a d -> p (a d)"),
                                      norm.mv[:, bass.ds(t, 1), 0], norm.rstd[:, bass.ds(t, 1)],
                                      ALU.subtract, ALU.mult).then_inc(xn_made, 1)
                dve.wait_ge(lg_out[0], NT // 2)
                dve.wait_ge(lg_out[1], NT // 2)
                if actor:
                    dve.wait_ge(w_in, 64)
                    dve.tensor_tensor(ah[:], lg[:, :, NE:R], bc(b1[:].unsqueeze(1), [P, NT, A]), ALU.add).then_inc(a_in, 1)
                do(dve.tensor_reduce(top[:], lg[:, :, 0:NE], AXX, ALU.max))
                dve.tensor_tensor(V[:], lg[:, :, 0:NE], bc(top[:].unsqueeze(2), [P, NT, NE]), ALU.subtract).then_inc(to_exp, 1)
                dve.wait_ge(from_exp, 1)
                if actor:
                    do(dve.tensor_reduce(tot[:], V[:], AXX, ALU.add))
                    do(dve.reciprocal(top[:], tot[:]))
                    do(dve.tensor_tensor(V[:], V[:], bc(top[:].unsqueeze(2), [P, NT, NE]), ALU.mult))
                    by = V[:]
                else:
                    by = lg[:, :, 0:NE]
                other, own = bc(by.unsqueeze(2), [P, NT, NE, NE]), bc(by.unsqueeze(3), [P, NT, NE, NE])
                dve.wait_ge(consts, 8)
                do(dve.tensor_tensor(big[0][:], other, own, ALU.is_equal))
                do(dve.tensor_tensor(big[0][:], big[0][:], bc(before[:].unsqueeze(1), [P, NT, NE, NE]), ALU.mult))
                do(dve.tensor_tensor(big[1][:], other, own, ALU.is_gt))
                do(dve.tensor_tensor(big[0][:], big[0][:], big[1][:], ALU.add))
                do(dve.tensor_reduce(rank[:], big[0][:], AXX, ALU.add))
                if actor:
                    dve.wait_ge(a2_mm, 1)
                    do(dve.tensor_tensor(al[:], pl[0][:, 0:NT * AK].rearrange("p (t k) -> p t k", k=AK),
                                         bc(b2[:].unsqueeze(1), [P, NT, AK]), ALU.add))
                    do(dve.tensor_scalar(al[:], al[:], -30.0, 30.0, ALU.max, ALU.min))
                    do(dve.tensor_reduce(tot[:], al[:], AXX, ALU.max))
                    do(dve.tensor_tensor(al[:], al[:], bc(tot[:].unsqueeze(2), [P, NT, AK]), ALU.is_equal))
                    dve.wait_ge(lanes_made, 1)
                    do(dve.tensor_tensor(al[:], al[:], bc(number[:].unsqueeze(1), [P, NT, AK]), ALU.mult))
                    do(dve.tensor_reduce(tot[:], al[:], AXX, ALU.min))
                    do(dve.tensor_scalar(tot[:], tot[:], AK + 1.0, None, ALU.add))
                    dve.tensor_tensor(M[:], rank[:], bc(tot[:].unsqueeze(2), [P, NT, NE]), ALU.is_lt).then_inc(masked, 1)
                    dve.wait_ge(masked, 1)
                    do(dve.tensor_tensor(W[:], V[:], M[:], ALU.mult))
                else:
                    dve.tensor_scalar(M[:], rank[:], 2.0, None, ALU.is_lt).then_inc(masked, 1)
                    dve.wait_ge(masked, 1)
                    do(dve.tensor_tensor(W[:], V[:], M[:], ALU.mult))
                    do(dve.tensor_reduce(tot[:], W[:], AXX, ALU.add))
                    do(dve.reciprocal(top[:], tot[:]))
                    do(dve.tensor_tensor(W[:], W[:], bc(top[:].unsqueeze(2), [P, NT, NE]), ALU.mult))
                dve.wait_ge(counted, 1)
                do(dve.tensor_copy(cum[0][:], pcount[:, 1, :, :]))
                src = 0
                for d in (1, 2, 4, 8):
                    a, b = cum[src], cum[1 - src]
                    do(dve.tensor_copy(b[:, 0:d, :], a[:, 0:d, :]))
                    do(dve.tensor_tensor(b[:, d:NT, :], a[:, d:NT, :], a[:, 0:NT - d, :], ALU.add))
                    src = 1 - src
                incl = cum[src]
                do(dve.tensor_copy(cnt[:], incl[:, NT - 1, :]))
                do(dve.tensor_copy(slot[:, 0:1, :], pcount[:, 0, 0:1, :]))
                do(dve.tensor_tensor(slot[:, 1:NT, :], pcount[:, 0, 1:NT, :], incl[:, 0:NT - 1, :], ALU.add))
                do(dve.tensor_scalar(slot[:], slot[:], 1.0, None, ALU.add))
                do(dve.tensor_tensor(slot[:], slot[:], M[:], ALU.mult))
                do(dve.tensor_scalar(slot[:], slot[:], -1.0, None, ALU.add))
                do(dve.tensor_copy(sloti[:], slot[:]))
                do(dve.tensor_scalar(parti[:, 0], sloti[:], P - 1, None, ALU.bitwise_and))
                do(dve.tensor_scalar(parti[:, 1], sloti[:], 7, None, ALU.arith_shift_right))
                dve.tensor_copy(part[:], parti[:]).then_inc(parts_ready, 1)
                dve.wait_ge(parts_ready, 1)
                dve.tensor_tensor(hot_hi[:].rearrange("p t e h -> p (t e) h"),
                                  bc(lanes[:, 0:HI].unsqueeze(1), [P, NT * NE, HI]),
                                  bc(part[:, 1].rearrange("p t e -> p (t e)").unsqueeze(2), [P, NT * NE, HI]),
                                  ALU.is_equal).then_inc(parts_ready, 1)
                for t in range(NT):
                    u, i = t % 2, t // 2
                    wait(dve, tab_mm[u], i)
                    dve.tensor_tensor(hot_lo[u][:], bc(lanes[:].unsqueeze(1), [P, NE, P]),
                                      bc(part[:, 0, t, :].unsqueeze(2), [P, NE, P]), ALU.is_equal).then_inc(lo_made[u], 1)
                do(dve.tensor_scalar(cnt[:], cnt[:], PAIR - 1.0, float(PAIR), ALU.add, ALU.max))
                do(dve.tensor_copy(tables.pairs[:, 0, :], cnt[:]))
                do(dve.tensor_scalar(tables.pairs[:, 0, :], tables.pairs[:, 0, :], 8, None, ALU.arith_shift_right))
                do(dve.tensor_copy(cnt[:], tables.pairs[:, 0, :]))
                do(dve.tensor_tensor(big[0][:, 0], bc(cnt[:].unsqueeze(1), [P, NE, NE]), before[:], ALU.mult))
                do(dve.tensor_reduce(rank[:, 0, :], big[0][:, 0], AXX, ALU.add))
                do(dve.tensor_copy(tables.pairs[:, 1, :], rank[:, 0, :]))
                do(dve.memset(packed[:], 0.0))
                dve.wait_ge(tab_mm[0], NT // 2)
                dve.wait_ge(tab_mm[1], NT // 2)
                for e in range(NE):
                    first = dve.value_load(tables.pairs[0:1, 1, e:e + 1], min_val=0, max_val=(T // PAIR) * NE - 8)
                    do(dve.tensor_copy(packed[:, :, bass.ds(2 * first, HI)], ptab[:, e, :, :]))
                do(dve.tensor_scalar(rowf[:], packed[:, 0, :], -1.0, 0.0, ALU.add, ALU.max))
                do(dve.tensor_copy(tables.gather[:], rowf[:]))
                do(dve.tensor_scalar(rowf[:], packed[:, 0, :], 0.0, spare[:, 0:1], ALU.is_equal, ALU.mult))
                do(dve.tensor_tensor(rowf[:], rowf[:], packed[:, 0, :], ALU.add))
                do(dve.tensor_scalar(rowf[:], rowf[:], -1.0, None, ALU.add))
                do(dve.tensor_copy(tables.scatter[:], rowf[:]))
                do(dve.tensor_copy(tables.weight[:], packed[:, 1, :]))


def experts(nc, tag, ident, tables, rows, acc, gu, dn, inner, cw, nbuf):
    NC = inner // cw
    with Mem(nc, tag) as m:
        graw = m.sb("graw", [P, FC, 2 * inner])
        draw = m.sb("draw", [cw, NC, D])
        gh = [m.sb(f"gh{n}", [P, FC, 2 * inner], F32R) for n in range(nbuf)]
        gl = [m.sb(f"gl{n}", [P, FC, 2 * inner], F32R) for n in range(nbuf)]
        dh = [m.sb(f"dh{n}", [cw, NC, D], F32R) for n in range(nbuf)]
        dl = [m.sb(f"dl{n}", [cw, NC, D], F32R) for n in range(nbuf)]
        gidx = m.sb("gidx", [P, 2], I32)
        sidx = m.sb("sidx", [P, 2], I32)

        xg = m.sb("xg", [P, 2, D])
        xh = m.sb("xh", [P, FC, PAIR], F32R)
        xl = m.sb("xl", [P, FC, PAIR], F32R)
        sg = [m.sb(f"sg{n}", [cw, PAIR]) for n in range(2)]
        hf = [m.sb(f"hf{n}", [cw, PAIR]) for n in range(2)]
        hh = m.sb("hh", [cw, NC, PAIR], F32R)
        hl = m.sb("hl", [cw, NC, PAIR], F32R)
        ys = m.sb("ys", [P, 2, D])
        px = m.ps("px", [P, FC, PAIR])
        NG = min(NC, 3)
        pg = [m.ps(f"pg{n}", [P, 2, PAIR]) for n in range(NG)]
        py = m.ps("py", [P, 2, D])

        raw_in, hi_in, lo_made = m.sem("raw_in"), m.sems("hi_in", nbuf), m.sem("lo_made")
        index_made, gathered, scattered = m.sem("index_made"), m.sem("gathered"), m.sems("scattered")
        settled = m.sem("settled")
        x_mm, xh_made, xl_made = m.sem("x_mm"), m.sem("xh_made"), m.sem("xl_made")
        g_mm, silued, timed, hh_made, hl_made = (m.sem(n) for n in ("g_mm", "silued", "timed", "hh_made", "hl_made"))
        y_mm, y_out = m.sem("y_mm"), m.sem("y_out")

        def each(eng, body, between=None):
            for e in range(NE):
                n = eng.value_load(tables.pairs[0:1, 0, e:e + 1], min_val=1, max_val=T // PAIR)
                first = eng.value_load(tables.pairs[0:1, 1, e:e + 1], min_val=e, max_val=e * (T // PAIR))
                if between:
                    between(e, first)
                with eng.Fori(0, n) as i:
                    body(e, first + i)

        with nc.Block() as block:
            @block.sync
            def _(sp):
                for e in range(NE):
                    if e >= 1:
                        sp.wait_ge(lo_made, 2 * e)
                    sp.dma_start(graw[:], gu[e].rearrange("(c p) n -> p c n", p=P)).then_inc(raw_in, 16)
                    sp.dma_start(draw[:], dn[e].rearrange("(c p) n -> p c n", p=cw)).then_inc(raw_in, 16)
                sp.wait_ge(raw_in, 32 * NE)

            @block.gpsimd
            def _(pool):
                def settle(sem, value):
                    pool.wait_ge(sem, value)
                    pool.sem_inc(settled, 1)

                def high(e):
                    n = e % nbuf
                    pool.dma_start(gh[n][:], gu[e].rearrange("(c p) n -> p c n", p=P)).then_inc(hi_in[n], 16)
                    pool.dma_start(dh[n][:], dn[e].rearrange("(c p) n -> p c n", p=cw)).then_inc(hi_in[n], 16)

                def low(e):
                    n = e % nbuf
                    pool.wait_ge(raw_in, 32 * (e + 1))
                    pool.wait_ge(hi_in[n], 32 * (e // nbuf + 1))
                    pool.tensor_tensor(gl[n][:], graw[:], gh[n][:], ALU.subtract).then_inc(lo_made, 1)
                    pool.tensor_tensor(dl[n][:], draw[:], dh[n][:], ALU.subtract).then_inc(lo_made, 1)

                def gather(q, k):
                    pool.tensor_copy(gidx[:], tables.gather[:, bass.ds(2 * q, 2)]).then_inc(index_made, 1)
                    settle(index_made, k)
                    for t in range(2):
                        pool.indirect_dma_start(out=xg[:, t, :], out_offset=None, in_=rows,
                                                in_offset=bass.IndirectOffsetOnAxis(ap=gidx[:, t:t + 1], axis=0)
                                                ).then_inc(gathered, 16)

                def pair(e, q):
                    settle(x_mm, q + 1)
                    gather(q + 1, 2 * q + 2)
                    settle(y_out, 2 * q + 2)
                    for t in range(2):
                        settle(scattered[t], 16 * q + 16)
                    pool.tensor_copy(sidx[:], tables.scatter[:, bass.ds(2 * q, 2)]).then_inc(index_made, 1)
                    settle(index_made, 2 * q + 3)
                    for t in range(2):
                        pool.indirect_dma_start(out=acc[t], out_offset=bass.IndirectOffsetOnAxis(ap=sidx[:, t:t + 1], axis=0),
                                                in_=ys[:, t, :], in_offset=None, compute_op=ALU.add
                                                ).then_inc(scattered[t], 16)



                def between(e, first):
                    if e + 1 < NE:
                        low(e + 1)
                    if e + 2 < NE:
                        if e + 2 >= nbuf:
                            settle(y_mm, first)
                        high(e + 2)


                for t in range(2):
                    pool.dma_start(sidx[:, t:t + 1], tables.scatter[:, t:t + 1]).then_inc(scattered[t], 16)
                high(0)
                high(1)
                gather(0, 1)
                low(0)
                each(pool, pair, between)
                total = pool.value_load(tables.pairs[0:1, 1, NE - 1:NE], min_val=NE - 1, max_val=COLS // 2) \
                    + pool.value_load(tables.pairs[0:1, 0, NE - 1:NE], min_val=1, max_val=T // PAIR)
                for t in range(2):
                    settle(scattered[t], 16 * total + 16)
                settle(gathered, 32 * total + 32)

            @block.tensor
            def _(pe):
                def transposes(q):
                    pe.wait_ge(gathered, 32 * q + 32)
                    for t in range(2):
                        for c in range(FC):
                            last = pe.transpose(px[:, c, t * P:(t + 1) * P], xg[:, t, c * P:(c + 1) * P], ident[:])
                    last.then_inc(x_mm, 1)

                def pair(e, q):
                    n = e % nbuf
                    pe.wait_ge(xl_made, q + 1)
                    for c in range(NC):
                        if c >= NG:
                            pe.wait_ge(timed, NC * q + c - NG + 1)
                        for s in range(2):
                            cols = slice(s * inner + c * cw, s * inner + (c + 1) * cw)
                            last = three_products(pe, pg[c % NG][0:cw, s, :],
                                                  (lambda f: gh[n][:, f, cols], lambda f: gl[n][:, f, cols]),
                                                  (lambda f: xh[:, f, :], lambda f: xl[:, f, :]), range(FC), True, True)
                        last.then_inc(g_mm, 1)
                    transposes(q + 1)
                    for c in range(NC):
                        pe.wait_ge(hl_made, NC * q + c + 1)
                        for t in range(2):
                            cols = slice(t * P, (t + 1) * P)
                            for k, (a, b) in enumerate(((hh, dh[n]), (hl, dh[n]), (hh, dl[n]))):
                                last = pe.matmul(py[:, t, :], a[:, c, cols], b[:, c, :], start=(c == 0 and t == 0 and k == 0),
                                                 stop=(c == NC - 1 and k == 2), skip_group_check=True)
                    last.then_inc(y_mm, 1)

                def between(e, first):
                    pe.wait_ge(lo_made, 2 * e + 2)

                transposes(0)
                each(pe, pair, between)

            @block.scalar
            def _(act):
                def xhigh(q):
                    act.wait_ge(x_mm, q + 1)
                    act.activation(xh[:], px[:], ACT.Copy).then_inc(xh_made, 1)

                def pair(e, q):
                    for c in range(NC):
                        k = NC * q + c + 1
                        act.wait_ge(g_mm, k)
                        act.activation(sg[c % 2][:], pg[c % NG][0:cw, 0, :], ACT.Silu).then_inc(silued, 1)
                        act.wait_ge(timed, k)
                        act.activation(hh[:, c, :], hf[c % 2][:], ACT.Copy).then_inc(hh_made, 1)
                    xhigh(q + 1)

                xhigh(0)
                each(act, pair)

            @block.vector
            def _(dve):
                def xlow(q):
                    dve.wait_ge(xh_made, q + 1)
                    dve.tensor_tensor(xl[:], px[:], xh[:], ALU.subtract).then_inc(xl_made, 1)

                def pair(e, q):
                    for c in range(NC):
                        k = NC * q + c + 1
                        dve.wait_ge(silued, k)
                        dve.tensor_tensor(hf[c % 2][:], pg[c % NG][0:cw, 1, :], sg[c % 2][:], ALU.mult).then_inc(timed, 1)
                        dve.wait_ge(hh_made, k)
                        dve.tensor_tensor(hl[:, c, :], hf[c % 2][:], hh[:, c, :], ALU.subtract).then_inc(hl_made, 1)
                    xlow(q + 1)
                    dve.wait_ge(y_mm, q + 1)
                    for t in range(2):
                        dve.wait_ge(scattered[t], 16 * q + 16)
                        dve.tensor_scalar(ys[:, t, :], py[:, t, :], tables.weight[:, bass.ds(2 * q + t, 1)], None,
                                          ALU.mult).then_inc(y_out, 1)

                xlow(0)
                each(dve, pair)


def moe(nc, tag, x_sb, ident, rows, acc, router, actor, gu, dn, inner, cw, nbuf):
    with Mem(nc, tag) as m:
        tables = Tables(m)
        route(nc, tag + "route", x_sb, ident, tables, rows, acc, router, actor)
        experts(nc, tag + "experts", ident, tables, rows, acc, gu, dn, inner, cw, nbuf)


def attention(nc, tag, x_sb, c_sb, ctx_sb, va, ident, scratch, wq, wk, wv, bqk, bv, wo=None, bo=None):
    names = ["q", "k", "v"] + (["o"] if wo is not None else [])
    with Mem(nc, tag) as m:
        hi = {n: m.sb(f"w{n}h", [P, FC, D], F32R) for n in names}
        lo = {n: m.sb(f"w{n}l", [P, FC, D], F32R) for n in names}
        with Mem(nc, tag + "raw") as r:
            raws = [r.sb(f"w{n}", [P, FC, D]) for n in names]
            split_weights(nc, tag + "split", [x[:] for x in raws], [hi[n][:] for n in names], [lo[n][:] for n in names],
                          [w.rearrange("(c p) n -> p c n", p=P) for w in (wq, wk, wv, wo)[:len(names)]])
        project(nc, tag + "project", x_sb, c_sb, va, ident,
                [part[n] for n in "qkv" for part in (hi, lo)], bqk, bv, scratch)
        attend(nc, tag + "attend", x_sb, ctx_sb, va, ident, scratch, bo)
        if wo is not None:
            project_out(nc, tag + "out", x_sb, ctx_sb, ident, (hi["o"], lo["o"]))


def reload(nc, tag, x_sb, acc, out=None):
    Q = 4
    with Mem(nc, tag) as m:
        half = m.sb("half", [P, NT, D])
        loaded, summed, stored = m.sems("loaded", Q), m.sem("summed"), m.sem("stored")
        tiles = [slice(q * NT // Q, (q + 1) * NT // Q) for q in range(Q)]

        def dram(ap, q):
            return ap[q * T // Q:(q + 1) * T // Q, :].rearrange("(n p) d -> p n d", p=P)

        with nc.Block() as block:
            @block.sync
            def _(sp):
                for q in range(Q):
                    sp.dma_start(x_sb[:, tiles[q], :], dram(acc[0], q)).then_inc(loaded[q], 16)
                    sp.dma_start(half[:, tiles[q], :], dram(acc[1], q)).then_inc(loaded[q], 16)
                for q in range(Q if out is not None else 0):
                    sp.wait_ge(summed, q + 1)
                    sp.dma_start(dram(out, q), x_sb[:, tiles[q], :]).then_inc(stored, 16)
                if out is not None:
                    sp.wait_ge(stored, 16 * Q)

            @block.vector
            def _(dve):
                for q in range(Q):
                    dve.wait_ge(loaded[q], 32)
                    dve.tensor_tensor(x_sb[:, tiles[q], :], x_sb[:, tiles[q], :], half[:, tiles[q], :],
                                      ALU.add).then_inc(summed, 1)


def build(nc, a, out, stages):
    Mem.held = []
    scratch = [nc.dram_tensor(n, (B, 2, P, S), F32, kind="Internal").ap() for n in ("qh", "ql", "kh", "kl")]
    rows = [nc.dram_tensor(f"rows{n}", (T, D), F32, kind="Internal").ap() for n in range(2)]
    acc = [[nc.dram_tensor(f"acc{n}{t}", (T + P, D), F32, kind="Internal").ap() for t in range(2)] for n in range(2)]
    with Mem(nc, "all") as m:
        ident = m.sb("ident", [P, P])
        x_sb = m.sb("x", [P, NT, D])
        with Mem(nc, "attn") as t:
            c_sb = t.sb("c", [P, FC, T])
            ctx_sb = t.sb("ctx", [P, NT, D])
            va = t.sb("va", [P, NT, NH, VW])
            constants(nc, ident, x_sb, c_sb, va, a["x"], a["ctx_t"])
            if 0 in stages:
                attention(nc, "a0", x_sb, c_sb, ctx_sb, va, ident, scratch,
                          a["wq0"], a["wk0"], a["wv0"], a["bqk0"], a["bv0"], a["wo0"], a["bo0"])
            if 1 in stages:
                moe(nc, "m0", x_sb, ident, rows[0], acc[0], a["router0"], None, a["gu0"], a["dn0"], I0, P, 3)
                reload(nc, "back", x_sb, acc[0])
            Mem.release(nc)
            if 2 in stages:
                attention(nc, "a1", x_sb, c_sb, ctx_sb, va, ident, scratch,
                          a["wq1"], a["wk1"], a["wv1"], a["bqk1"], a["bv1"])
        if 3 in stages:
            moe(nc, "m1", x_sb, ident, rows[1], acc[1], a["router1"],
                {"w1n": A1, "b1": a["ab1"], "b2": a["ab2"], "w2": a["aw2"]}, a["gu1"], a["dn1"], I1, 112, 3)
            reload(nc, "last", x_sb, acc[1], out)
            return
        done = m.sem("stored")
        with nc.Block() as block:
            @block.sync
            def _(sp):
                sp.dma_start(out[0:T, :].rearrange("(n p) d -> p n d", p=P), x_sb[:]).then_inc(done, 16)
                sp.wait_ge(done, 16)


def layouts(v):
    import numpy as np

    def by_half(w):
        return w.reshape(-1, NP, 2, HD).transpose(0, 2, 1, 3).reshape(-1, D)

    a = {"x": v["x"].reshape(T, D), "ctx_t": v["ctx_1024"].reshape(T, D).T}
    for n, l in enumerate(("L0_xattn_", "L1_xattn_")):
        a[f"wq{n}"], a[f"wk{n}"], a[f"wv{n}"] = by_half(v[l + "Wq"]), by_half(v[l + "Wk"]), v[l + "Wv"]
        a[f"bqk{n}"] = np.concatenate([by_half(v[l + x][None])[0].reshape(2, P) for x in ("bq", "bk")]).T
        a[f"bv{n}"] = v[l + "bv"]
    a["wo0"], a["bo0"] = v["L0_xattn_Wo"], v["L0_xattn_bo"]
    a["router0"] = v["L0_ffn_router_weight"].T
    a["gu0"], a["dn0"] = v["L0_ffn_w1"].transpose(0, 2, 1), v["L0_ffn_w2"].transpose(0, 2, 1)
    a["router1"] = np.concatenate([v["L1_ffn_router_w"], v["L1_ffn_actor_w1"]]).T
    a["ab1"], a["ab2"], a["aw2"] = v["L1_ffn_actor_b1"], v["L1_ffn_actor_b2"], v["L1_ffn_actor_w2"].T
    a["gu1"] = np.concatenate([v["L1_ffn_gate_w"], v["L1_ffn_up_w"]], axis=1).transpose(0, 2, 1)
    a["dn1"] = v["L1_ffn_down_w"].transpose(0, 2, 1)
    return {k: np.ascontiguousarray(x) for k, x in a.items()}


STAGES = (0, 1, 2, 3)


def kernel(**inputs):
    import numpy as np
    import concourse.bacc as bacc
    from concourse.bass_utils import run_bass_kernel_spmd

    arrays = layouts({k: np.asarray(x) for k, x in inputs.items()})
    nc = bacc.Bacc("TRN2", target_bir_lowering=False, num_devices=1)
    aps = {k: nc.dram_tensor(f"in_{k}", x.shape, mybir.dt.from_np(x.dtype), kind="ExternalInput").ap()
           for k, x in arrays.items()}
    out = nc.dram_tensor("out", (T, D), F32, kind="ExternalOutput").ap()
    build(nc, aps, out, STAGES)
    r = run_bass_kernel_spmd(nc, [{f"in_{k}": x for k, x in arrays.items()}], core_ids=[0])
    return r.results[0]["out"].reshape(B, S, D)
```

```python
import concourse.bass as bass
from concourse import mybir
from contextlib import ExitStack

F32 = mybir.dt.float32
F32R = mybir.dt.float32r
BF16 = mybir.dt.bfloat16
I32 = mybir.dt.int32
ALU = mybir.AluOpType
ACT = mybir.ActivationFunctionType
AXX = mybir.AxisListType.X

P = 128
B, S, D = 8, 256, 256
T = B * S
NT = T // P
TB = S // P
FC = D // P
NH, HD = 16, 16
NP = NH // 2
KR = 3 * HD
VW = 32
EPS = 1e-5
SCORE_SCALE = 0.25
GROUPS = 2
NBUF = 4
LEAD = 12


class Mem:

    held = []

    def __init__(self, nc, tag):
        self.nc, self.tag, self.stack = nc, tag, ExitStack()

    def __enter__(self):
        return self

    def __exit__(self, *a):
        self.stack.close()

    def sb(self, name, shape, dt=F32):
        return self.stack.enter_context(self.nc.sbuf_tensor(f"{self.tag}_{name}", shape, dt))

    def ps(self, name, shape, dt=F32):
        return self.stack.enter_context(self.nc.psum_tensor(f"{self.tag}_{name}", shape, dt))

    def sem(self, name):
        Mem.held.append(self.nc.alloc_semaphore(f"{self.tag}_{name}"))
        return Mem.held[-1]

    @staticmethod
    def release(nc):
        nc.clear_and_free_semaphores(Mem.held)
        Mem.held = []
        nc.all_engine_barrier()

    def sems(self, name, n=2):
        return [self.sem(f"{name}{i}") for i in range(n)]


class Chain:

    def __init__(self, eng, sem):
        self.eng, self.sem, self.n = eng, sem, 0

    def step(self, ins):
        self.n += 1
        ins.then_inc(self.sem, 1)

    def wait(self):
        self.eng.wait_ge(self.sem, self.n)


def loop(eng, n, body):
    body(0)
    with eng.Fori(1, n) as i:
        body(i)


def wait(eng, sem, value):
    if not (isinstance(value, int) and value <= 0):
        eng.wait_ge(sem, value)


class Norm:

    def __init__(self, m):
        self.st = m.sb("st", [P, NT, 6])
        self.mv = m.sb("mv", [P, NT, 2])
        self.ve = m.sb("ve", [P, NT])
        self.root_sb = m.sb("root", [P, NT])
        self.y = m.sb("y", [P, NT])
        self.z = m.sb("z", [P, NT])
        self.rstd = m.sb("rstd", [P, NT])
        self.stats, self.aggr, self.steps, self.rooted = (m.sem(n) for n in ("stats", "aggr", "steps", "rooted"))

    def statistics(self, dve, x_sb, g):
        tiles = slice(g * NT // GROUPS, (g + 1) * NT // GROUPS)
        n = NT // GROUPS
        for t in range(NT)[tiles]:
            dve.bn_stats(self.st[:, t, :], x_sb[:, t, :]).then_inc(self.stats, 1)
        dve.wait_ge(self.stats, n * (g + 1))
        for t in range(NT)[tiles]:
            dve.bn_aggr(self.mv[:, t, :], self.st[:, t, :]).then_inc(self.aggr, 1)
        dve.wait_ge(self.aggr, n * (g + 1))
        ve, y, z = self.ve[:, tiles], self.y[:, tiles], self.z[:, tiles]
        done = 6 * g
        dve.tensor_scalar(ve, self.mv[:, tiles, 1], EPS, None, ALU.add).then_inc(self.steps, 1)
        dve.wait_ge(self.rooted, g + 1)
        dve.reciprocal(y, self.root_sb[:, tiles]).then_inc(self.steps, 1)
        dve.wait_ge(self.steps, done + 2)
        dve.tensor_tensor(z, y, y, ALU.mult).then_inc(self.steps, 1)
        dve.wait_ge(self.steps, done + 3)
        dve.tensor_tensor(z, z, ve, ALU.mult).then_inc(self.steps, 1)
        dve.wait_ge(self.steps, done + 4)
        dve.tensor_scalar(z, z, -0.5, 1.5, ALU.mult, ALU.add).then_inc(self.steps, 1)
        dve.wait_ge(self.steps, done + 5)
        dve.tensor_tensor(self.rstd[:, tiles], z, y, ALU.mult).then_inc(self.steps, 1)
        dve.wait_ge(self.steps, done + 6)

    def root(self, act):
        for g in range(GROUPS):
            tiles = slice(g * NT // GROUPS, (g + 1) * NT // GROUPS)
            act.wait_ge(self.steps, 6 * g + 1)
            act.activation(self.root_sb[:, tiles], self.ve[:, tiles], ACT.Sqrt).then_inc(self.rooted, 1)


def constants(nc, ident, x_sb, c_sb, va, x_in, ctx_t):
    with Mem(nc, "init") as m:
        loaded, zeroed, va_zeroed = m.sem("loaded"), m.sem("zeroed"), m.sem("va_zeroed")
        with nc.Block() as block:
            @block.sync
            def _(sp):
                sp.dma_start(x_sb[:], x_in.rearrange("(n p) d -> p n d", p=P)).then_inc(loaded, 16)
                sp.dma_start(c_sb[:], ctx_t.rearrange("(c p) t -> p c t", p=P)).then_inc(loaded, 16)
                sp.wait_ge(loaded, 32)

            @block.gpsimd
            def _(pool):
                pool.memset(ident[:], 0.0).then_inc(zeroed, 1)
                pool.wait_ge(zeroed, 1)
                pool.affine_select(out=ident[:], in_=ident[:], compare_op=ALU.not_equal, fill=1.0, base=0,
                                   pattern=[[-1, P]], channel_multiplier=1)

            @block.vector
            def _(dve):
                dve.memset(va[:], 0.0).then_inc(va_zeroed, 1)
                dve.wait_ge(va_zeroed, 1)
                dve.memset(va[:, :, :, HD:HD + 1], 1.0)


def split_weights(nc, tag, raws, his, los, srcs):
    with Mem(nc, tag) as m:
        loaded = m.sems("loaded", len(srcs))
        rounded = m.sem("rounded")
        with nc.Block() as block:
            @block.sync
            def _(sp):
                for raw, src, done in zip(raws, srcs, loaded):
                    sp.dma_start(raw, src).then_inc(done, 16)

            @block.vector
            def _(dve):
                for n, (raw, hi, lo) in enumerate(zip(raws, his, los)):
                    dve.wait_ge(loaded[n], 16)
                    dve.tensor_copy(hi, raw).then_inc(rounded, 1)
                    dve.wait_ge(rounded, n + 1)
                    dve.tensor_tensor(lo, raw, hi, ALU.subtract)


def three_products(pe, out, lhs, rhs, terms, start, stop):
    n = len(terms)
    for a, t in enumerate(terms):
        lh, ll = lhs[0](t), lhs[1](t)
        rh, rl = rhs[0](t), rhs[1](t)
        pe.matmul(out, lh, rh, start=start and a == 0, stop=False)
        pe.matmul(out, ll, rh, start=False, stop=False)
        last = pe.matmul(out, lh, rl, start=False, stop=stop and a == n - 1)
    return last


def project(nc, tag, x_sb, c_sb, va, ident, w, bqk, bv, parts):
    with Mem(nc, tag) as m:
        wqh, wql, wkh, wkl, wvh, wvl = w
        bvb = m.sb("bvb", [P, D])
        bqk_sb = m.sb("bqk", [P, 4])
        xn = [m.sb(f"xn{u}", [P, TB, D]) for u in range(2)]
        norm = Norm(m)
        xh = [m.sb(f"xh{u}", [P, FC, S], F32R) for u in range(2)]
        xl = [m.sb(f"xl{u}", [P, FC, S], F32R) for u in range(2)]
        ch = [m.sb(f"ch{u}", [P, FC, S], F32R) for u in range(2)]
        cl = [m.sb(f"cl{u}", [P, FC, S], F32R) for u in range(2)]
        qkh = [[m.sb(f"{n}h{u}", [P, 2, S], F32R) for u in range(2)] for n in "qk"]
        qkl = [[m.sb(f"{n}l{u}", [P, 2, S], F32R) for u in range(2)] for n in "qk"]
        pt = [m.ps(f"pt{u}", [P, FC, S]) for u in range(2)]
        pq = [[m.ps(f"p{n}{u}", [P, 2, S]) for u in range(2)] for n in "qk"]
        pv = [m.ps(f"pv{u}", [P, TB, D]) for u in range(2)]

        biases = m.sem("biases")
        ln = m.sem("ln")
        xn_ready, xt_ready = m.sems("xn_ready"), m.sems("xt_ready")
        xh_ready, xl_ready = m.sems("xh_ready"), m.sems("xl_ready")
        ch_ready, cl_ready = m.sems("ch_ready"), m.sems("cl_ready")
        mm_ready = [m.sems("q_mm"), m.sems("k_mm")]
        v_mm = m.sems("v_mm")
        hi_ready = [m.sems("qh_ready"), m.sems("kh_ready")]
        lo_ready = [m.sems("ql_ready"), m.sems("kl_ready")]
        v_ready = m.sems("v_ready")
        stored = [m.sems("q_stored"), m.sems("k_stored")]

        with nc.Block() as block:
            @block.sync
            def _(sp):
                sp.dma_start(bvb[:], bv.partition_broadcast(P)).then_inc(biases, 16)
                sp.dma_start(bqk_sb[:], bqk).then_inc(biases, 16)
                def batches(i):
                    for u in range(2):
                        for n in (1, 0):
                            for src, dst, ready in ((qkh[n][u], parts[2 * n], hi_ready[n][u]),
                                                    (qkl[n][u], parts[2 * n + 1], lo_ready[n][u])):
                                sp.wait_ge(ready, 2 * i + 2)
                                sp.dma_start(dst[bass.ds(2 * i + u, 1)].rearrange("a j r s -> r (a j) s"),
                                             src[:].bitcast(F32)).then_inc(stored[n][u], 16)
                loop(sp, B // 2, batches)
                for n in range(2):
                    for u in range(2):
                        sp.wait_ge(stored[n][u], 32 * (B // 2))

            @block.gpsimd
            def _(pool):
                for b in range(B):
                    u, i = b % 2, b // 2
                    wait(pool, v_mm[u], i)
                    c = c_sb[:, :, b * S:(b + 1) * S]
                    pool.tensor_copy(ch[u][:], c).then_inc(ch_ready[u], 1)
                    pool.wait_ge(ch_ready[u], i + 1)
                    pool.tensor_tensor(cl[u][:], c, ch[u][:], ALU.subtract).then_inc(cl_ready[u], 1)

            @block.vector
            def _(dve):
                for g in range(GROUPS):
                    norm.statistics(dve, x_sb, g)
                dve.wait_ge(biases, 32)

                def normalise(i, u):
                    wait(dve, xt_ready[u], i)
                    for t in range(TB):
                        tile = 2 * (2 * i + u) + t
                        dve.tensor_scalar(xn[u][:, t, :], x_sb[:, bass.ds(tile, 1), :].rearrange("p a d -> p (a d)"),
                                          norm.mv[:, bass.ds(tile, 1), 0], norm.rstd[:, bass.ds(tile, 1)],
                                          ALU.subtract, ALU.mult).then_inc(xn_ready[u], 1)

                def low(i, u, n):
                    for j in range(2):
                        dve.wait_ge(hi_ready[n][u], 2 * i + 2)
                        if j == 0:
                            wait(dve, stored[n][u], 32 * i)
                        dve.scalar_tensor_tensor(out=qkl[n][u][:, j, :], in0=pq[n][u][:, j, :],
                                                 scalar=bqk_sb[:, 2 * n + j:2 * n + j + 1], in1=qkh[n][u][:, j, :],
                                                 op0=ALU.add, op1=ALU.subtract).then_inc(lo_ready[n][u], 1)

                def batches(i):
                    for u in range(2):
                        normalise(i, u)
                        dve.wait_ge(xh_ready[u], i + 1)
                        dve.tensor_tensor(xl[u][:], pt[u][:], xh[u][:], ALU.subtract).then_inc(xl_ready[u], 1)
                        low(i, u, 1)
                        dve.wait_ge(v_mm[u], i + 1)
                        for t in range(TB):
                            dve.tensor_tensor(
                                va[:, bass.ds(2 * (2 * i + u) + t, 1), :, 0:HD].rearrange("p a h d -> p (a h) d"),
                                pv[u][:, t, :].rearrange("p (h d) -> p h d", h=NH),
                                bvb[:].rearrange("p (h d) -> p h d", h=NH), ALU.add).then_inc(v_ready[u], 1)
                        low(i, u, 0)

                loop(dve, B // 2, batches)

            @block.scalar
            def _(act):
                norm.root(act)
                act.wait_ge(biases, 32)
                def batches(i):
                    for u in range(2):
                        act.wait_ge(xt_ready[u], i + 1)
                        wait(act, mm_ready[0][u], i)
                        act.activation(xh[u][:], pt[u][:], ACT.Copy).then_inc(xh_ready[u], 1)
                        for n in (1, 0):
                            act.wait_ge(mm_ready[n][u], i + 1)
                            wait(act, stored[n][u], 32 * i)
                            for j in range(2):
                                act.activation(qkh[n][u][:, j, :], pq[n][u][:, j, :], ACT.Identity,
                                               bias=bqk_sb[:, 2 * n + j:2 * n + j + 1]).then_inc(hi_ready[n][u], 1)

                loop(act, B // 2, batches)

            @block.tensor
            def _(pe):
                def batches(i):
                    for u in range(2):
                        pe.wait_ge(xn_ready[u], 2 * i + 2)
                        wait(pe, xl_ready[u], i)
                        for t in range(TB):
                            for c in range(FC):
                                last = pe.transpose(pt[u][:, c, t * P:(t + 1) * P], xn[u][:, t, c * P:(c + 1) * P], ident[:])
                        last.then_inc(xt_ready[u], 1)
                        pe.wait_ge(cl_ready[u], i + 1)

                        def qk(n, wh, wl, ah, al):
                            wait(pe, lo_ready[n][u], 2 * i)
                            for j in range(2):
                                last = three_products(
                                    pe, pq[n][u][:, j, :],
                                    (lambda c: wh[:, c, j * P:(j + 1) * P], lambda c: wl[:, c, j * P:(j + 1) * P]),
                                    (lambda c: ah[:, c, :], lambda c: al[:, c, :]), range(FC), True, True)
                            last.then_inc(mm_ready[n][u], 1)

                        qk(1, wkh, wkl, ch[u], cl[u])
                        wait(pe, v_ready[u], 2 * i)
                        for t in range(TB):
                            last = three_products(
                                pe, pv[u][:, t, :],
                                (lambda c: ch[u][:, c, t * P:(t + 1) * P], lambda c: cl[u][:, c, t * P:(t + 1) * P]),
                                (lambda c: wvh[:, c, :], lambda c: wvl[:, c, :]), range(FC), True, True)
                        last.then_inc(v_mm[u], 1)
                        pe.wait_ge(xl_ready[u], i + 1)
                        qk(0, wqh, wql, xh[u], xl[u])

                loop(pe, B // 2, batches)


def attend(nc, tag, x_sb, ctx_sb, va, ident, parts, bias=None):
    SLOTS = B * NP
    with Mem(nc, tag) as m:
        qs = [m.sb(f"qs{n}", [P, NP, S], F32R) for n in range(NBUF)]
        ks = [m.sb(f"ks{n}", [P, NP, S], F32R) for n in range(NBUF)]
        pT = [m.sb(f"pT{n}", [P, 2, TB, S]) for n in range(4)]
        mx = [m.sb(f"mx{n}", [P, TB, NH]) for n in range(2)]
        nm = [m.sb(f"nm{n}", [NH, S], F32R) for n in range(2)]
        oT = [m.sb(f"oT{n}", [P, 2, 2 * S]) for n in range(2)]
        rs = m.sb("rs", [P, TB, NH])
        sc = [m.ps(f"sc{n}", [P, TB, S]) for n in range(2)]
        sT = [m.ps(f"sT{n}", [P, 2, 2 * S]) for n in range(2)]
        po = m.ps("po", [P, 2, S])
        pf = m.ps("pf", [P, 512])

        ones = m.sem("ones")
        q_in, k_in = m.sems("q_in", NBUF), m.sems("k_in", NBUF)
        sc_mm, sc_max = m.sem("sc_mm"), m.sem("sc_max")
        mT_mm, nm_made, m_in = m.sem("mT_mm"), m.sem("nm_made"), m.sems("m_in", NBUF)
        sT_mm, exped = m.sem("sT_mm"), m.sem("exped")
        pv_mm, o_out = m.sem("pv_mm"), m.sem("o_out")
        oT_mm, recip, normed = m.sem("oT_mm"), m.sem("recip"), m.sem("normed")
        bias_in, added = m.sem("bias_in"), m.sem("added")
        bias_sb = m.sb("bias", [P, D]) if bias is not None else None

        with nc.Block() as block:
            @block.sync
            def _(sp):
                if bias is not None:
                    sp.dma_start(bias_sb[:], bias.partition_broadcast(P)).then_inc(bias_in, 16)
                sp.wait_ge(ones, 2 * NBUF)

                def load(b):
                    n = b % NBUF
                    if b >= NBUF:
                        sp.wait_ge(sT_mm, NP * (b - NBUF + 1))
                    for dst, hi, lo, kinds, done in ((qs[n], parts[0], parts[1], (0, 0, 1), q_in[n]),
                                                     (ks[n], parts[2], parts[3], (0, 1, 0), k_in[n])):
                        for j in range(2):
                            for r, kind in enumerate(kinds):
                                src = (hi, lo)[kind][b, j].rearrange("(p d) s -> d p s", d=HD)
                                row = 64 * j + HD * r
                                sp.dma_start(dst[row:row + HD, :, :].bitcast(F32), src).then_inc(done, 16)

                def maxima(b):
                    n = b % NBUF
                    sp.wait_ge(nm_made, b + 1)
                    for j in range(2):
                        row = 64 * j + KR
                        sp.dma_start(qs[n][row:row + 1, :, :].bitcast(F32), nm[b % 2][NP * j:NP * j + NP, :].bitcast(F32)).then_inc(m_in[n], 16)

                load(0)
                load(1)
                for b in range(B):
                    if b + 2 < B:
                        load(b + 2)
                    maxima(b)

            @block.gpsimd
            def _(pool):
                for n in range(NBUF):
                    for j in range(2):
                        pool.memset(ks[n][64 * j + 32:64 * j + 64, :, :].bitcast(F32), 1.0).then_inc(ones, 1)
                pool.wait_ge(ones, 2 * NBUF)
                if bias is not None:
                    pool.wait_ge(bias_in, 16)
                for k in range(NT):
                    if bias is None:
                        pool.wait_ge(normed, k + 1)
                    pool.tensor_tensor(x_sb[:, k, :], x_sb[:, k, :],
                                       ctx_sb[:, k, :] if bias is None else bias_sb[:], ALU.add)

            @block.tensor
            def _(pe):
                def scores(n):
                    b, p = divmod(n, NP)
                    if p == 0:
                        pe.wait_ge(q_in[b % NBUF], 96 * (b // NBUF + 1))
                        pe.wait_ge(k_in[b % NBUF], 96 * (b // NBUF + 1))
                    for j in range(2):
                        rows = slice(64 * j, 64 * j + KR)
                        if n >= 1:
                            pe.wait_ge(sc_max, 2 * (n - 1) + j + 1)
                        for qt in range(TB):
                            last = pe.matmul(sc[j][:, qt, :], qs[b % NBUF][rows, p, qt * P:(qt + 1) * P],
                                             ks[b % NBUF][rows, p, :], start=True, stop=True)
                        last.then_inc(sc_mm, 1)

                def maxima_T(b):
                    pe.wait_ge(sc_max, 2 * NP * (b + 1))
                    for qt in range(TB):
                        last = pe.transpose(pf[0:NH, qt * P:(qt + 1) * P], mx[b % 2][:, qt, :], ident[:])
                    last.then_inc(mT_mm, 1)

                def scores_T(t):
                    b, p = divmod(t, NP)
                    if p == 0:
                        pe.wait_ge(m_in[b % NBUF], 32 * (b // NBUF + 1))
                    if t >= 2:
                        pe.wait_ge(exped, t - 1)
                    for j in range(2):
                        rows = slice(64 * j, 64 * j + KR + 1)
                        for kt in range(TB):
                            last = pe.matmul(sT[t % 2][:, j, kt * S:(kt + 1) * S],
                                             ks[b % NBUF][rows, p, kt * P:(kt + 1) * P],
                                             qs[b % NBUF][rows, p, :], start=True, stop=True)
                    last.then_inc(sT_mm, 1)

                def values(g):
                    b, gb = divmod(g, NP // 2)
                    pe.wait_ge(exped, 2 * g + 2)
                    if g % 2 == 0 and g >= 2:
                        pe.wait_ge(o_out, g // 2)
                    for kt in range(TB):
                        for c in range(4):
                            last = pe.matmul(po[32 * c:32 * c + VW, g % 2, :], va[:, TB * b + kt, 4 * gb + c, :],
                                             pT[(2 * g + c // 2) % 4][:, c % 2, kt, :],
                                             start=(kt == 0), stop=(kt == TB - 1))
                    last.then_inc(pv_mm, 1)

                def outputs_T(b, qt):
                    pe.wait_ge(o_out, 2 * b + 2)
                    for g in range(4):
                        last = pe.transpose(pf[:, g * P:(g + 1) * P],
                                            oT[b % 2][:, g // 2, (g % 2) * S + qt * P:(g % 2) * S + (qt + 1) * P], ident[:])
                    last.then_inc(oT_mm, 1)

                shared = None
                for what, k in pe_order(SLOTS):
                    if what in ("mT", "oT"):
                        if shared is not None:
                            pe.wait_ge(nm_made if shared[0] == "mT" else normed, shared[1] + 1)
                        shared = what, k
                    if what == "sT":
                        scores_T(k)
                    elif what == "sc":
                        scores(k)
                    elif what == "mT":
                        maxima_T(k)
                    elif what == "pv":
                        values(k)
                    else:
                        outputs_T(k // TB, k % TB)

            @block.vector
            def _(dve):
                for n in range(SLOTS + LEAD + 6):
                    if n < SLOTS:
                        b, p = divmod(n, NP)
                        for j in range(2):
                            dve.wait_ge(sc_mm, 2 * n + j + 1)
                            if p == 0 and j == 0 and b >= 2:
                                dve.wait_ge(mT_mm, b - 1)
                            dve.tensor_reduce(mx[b % 2][:, :, NP * j + p], sc[j][:], AXX, ALU.max).then_inc(sc_max, 1)
                    if n >= 9 and (n - 9) % NP == 0 and (n - 9) // NP < B:
                        b = (n - 9) // NP
                        dve.wait_ge(mT_mm, b + 1)
                        if b >= 2:
                            dve.wait_ge(m_in[(b - 2) % NBUF], 32 * ((b - 2) // NBUF + 1))
                        dve.tensor_scalar(nm[b % 2][:], pf[0:NH, 0:S], -1.0, None, ALU.mult).then_inc(nm_made, 1)
                    t = n - LEAD
                    for qt in range(TB):
                        if t >= NP + 3 + qt and (t - NP - 3 - qt) % NP == 0 and (t - NP - 3 - qt) // NP < B:
                            k = TB * ((t - NP - 3 - qt) // NP) + qt
                            o = pf[:].rearrange("p (h w) -> p h w", w=VW)
                            dve.wait_ge(oT_mm, k + 1)
                            if k >= 1:
                                dve.wait_ge(normed, k)
                            dve.reciprocal(rs[:, k % 2, :], o[:, :, HD]).then_inc(recip, 1)
                            dve.wait_ge(recip, k + 1)
                            dve.tensor_tensor(ctx_sb[:, k, :].rearrange("p (h d) -> p h d", h=NH), o[:, :, 0:HD],
                                              rs[:, k % 2, :].unsqueeze(2).to_broadcast([P, NH, HD]),
                                              ALU.mult).then_inc(normed, 1)

            @block.scalar
            def _(act):
                for t in range(SLOTS + 2):
                    if t < SLOTS:
                        act.wait_ge(sT_mm, t + 1)
                        if t >= 4:
                            act.wait_ge(pv_mm, (t - 4) // 2 + 1)
                        act.activation(pT[t % 4][:].rearrange("p a b s -> p a (b s)"), sT[t % 2][:], ACT.Exp,
                                       scale=SCORE_SCALE).then_inc(exped, 1)
                    if t >= 5 and (t - 5) % 4 == 0 and (t - 5) // 4 < 2 * B:
                        h = (t - 5) // 4
                        act.wait_ge(pv_mm, 2 * h + 2)
                        if h >= 4 and h % 2 == 0:
                            act.wait_ge(oT_mm, TB * (h // 2 - 1))
                        act.activation(oT[(h // 2) % 2][:, h % 2, :], po[:].rearrange("p g s -> p (g s)"),
                                       ACT.Copy).then_inc(o_out, 1)


def pe_order(slots):
    order = []
    for n in range(slots + LEAD + 6):
        t = n - LEAD
        if 0 <= t < slots:
            order.append(("sT", t))
        if n < slots:
            order.append(("sc", n))
        if n >= 9 and (n - 9) % NP == 0 and (n - 9) // NP < B:
            order.append(("mT", (n - 9) // NP))
        if t >= 3 and (t - 3) % 2 == 0 and (t - 3) // 2 < slots // 2:
            order.append(("pv", (t - 3) // 2))
        for qt in range(TB):
            k = t - NP - 3 - qt
            if k >= 0 and k % NP == 0 and k // NP < B:
                order.append(("oT", TB * (k // NP) + qt))
    return order


def project_out(nc, tag, x_sb, ctx_sb, ident, w):
    with Mem(nc, tag) as m:
        wh, wl = w
        ch = [m.sb(f"ch{u}", [P, FC, S], F32R) for u in range(2)]
        cl = [m.sb(f"cl{u}", [P, FC, S], F32R) for u in range(2)]
        pt = [m.ps(f"pt{u}", [P, FC, S]) for u in range(2)]
        po = [m.ps(f"po{u}", [P, TB, D]) for u in range(2)]
        t_mm, h_ready, l_ready = m.sems("t_mm"), m.sems("h_ready"), m.sems("l_ready")
        o_mm, added = m.sems("o_mm"), m.sems("added")
        with nc.Block() as block:
            @block.tensor
            def _(pe):
                for b in range(B + 1):
                    if b < B:
                        u, i = b % 2, b // 2
                        wait(pe, l_ready[u], i)
                        for t in range(TB):
                            for c in range(FC):
                                last = pe.transpose(pt[u][:, c, t * P:(t + 1) * P],
                                                    ctx_sb[:, TB * b + t, c * P:(c + 1) * P], ident[:])
                        last.then_inc(t_mm[u], 1)
                    if b >= 1:
                        u, i = (b - 1) % 2, (b - 1) // 2
                        pe.wait_ge(l_ready[u], i + 1)
                        wait(pe, added[u], i)
                        for t in range(TB):
                            last = three_products(
                                pe, po[u][:, t, :],
                                (lambda c: ch[u][:, c, t * P:(t + 1) * P], lambda c: cl[u][:, c, t * P:(t + 1) * P]),
                                (lambda c: wh[:, c, :], lambda c: wl[:, c, :]), range(FC), True, True)
                        last.then_inc(o_mm[u], 1)

            @block.scalar
            def _(act):
                for b in range(B):
                    u, i = b % 2, b // 2
                    act.wait_ge(t_mm[u], i + 1)
                    wait(act, o_mm[u], i)
                    act.activation(ch[u][:], pt[u][:], ACT.Copy).then_inc(h_ready[u], 1)

            @block.vector
            def _(dve):
                for b in range(B + 1):
                    if b < B:
                        u, i = b % 2, b // 2
                        dve.wait_ge(h_ready[u], i + 1)
                        dve.tensor_tensor(cl[u][:], pt[u][:], ch[u][:], ALU.subtract).then_inc(l_ready[u], 1)
                    if b >= 1:
                        u, i = (b - 1) % 2, (b - 1) // 2
                        dve.wait_ge(o_mm[u], i + 1)
                        x = x_sb[:, TB * (b - 1):TB * b, :]
                        dve.tensor_tensor(x, po[u][:], x, ALU.add).then_inc(added[u], 1)


NE = 8
PAIR = 2 * P
HI = T // P
KINDS = 5
COLS = 2 * NE * (T // PAIR)
PAD_COLS = COLS + HI
AK = 6
I0, I1, A1 = 256, 672, 50


class Tables:

    def __init__(self, m):
        self.gather = m.sb("gather_rows", [P, PAD_COLS], I32)
        self.scatter = m.sb("scatter_rows", [P, PAD_COLS], I32)
        self.weight = m.sb("slot_weight", [P, PAD_COLS])
        self.pairs = m.sb("pairs", [P, 2, NE], I32)


def route(nc, tag, x_sb, ident, tables, weights, rows, acc, router, actor=None):
    A = actor["w1n"] if actor else 0
    R = NE + A
    with Mem(nc, tag) as m:
        norm = Norm(m)
        xn = m.sb("xn", [P, NT, D])
        xt = [m.sb(f"xt{u}", [P, FC, P]) for u in range(2)]
        rw = m.sb("rw", [P, FC, R])
        lg = m.sb("lg", [P, NT, R])
        ahead = m.sb("ahead", [P, NT, NE, NE])
        V = m.sb("value", [P, NT, NE])
        W = m.sb("w", [P, NT, NE])
        M = m.sb("mask", [P, NT, NE])
        rank = m.sb("rank", [P, NT, NE])
        top = m.sb("top", [P, NT])
        tot = m.sb("tot", [P, NT])
        cum = [m.sb(f"cum{n}", [P, NT, NE]) for n in range(2)]
        slot = m.sb("slot", [P, NT, NE])
        sloti = m.sb("sloti", [P, NT, NE], I32)
        parti = m.sb("parti", [P, 2, NT, NE], I32)
        part = m.sb("part", [P, 2, NT, NE])
        cnt = m.sb("cnt", [P, NE])
        before = m.sb("before", [P, NE, NE])
        tril = m.sb("tril", [P, P])
        allone = m.sb("allone", [P, P])
        lanes = m.sb("lanes", [P, P])
        lane1 = m.sb("lane1", [P, 1])
        spare = m.sb("spare", [P, 1])
        hot_lo = [m.sb(f"hot_lo{u}", [P, NE, P], BF16) for u in range(3)]
        hot_hi = m.sb("hot_hi", [P, NT, NE, HI], BF16)
        rest = [m.sb(f"rest{n}", [P, NT, NE]) for n in range(2)]
        piece = [m.sb(f"piece{n}", [P, NT, NE], BF16) for n in range(3)]
        kind = m.sb("kind", [P, NT, NE, KINDS, HI], BF16)
        packed = m.sb("packed", [P, KINDS, PAD_COLS])
        found = m.sb("found", [P, PAD_COLS])
        rowf = m.sb("rowf", [P, PAD_COLS])
        pt = [m.ps(f"pt{u}", [P, 512]) for u in range(2)]
        pl = [m.ps(f"pl{u}", [P, 512]) for u in range(2)]
        pcount = m.ps("pcount", [P, 2, NT, NE])
        ptab = m.ps("ptab", [P, NE, P])
        if actor:
            b1 = m.sb("b1", [P, A])
            b2 = m.sb("b2", [P, AK])
            w2 = m.sb("w2", [A, AK])
            ah = m.sb("ah", [P, NT, A])
            ag = m.sb("ag", [P, NT, A])
            at = m.sb("at", [A, NT, P])
            al = m.sb("al", [P, NT, AK])
            number = m.sb("number", [P, AK])
            pa = [x[:].rearrange("p (t c) -> p t c", t=4) for x in pt]

        zeros = m.sb("zeros", [P, 1, D])
        zeroed = m.sem("zeroed")
        w_in = m.sem("w_in")
        consts, lanes_made = m.sem("consts"), m.sem("lanes_made")
        xn_made, rows_out, acc_out = m.sem("xn_made"), m.sem("rows_out"), m.sem("acc_out")
        t_mm, xt_out, l_mm, lg_out = m.sems("t_mm"), m.sems("xt_out"), m.sems("l_mm"), m.sems("lg_out")
        a_in, a_act, a_mm, a_out, a2_mm = (m.sem(n) for n in ("a_in", "a_act", "a_mm", "a_out", "a2_mm"))
        step, to_exp, from_exp = m.sem("step"), m.sem("to_exp"), m.sem("from_exp")
        masked, counted = m.sem("masked"), m.sem("counted")
        parts_ready, paired, lo_made, tab_mm = m.sem("parts_ready"), m.sem("paired"), m.sem("lo_made"), m.sem("tab_mm")
        number_made, weight_made, low_weight_made = m.sem("number_made"), m.sem("weight_made"), m.sem("low_weight_made")
        packed_zero, packing = m.sem("packed_zero"), m.sem("packing")


        def bc(ap, shape):
            return ap.to_broadcast(shape)

        with nc.Block() as block:
            @block.sync
            def _(sp):
                sp.dma_start(rw[:], router.rearrange("(c p) n -> p c n", p=P)).then_inc(w_in, 16)
                n_in = 16
                if actor:
                    sp.dma_start(b1[:], actor["b1"].partition_broadcast(P)).then_inc(w_in, 16)
                    sp.dma_start(b2[:], actor["b2"].partition_broadcast(P)).then_inc(w_in, 16)
                    sp.dma_start(w2[:], actor["w2"]).then_inc(w_in, 16)
                    n_in = 64
                weights.load(sp, 0)
                sp.dma_start(acc[0][0:T, :].rearrange("(n p) d -> p n d", p=P), x_sb[:]).then_inc(acc_out, 16)
                sp.dma_start(acc[0][T:T + P, :], x_sb[:, 0, :]).then_inc(acc_out, 16)
                sp.wait_ge(zeroed, 1)
                sp.dma_start(acc[1].rearrange("(n p) d -> p n d", p=P),
                             bc(zeros[:], [P, NT + 1, D])).then_inc(acc_out, 16)
                sp.wait_ge(xn_made, NT)
                sp.dma_start(rows.rearrange("(n p) d -> p n d", p=P), xn[:]).then_inc(rows_out, 16)
                weights.load(sp, 1)
                sp.wait_ge(acc_out, 48)
                sp.wait_ge(rows_out, 16)
                sp.wait_ge(w_in, n_in)

            @block.gpsimd
            def _(pool):
                pool.memset(zeros[:], 0.0).then_inc(zeroed, 1)
                pool.memset(tril[:], 0.0).then_inc(consts, 1)
                pool.memset(allone[:], 1.0).then_inc(consts, 1)
                pool.memset(before[:], 0.0).then_inc(consts, 1)
                pool.iota(lanes[:], [[1, P]], base=0, channel_multiplier=0, allow_small_or_imprecise_dtypes=True).then_inc(consts, 1)
                pool.iota(lane1[:], [[0, 1]], base=1, channel_multiplier=1, allow_small_or_imprecise_dtypes=True).then_inc(consts, 1)
                pool.memset(packed[:], 0.0).then_inc(packed_zero, 1)
                pool.iota(spare[:], [[0, 1]], base=T + 1, channel_multiplier=1, allow_small_or_imprecise_dtypes=True).then_inc(consts, 1)
                if actor:
                    pool.iota(number[:], [[1, AK]], base=-AK, channel_multiplier=0, allow_small_or_imprecise_dtypes=True).then_inc(lanes_made, 1)
                pool.wait_ge(consts, 6)
                pool.affine_select(out=tril[:], in_=tril[:], compare_op=ALU.is_ge, fill=1.0, base=0,
                                   pattern=[[-1, P]], channel_multiplier=1).then_inc(consts, 1)
                pool.affine_select(out=before[:], in_=before[:], compare_op=ALU.is_ge, fill=1.0, base=0,
                                   pattern=[[-1, NE], [1, NE]], channel_multiplier=0).then_inc(consts, 1)
                pool.wait_ge(parts_ready, 2)
                for t in range(0, NT, 4):
                    pool.tensor_tensor(kind[:, t:t + 4, :, 4, :], hot_hi[:, t:t + 4],
                                       bc(piece[2][:, t:t + 4].unsqueeze(3), [P, 4, NE, HI]), ALU.mult).then_inc(low_weight_made, 1)

            @block.scalar
            def _(act):
                norm.root(act)
                for c in range(weights.NC):
                    weights.high(act, 0, c)

                for t in range(NT + 1):
                    if t < NT:
                        u, i = t % 2, t // 2
                        act.wait_ge(t_mm[u], i + 1)
                        wait(act, l_mm[u], i)
                        act.activation(xt[u][:].rearrange("p c t -> p (c t)"), pt[u][:, 0:FC * P], ACT.Copy).then_inc(xt_out[u], 1)
                    if t >= 1:
                        u, i = (t - 1) % 2, (t - 1) // 2
                        act.wait_ge(l_mm[u], i + 1)
                        act.activation(lg[:, t - 1, :], pl[u][:, 0:R], ACT.Copy).then_inc(lg_out[u], 1)
                act.wait_ge(to_exp, 1)
                act.activation(V[:], V[:], ACT.Exp).then_inc(from_exp, 1)
                if actor:
                    act.wait_ge(a_in, 1)
                    act.activation(ag[:], ah[:], ACT.Gelu_apprx_tanh).then_inc(a_act, 1)
                    for g in range(4):
                        act.wait_ge(a_mm, g + 1)
                        act.activation(at[:, 4 * g:4 * g + 4, :], pa[g % 2][0:A], ACT.Copy).then_inc(a_out, 1)
                act.wait_ge(consts, 8)
                act.wait_ge(parts_ready, 2)
                for t in range(NT):
                    act.activation(kind[:, t, :, 0, :], hot_hi[:, t], ACT.Copy, scale=lane1[:, 0:1]).then_inc(number_made, 1)
                    act.activation(kind[:, t, :, 1, :], hot_hi[:, t], ACT.Copy, scale=float(P * t)).then_inc(number_made, 1)
                act.wait_ge(paired, 1)
                firsts = [act.value_load(tables.pairs[0:1, 1, e:e + 1], min_val=0, max_val=(T // PAIR) * NE - 8)
                          for e in range(NE)]
                act.wait_ge(packed_zero, 1)
                act.wait_ge(tab_mm, NT)
                for e, first in enumerate(firsts):
                    if e >= 1:
                        act.wait_ge(packing, e)
                    act.activation(packed[:, :, bass.ds(2 * first, HI)],
                                   ptab[:, e, 0:KINDS * HI].rearrange("p (k h) -> p k h", k=KINDS), ACT.Copy).then_inc(packing, 1)

            @block.tensor
            def _(pe):
                pe.wait_ge(w_in, 64 if actor else 16)

                for t in range(NT + 1):
                    if t < NT:
                        u, i = t % 2, t // 2
                        pe.wait_ge(xn_made, t + 1)
                        wait(pe, xt_out[u], i)
                        for c in range(FC):
                            last = pe.transpose(pt[u][:, c * P:(c + 1) * P], xn[:, t, c * P:(c + 1) * P], ident[:])
                        last.then_inc(t_mm[u], 1)
                    if t >= 1:
                        u, i = (t - 1) % 2, (t - 1) // 2
                        pe.wait_ge(xt_out[u], i + 1)
                        wait(pe, lg_out[u], i)
                        for c in range(FC):
                            last = pe.matmul(pl[u][:, 0:R], xt[u][:, c, :], rw[:, c, :], start=(c == 0), stop=(c == FC - 1))
                        last.then_inc(l_mm[u], 1)
                if actor:
                    pe.wait_ge(a_act, 1)
                    for g in range(4):
                        if g >= 2:
                            pe.wait_ge(a_out, g - 1)
                        for t in range(4):
                            last = pe.transpose(pa[g % 2][0:A, t, :], ag[:, 4 * g + t, :], ident[:])
                        last.then_inc(a_mm, 1)
                    pe.wait_ge(a_out, 4)
                    for t in range(NT):
                        last = pe.matmul(pl[0][:, AK * t:AK * t + AK], at[:, t, :], w2[:], start=True, stop=True)
                    last.then_inc(a2_mm, 1)
                pe.wait_ge(masked, 1)
                pe.wait_ge(consts, 8)
                pe.matmul(pcount[:, 0, :, :], tril[:], M[:], start=True, stop=True)
                pe.matmul(pcount[:, 1, :, :], allone[:], M[:], start=True, stop=True).then_inc(counted, 1)
                pe.wait_ge(weight_made, 2)
                for t in range(NT):
                    pe.wait_ge(lo_made, t + 1)
                    pe.wait_ge(number_made, 2 * t + 2)
                    if t % 4 == 0:
                        pe.wait_ge(low_weight_made, t // 4 + 1)
                    for e in range(NE):
                        last = pe.matmul(ptab[:, e, 0:KINDS * HI], hot_lo[t % 3][:, e, :],
                                         kind[:, t, e].rearrange("p k h -> p (k h)"), start=(t == 0 and e % 4 == 0),
                                         stop=(t == NT - 1 and e % 4 == 3), skip_group_check=True)
                    last.then_inc(tab_mm, 1)

            @block.vector
            def _(dve):
                chain = Chain(dve, step)

                def do(ins):
                    chain.step(ins)
                    chain.wait()

                def pairs_by_expert():
                    do(dve.tensor_scalar(cnt[:], cnt[:], PAIR - 1.0, float(PAIR), ALU.add, ALU.max))
                    do(dve.tensor_copy(tables.pairs[:, 0, :], cnt[:]))
                    do(dve.tensor_scalar(tables.pairs[:, 0, :], tables.pairs[:, 0, :], 8, None, ALU.arith_shift_right))
                    do(dve.tensor_copy(cnt[:], tables.pairs[:, 0, :]))
                    do(dve.tensor_tensor(ahead[:, 0], bc(cnt[:].unsqueeze(1), [P, NE, NE]), before[:], ALU.mult))
                    do(dve.tensor_reduce(rank[:, 0, :], ahead[:, 0], AXX, ALU.add))
                    dve.tensor_copy(tables.pairs[:, 1, :], rank[:, 0, :]).then_inc(paired, 1)

                do(dve.memset(ahead[:], 0.0))

                for g in range(GROUPS):
                    norm.statistics(dve, x_sb, g)
                    for t in range(NT)[g * NT // GROUPS:(g + 1) * NT // GROUPS]:
                        dve.tensor_scalar(xn[:, t, :], x_sb[:, t, :], norm.mv[:, t, 0:1], norm.rstd[:, t:t + 1],
                                          ALU.subtract, ALU.mult).then_inc(xn_made, 1)
                for c in range(weights.NC):
                    weights.low(dve, 0, c)
                dve.wait_ge(lg_out[0], NT // 2)
                dve.wait_ge(lg_out[1], NT // 2)
                do(dve.tensor_reduce(top[:], lg[:, :, 0:NE], AXX, ALU.max))
                dve.tensor_tensor(V[:], lg[:, :, 0:NE], bc(top[:].unsqueeze(2), [P, NT, NE]), ALU.subtract).then_inc(to_exp, 1)
                if actor:
                    dve.wait_ge(w_in, 64)
                    dve.tensor_tensor(ah[:], lg[:, :, NE:R], bc(b1[:].unsqueeze(1), [P, NT, A]), ALU.add).then_inc(a_in, 1)
                dve.wait_ge(from_exp, 1)
                if actor:
                    do(dve.tensor_reduce(tot[:], V[:], AXX, ALU.add))
                    do(dve.reciprocal(top[:], tot[:]))
                    do(dve.tensor_tensor(V[:], V[:], bc(top[:].unsqueeze(2), [P, NT, NE]), ALU.mult))
                    by = V[:]
                else:
                    by = lg[:, :, 0:NE]
                for e in range(NE):
                    for rest_of, op in (((0, e), ALU.is_ge), ((e + 1, NE), ALU.is_gt)):
                        a, b = rest_of
                        if b > a:
                            chain.step(dve.tensor_tensor(ahead[:, :, e, a:b], by[:, :, a:b],
                                                         bc(by[:, :, e:e + 1], [P, NT, b - a]), op))
                chain.wait()
                do(dve.tensor_reduce(rank[:], ahead[:], AXX, ALU.add))
                if actor:
                    dve.wait_ge(a2_mm, 1)
                    do(dve.tensor_tensor(al[:], pl[0][:, 0:NT * AK].rearrange("p (t k) -> p t k", k=AK),
                                         bc(b2[:].unsqueeze(1), [P, NT, AK]), ALU.add))
                    do(dve.tensor_scalar(al[:], al[:], -30.0, 30.0, ALU.max, ALU.min))
                    do(dve.tensor_reduce(tot[:], al[:], AXX, ALU.max))
                    do(dve.tensor_tensor(al[:], al[:], bc(tot[:].unsqueeze(2), [P, NT, AK]), ALU.is_equal))
                    dve.wait_ge(lanes_made, 1)
                    do(dve.tensor_tensor(al[:], al[:], bc(number[:].unsqueeze(1), [P, NT, AK]), ALU.mult))
                    do(dve.tensor_reduce(tot[:], al[:], AXX, ALU.min))
                    do(dve.tensor_scalar(tot[:], tot[:], AK + 1.0, None, ALU.add))
                    dve.tensor_tensor(M[:], rank[:], bc(tot[:].unsqueeze(2), [P, NT, NE]), ALU.is_lt).then_inc(masked, 1)
                    dve.wait_ge(masked, 1)
                    do(dve.tensor_tensor(W[:], V[:], M[:], ALU.mult))
                else:
                    dve.tensor_scalar(M[:], rank[:], 2.0, None, ALU.is_lt).then_inc(masked, 1)
                    dve.wait_ge(masked, 1)
                    do(dve.tensor_tensor(W[:], V[:], M[:], ALU.mult))
                    do(dve.tensor_reduce(tot[:], W[:], AXX, ALU.add))
                    do(dve.reciprocal(top[:], tot[:]))
                    do(dve.tensor_tensor(W[:], W[:], bc(top[:].unsqueeze(2), [P, NT, NE]), ALU.mult))
                do(dve.tensor_copy(piece[0][:], W[:]))
                do(dve.tensor_tensor(rest[0][:], W[:], piece[0][:], ALU.subtract))
                do(dve.tensor_copy(piece[1][:], rest[0][:]))
                do(dve.tensor_tensor(piece[2][:], rest[0][:], piece[1][:], ALU.subtract))
                dve.wait_ge(counted, 1)
                do(dve.tensor_copy(cum[0][:], pcount[:, 1, :, :]))
                src = 0
                for d in (1, 2, 4, 8):
                    a, b = cum[src], cum[1 - src]
                    do(dve.tensor_copy(b[:, 0:d, :], a[:, 0:d, :]))
                    do(dve.tensor_tensor(b[:, d:NT, :], a[:, d:NT, :], a[:, 0:NT - d, :], ALU.add))
                    src = 1 - src
                incl = cum[src]
                do(dve.tensor_copy(cnt[:], incl[:, NT - 1, :]))
                do(dve.tensor_copy(slot[:, 0:1, :], pcount[:, 0, 0:1, :]))
                do(dve.tensor_tensor(slot[:, 1:NT, :], pcount[:, 0, 1:NT, :], incl[:, 0:NT - 1, :], ALU.add))
                do(dve.tensor_scalar(slot[:], slot[:], 1.0, None, ALU.add))
                do(dve.tensor_tensor(slot[:], slot[:], M[:], ALU.mult))
                do(dve.tensor_scalar(slot[:], slot[:], -1.0, None, ALU.add))
                do(dve.tensor_copy(sloti[:], slot[:]))
                do(dve.tensor_scalar(parti[:, 0], sloti[:], P - 1, None, ALU.bitwise_and))
                do(dve.tensor_scalar(parti[:, 1], sloti[:], 7, None, ALU.arith_shift_right))
                dve.tensor_copy(part[:], parti[:]).then_inc(parts_ready, 1)
                dve.wait_ge(parts_ready, 1)
                dve.tensor_tensor(hot_hi[:].rearrange("p t e h -> p (t e) h"),
                                  bc(lanes[:, 0:HI].unsqueeze(1), [P, NT * NE, HI]),
                                  bc(part[:, 1].rearrange("p t e -> p (t e)").unsqueeze(2), [P, NT * NE, HI]),
                                  ALU.is_equal).then_inc(parts_ready, 1)
                dve.wait_ge(parts_ready, 2)
                for n in range(2):
                    dve.tensor_tensor(kind[:, :, :, 2 + n, :], hot_hi[:], bc(piece[n][:].unsqueeze(3), [P, NT, NE, HI]),
                                      ALU.mult).then_inc(weight_made, 1)
                for t in range(NT):
                    if t >= 3:
                        dve.wait_ge(tab_mm, t - 2)
                    dve.tensor_tensor(hot_lo[t % 3][:], bc(lanes[:].unsqueeze(1), [P, NE, P]),
                                      bc(part[:, 0, t, :].unsqueeze(2), [P, NE, P]), ALU.is_equal).then_inc(lo_made, 1)
                    if t == 2:
                        pairs_by_expert()
                dve.wait_ge(packing, NE)
                do(dve.tensor_tensor(found[:], packed[:, 0, :], packed[:, 1, :], ALU.add))
                do(dve.tensor_scalar(tables.gather[:], found[:], -1.0, 0.0, ALU.add, ALU.max))
                do(dve.tensor_scalar(rowf[:], found[:], 0.0, spare[:, 0:1], ALU.is_equal, ALU.mult))
                do(dve.tensor_tensor(rowf[:], rowf[:], found[:], ALU.add))
                do(dve.tensor_scalar(tables.scatter[:], rowf[:], -1.0, None, ALU.add))
                do(dve.tensor_tensor(rowf[:], packed[:, 3, :], packed[:, 4, :], ALU.add))
                do(dve.tensor_tensor(tables.weight[:], rowf[:], packed[:, 2, :], ALU.add))


class Weights:

    def __init__(self, m, gu, dn, inner, cw):
        self.gu, self.dn, self.inner, self.cw, self.NC = gu, dn, inner, cw, inner // cw
        self.graw = m.sb("graw", [P, FC, 2 * inner])
        self.draw = m.sb("draw", [cw, self.NC, D])
        self.gh, self.gl = ([m.sb(f"g{x}{n}", [P, FC, 2 * inner], F32R) for n in range(2)] for x in "hl")
        self.dh, self.dl = ([m.sb(f"d{x}{n}", [cw, self.NC, D], F32R) for n in range(2)] for x in "hl")
        self.raw_in, self.hi_made, self.lo_made = m.sem("raw_in"), m.sem("hi_made"), m.sem("lo_made")

    def load(self, sp, e):
        if e >= 1:
            sp.wait_ge(self.lo_made, 2 * self.NC * e)
        sp.dma_start(self.graw[:], self.gu[e].rearrange("(c p) n -> p c n", p=P)).then_inc(self.raw_in, 16)
        sp.dma_start(self.draw[:], self.dn[e].rearrange("(c p) n -> p c n", p=self.cw)).then_inc(self.raw_in, 16)

    def slices(self, e, c):
        g = slice(2 * self.cw * c, 2 * self.cw * (c + 1))
        return ((self.graw[:, :, g], self.gh[e % 2][:, :, g], self.gl[e % 2][:, :, g]),
                (self.draw[:, c, :], self.dh[e % 2][:, c, :], self.dl[e % 2][:, c, :]))

    def high(self, act, e, c):
        act.wait_ge(self.raw_in, 32 * (e + 1))
        for raw, hi, lo in self.slices(e, c):
            act.activation(hi, raw, ACT.Copy).then_inc(self.hi_made, 1)

    def low(self, dve, e, c):
        dve.wait_ge(self.hi_made, 2 * (self.NC * e + c + 1))
        for raw, hi, lo in self.slices(e, c):
            dve.tensor_tensor(lo, raw, hi, ALU.subtract).then_inc(self.lo_made, 1)


def experts(nc, tag, ident, tables, rows, acc, weights):
    NC, cw, inner = weights.NC, weights.cw, weights.inner
    gh, gl, dh, dl = weights.gh, weights.gl, weights.dh, weights.dl
    with Mem(nc, tag) as m:
        gidx = m.sb("gidx", [P, 2], I32)
        sidx = m.sb("sidx", [P, 2], I32)

        xg = m.sb("xg", [P, 2, D])
        xh = m.sb("xh", [P, FC, PAIR], F32R)
        xl = m.sb("xl", [P, FC, PAIR], F32R)
        sg = [m.sb(f"sg{n}", [cw, PAIR]) for n in range(2)]
        hf = [m.sb(f"hf{n}", [cw, PAIR]) for n in range(2)]
        hh = m.sb("hh", [cw, NC, PAIR], F32R)
        hl = m.sb("hl", [cw, NC, PAIR], F32R)
        ys = m.sb("ys", [P, 2, D])
        px = m.ps("px", [P, FC, PAIR])
        NG = min(NC, 3)
        pg = [m.ps(f"pg{n}", [P, 2, PAIR]) for n in range(NG)]
        py = m.ps("py", [P, 2, D])

        index_made, gathered, scattered = m.sem("index_made"), m.sem("gathered"), m.sems("scattered")
        settled = m.sem("settled")
        x_mm, xh_made, xl_made = m.sem("x_mm"), m.sem("xh_made"), m.sem("xl_made")
        g_mm, silued, timed, hh_made, hl_made = (m.sem(n) for n in ("g_mm", "silued", "timed", "hh_made", "hl_made"))
        y_mm, y_out = m.sem("y_mm"), m.sem("y_out")

        def each(eng, body, between=None, opening=None):
            for e in range(NE):
                n = eng.value_load(tables.pairs[0:1, 0, e:e + 1], min_val=1, max_val=T // PAIR)
                first = eng.value_load(tables.pairs[0:1, 1, e:e + 1], min_val=e, max_val=e * (T // PAIR))
                if between:
                    between(e)
                if opening:
                    opening(e, first)
                with eng.Fori(1 if opening else 0, n) as i:
                    body(e, first + i)

        with nc.Block() as block:
            @block.sync
            def _(sp):
                for e in range(2, NE):
                    weights.load(sp, e)
                sp.wait_ge(weights.raw_in, 32 * NE)

            @block.gpsimd
            def _(pool):
                def settle(sem, value):
                    pool.wait_ge(sem, value)
                    pool.sem_inc(settled, 1)

                def gather(q, k):
                    pool.tensor_copy(gidx[:], tables.gather[:, bass.ds(2 * q, 2)]).then_inc(index_made, 1)
                    settle(index_made, k)
                    for t in range(2):
                        pool.indirect_dma_start(out=xg[:, t, :], out_offset=None, in_=rows,
                                                in_offset=bass.IndirectOffsetOnAxis(ap=gidx[:, t:t + 1], axis=0)
                                                ).then_inc(gathered, 16)

                def pair(e, q):
                    settle(x_mm, q + 2)
                    gather(q + 2, 2 * q + 3)
                    settle(y_out, 2 * q + 2)
                    for t in range(2):
                        settle(scattered[t], 16 * q + 16)
                    pool.tensor_copy(sidx[:], tables.scatter[:, bass.ds(2 * q, 2)]).then_inc(index_made, 1)
                    settle(index_made, 2 * q + 4)
                    for t in range(2):
                        pool.indirect_dma_start(out=acc[t], out_offset=bass.IndirectOffsetOnAxis(ap=sidx[:, t:t + 1], axis=0),
                                                in_=ys[:, t, :], in_offset=None, compute_op=ALU.add
                                                ).then_inc(scattered[t], 16)



                for t in range(2):
                    pool.dma_start(sidx[:, t:t + 1], tables.scatter[:, t:t + 1]).then_inc(scattered[t], 16)
                gather(0, 1)
                settle(x_mm, 1)
                gather(1, 2)
                each(pool, pair)
                total = pool.value_load(tables.pairs[0:1, 1, NE - 1:NE], min_val=NE - 1, max_val=COLS // 2) \
                    + pool.value_load(tables.pairs[0:1, 0, NE - 1:NE], min_val=1, max_val=T // PAIR)
                for t in range(2):
                    settle(scattered[t], 16 * total + 16)
                settle(gathered, 32 * total + 64)

            @block.tensor
            def _(pe):
                def transposes(q):
                    pe.wait_ge(gathered, 32 * q + 32)
                    for t in range(2):
                        for c in range(FC):
                            last = pe.transpose(px[:, c, t * P:(t + 1) * P], xg[:, t, c * P:(c + 1) * P], ident[:])
                    last.then_inc(x_mm, 1)

                def pair(e, q):
                    n = e % 2
                    pe.wait_ge(xl_made, q + 1)
                    for c in range(NC):
                        if c >= NG:
                            pe.wait_ge(timed, NC * q + c - NG + 1)
                        for s in range(2):
                            cols = slice(s * inner + c * cw, s * inner + (c + 1) * cw)
                            last = three_products(pe, pg[c % NG][0:cw, s, :],
                                                  (lambda f: gh[n][:, f, cols], lambda f: gl[n][:, f, cols]),
                                                  (lambda f: xh[:, f, :], lambda f: xl[:, f, :]), range(FC), True, True)
                        last.then_inc(g_mm, 1)
                    transposes(q + 1)
                    for c in range(NC):
                        pe.wait_ge(hl_made, NC * q + c + 1)
                        for t in range(2):
                            cols = slice(t * P, (t + 1) * P)
                            for k, (a, b) in enumerate(((hh, dh[n]), (hl, dh[n]), (hh, dl[n]))):
                                last = pe.matmul(py[:, t, :], a[:, c, cols], b[:, c, :], start=(c == 0 and t == 0 and k == 0),
                                                 stop=(c == NC - 1 and k == 2), skip_group_check=True)
                    last.then_inc(y_mm, 1)

                def between(e):
                    pe.wait_ge(weights.lo_made, 2 * NC * (e + 1))

                transposes(0)
                each(pe, pair, between)

            @block.scalar
            def _(act):
                def xhigh(q):
                    act.wait_ge(x_mm, q + 1)
                    act.activation(xh[:], px[:], ACT.Copy).then_inc(xh_made, 1)

                def opening(e, q):
                    if e >= 1:
                        act.wait_ge(y_mm, q)
                    pair(e, q, split=e + 1 < NE)

                def pair(e, q, split=False):
                    for c in range(NC):
                        k = NC * q + c + 1
                        act.wait_ge(g_mm, k)
                        act.activation(sg[c % 2][:], pg[c % NG][0:cw, 0, :], ACT.Silu).then_inc(silued, 1)
                        if split:
                            weights.high(act, e + 1, c)
                        act.wait_ge(timed, k)
                        act.activation(hh[:, c, :], hf[c % 2][:], ACT.Copy).then_inc(hh_made, 1)
                    xhigh(q + 1)

                xhigh(0)
                each(act, pair, opening=opening)

            @block.vector
            def _(dve):
                def xlow(q):
                    dve.wait_ge(xh_made, q + 1)
                    dve.tensor_tensor(xl[:], px[:], xh[:], ALU.subtract).then_inc(xl_made, 1)

                def opening(e, q):
                    pair(e, q, split=e + 1 < NE)

                def pair(e, q, split=False):
                    for c in range(NC):
                        k = NC * q + c + 1
                        dve.wait_ge(silued, k)
                        dve.tensor_tensor(hf[c % 2][:], pg[c % NG][0:cw, 1, :], sg[c % 2][:], ALU.mult).then_inc(timed, 1)
                        if split:
                            weights.low(dve, e + 1, c)
                        dve.wait_ge(hh_made, k)
                        dve.tensor_tensor(hl[:, c, :], hf[c % 2][:], hh[:, c, :], ALU.subtract).then_inc(hl_made, 1)
                    xlow(q + 1)
                    dve.wait_ge(y_mm, q + 1)
                    for t in range(2):
                        dve.wait_ge(scattered[t], 16 * q + 16)
                        dve.tensor_scalar(ys[:, t, :], py[:, t, :], tables.weight[:, bass.ds(2 * q + t, 1)], None,
                                          ALU.mult).then_inc(y_out, 1)

                xlow(0)
                each(dve, pair, opening=opening)


def moe(nc, tag, x_sb, ident, rows, acc, router, actor, gu, dn, inner, cw):
    with Mem(nc, tag) as m:
        tables = Tables(m)
        weights = Weights(m, gu, dn, inner, cw)
        route(nc, tag + "route", x_sb, ident, tables, weights, rows, acc, router, actor)
        experts(nc, tag + "experts", ident, tables, rows, acc, weights)


def attention(nc, tag, x_sb, c_sb, ctx_sb, va, ident, scratch, wq, wk, wv, bqk, bv, wo=None, bo=None):
    names = ["q", "k", "v"] + (["o"] if wo is not None else [])
    with Mem(nc, tag) as m:
        hi = {n: m.sb(f"w{n}h", [P, FC, D], F32R) for n in names}
        lo = {n: m.sb(f"w{n}l", [P, FC, D], F32R) for n in names}
        with Mem(nc, tag + "raw") as r:
            raws = [r.sb(f"w{n}", [P, FC, D]) for n in names]
            split_weights(nc, tag + "split", [x[:] for x in raws], [hi[n][:] for n in names], [lo[n][:] for n in names],
                          [w.rearrange("(c p) n -> p c n", p=P) for w in (wq, wk, wv, wo)[:len(names)]])
        project(nc, tag + "project", x_sb, c_sb, va, ident,
                [part[n] for n in "qkv" for part in (hi, lo)], bqk, bv, scratch)
        attend(nc, tag + "attend", x_sb, ctx_sb, va, ident, scratch, bo)
        if wo is not None:
            project_out(nc, tag + "out", x_sb, ctx_sb, ident, (hi["o"], lo["o"]))


def reload(nc, tag, x_sb, acc, out=None):
    Q = 4
    with Mem(nc, tag) as m:
        half = m.sb("half", [P, NT, D])
        loaded, summed, stored = m.sems("loaded", Q), m.sem("summed"), m.sem("stored")
        tiles = [slice(q * NT // Q, (q + 1) * NT // Q) for q in range(Q)]

        def dram(ap, q):
            return ap[q * T // Q:(q + 1) * T // Q, :].rearrange("(n p) d -> p n d", p=P)

        with nc.Block() as block:
            @block.sync
            def _(sp):
                for q in range(Q):
                    sp.dma_start(x_sb[:, tiles[q], :], dram(acc[0], q)).then_inc(loaded[q], 16)
                    sp.dma_start(half[:, tiles[q], :], dram(acc[1], q)).then_inc(loaded[q], 16)
                for q in range(Q if out is not None else 0):
                    sp.wait_ge(summed, q + 1)
                    sp.dma_start(dram(out, q), x_sb[:, tiles[q], :]).then_inc(stored, 16)
                if out is not None:
                    sp.wait_ge(stored, 16 * Q)

            @block.vector
            def _(dve):
                for q in range(Q):
                    dve.wait_ge(loaded[q], 32)
                    dve.tensor_tensor(x_sb[:, tiles[q], :], x_sb[:, tiles[q], :], half[:, tiles[q], :],
                                      ALU.add).then_inc(summed, 1)


def build(nc, a, out, stages):
    Mem.held = []
    scratch = [nc.dram_tensor(n, (B, 2, P, S), F32, kind="Internal").ap() for n in ("qh", "ql", "kh", "kl")]
    rows = [nc.dram_tensor(f"rows{n}", (T, D), F32, kind="Internal").ap() for n in range(2)]
    acc = [[nc.dram_tensor(f"acc{n}{t}", (T + P, D), F32, kind="Internal").ap() for t in range(2)] for n in range(2)]
    with Mem(nc, "all") as m:
        ident = m.sb("ident", [P, P])
        x_sb = m.sb("x", [P, NT, D])
        with Mem(nc, "attn") as t:
            c_sb = t.sb("c", [P, FC, T])
            ctx_sb = t.sb("ctx", [P, NT, D])
            va = t.sb("va", [P, NT, NH, VW])
            constants(nc, ident, x_sb, c_sb, va, a["x"], a["ctx_t"])
            if 0 in stages:
                attention(nc, "a0", x_sb, c_sb, ctx_sb, va, ident, scratch,
                          a["wq0"], a["wk0"], a["wv0"], a["bqk0"], a["bv0"], a["wo0"], a["bo0"])
            if 1 in stages:
                moe(nc, "m0", x_sb, ident, rows[0], acc[0], a["router0"], None, a["gu0"], a["dn0"], I0, P)
                reload(nc, "back", x_sb, acc[0])
            Mem.release(nc)
            if 2 in stages:
                attention(nc, "a1", x_sb, c_sb, ctx_sb, va, ident, scratch,
                          a["wq1"], a["wk1"], a["wv1"], a["bqk1"], a["bv1"])
        if 3 in stages:
            moe(nc, "m1", x_sb, ident, rows[1], acc[1], a["router1"],
                {"w1n": A1, "b1": a["ab1"], "b2": a["ab2"], "w2": a["aw2"]}, a["gu1"], a["dn1"], I1, 112)
            reload(nc, "last", x_sb, acc[1], out)
            return
        done = m.sem("stored")
        with nc.Block() as block:
            @block.sync
            def _(sp):
                sp.dma_start(out[0:T, :].rearrange("(n p) d -> p n d", p=P), x_sb[:]).then_inc(done, 16)
                sp.wait_ge(done, 16)


def layouts(v):
    import numpy as np

    def by_half(w):
        return w.reshape(-1, NP, 2, HD).transpose(0, 2, 1, 3).reshape(-1, D)

    a = {"x": v["x"].reshape(T, D), "ctx_t": v["ctx_1024"].reshape(T, D).T}
    for n, l in enumerate(("L0_xattn_", "L1_xattn_")):
        a[f"wq{n}"], a[f"wk{n}"], a[f"wv{n}"] = by_half(v[l + "Wq"]), by_half(v[l + "Wk"]), v[l + "Wv"]
        a[f"bqk{n}"] = np.concatenate([by_half(v[l + x][None])[0].reshape(2, P) for x in ("bq", "bk")]).T
        a[f"bv{n}"] = v[l + "bv"]
    a["wo0"], a["bo0"] = v["L0_xattn_Wo"], v["L0_xattn_bo"]
    a["router0"] = v["L0_ffn_router_weight"].T
    a["gu0"], a["dn0"] = v["L0_ffn_w1"].transpose(0, 2, 1), v["L0_ffn_w2"].transpose(0, 2, 1)
    a["router1"] = np.concatenate([v["L1_ffn_router_w"], v["L1_ffn_actor_w1"]]).T
    a["ab1"], a["ab2"], a["aw2"] = v["L1_ffn_actor_b1"], v["L1_ffn_actor_b2"], v["L1_ffn_actor_w2"].T
    a["gu1"] = np.concatenate([v["L1_ffn_gate_w"], v["L1_ffn_up_w"]], axis=1).transpose(0, 2, 1)
    a["dn1"] = v["L1_ffn_down_w"].transpose(0, 2, 1)
    return {k: np.ascontiguousarray(x) for k, x in a.items()}


STAGES = (0, 1, 2, 3)


def kernel(**inputs):
    import numpy as np
    import concourse.bacc as bacc
    from concourse.bass_utils import run_bass_kernel_spmd

    arrays = layouts({k: np.asarray(x) for k, x in inputs.items()})
    nc = bacc.Bacc("TRN2", target_bir_lowering=False, num_devices=1)
    aps = {k: nc.dram_tensor(f"in_{k}", x.shape, mybir.dt.from_np(x.dtype), kind="ExternalInput").ap()
           for k, x in arrays.items()}
    out = nc.dram_tensor("out", (T, D), F32, kind="ExternalOutput").ap()
    build(nc, aps, out, STAGES)
    r = run_bass_kernel_spmd(nc, [{f"in_{k}": x for k, x in arrays.items()}], core_ids=[0])
    return r.results[0]["out"].reshape(B, S, D)
```

```python
import concourse.bass as bass
from concourse import mybir
from contextlib import ExitStack

F32 = mybir.dt.float32
F32R = mybir.dt.float32r
BF16 = mybir.dt.bfloat16
I32 = mybir.dt.int32
ALU = mybir.AluOpType
ACT = mybir.ActivationFunctionType
AXX = mybir.AxisListType.X

P = 128
B, S, D = 8, 256, 256
T = B * S
NT = T // P
TB = S // P
FC = D // P
NH, HD = 16, 16
NP = NH // 2
KR = 3 * HD
VW = 32
EPS = 1e-5
SCORE_SCALE = 0.25
GROUPS = 4
STEPS = 7
NBUF = 4
DIRECT = 2
BANKS = 3
LEAD = 12


class Mem:

    held = []

    def __init__(self, nc, tag):
        self.nc, self.tag, self.stack = nc, tag, ExitStack()

    def __enter__(self):
        return self

    def __exit__(self, *a):
        self.stack.close()

    def sb(self, name, shape, dt=F32):
        return self.stack.enter_context(self.nc.sbuf_tensor(f"{self.tag}_{name}", shape, dt))

    def ps(self, name, shape, dt=F32):
        return self.stack.enter_context(self.nc.psum_tensor(f"{self.tag}_{name}", shape, dt))

    def sem(self, name):
        Mem.held.append(self.nc.alloc_semaphore(f"{self.tag}_{name}"))
        return Mem.held[-1]

    @staticmethod
    def release(nc):
        nc.clear_and_free_semaphores(Mem.held)
        Mem.held = []
        nc.all_engine_barrier()

    def sems(self, name, n=2):
        return [self.sem(f"{name}{i}") for i in range(n)]


class Chain:

    def __init__(self, eng, sem):
        self.eng, self.sem, self.n = eng, sem, 0

    def step(self, ins):
        self.n += 1
        ins.then_inc(self.sem, 1)

    def wait(self):
        self.eng.wait_ge(self.sem, self.n)


def wait(eng, sem, value):
    if not (isinstance(value, int) and value <= 0):
        eng.wait_ge(sem, value)


class Norm:

    def __init__(self, m):
        self.st = m.sb("st", [P, NT, 6])
        self.mv = m.sb("mv", [P, NT, 2])
        self.ve = m.sb("ve", [P, NT])
        self.root_sb = m.sb("root", [P, NT])
        self.y = m.sb("y", [P, NT])
        self.z = m.sb("z", [P, NT])
        self.rstd = m.sb("rstd", [P, NT])
        self.shift = m.sb("shift", [P, NT])
        self.stats, self.aggr, self.steps, self.rooted = (m.sem(n) for n in ("stats", "aggr", "steps", "rooted"))

    def statistics(self, dve, x_sb, g):
        n = NT // GROUPS
        tiles = slice(n * g, n * g + n)
        for t in range(NT)[tiles]:
            dve.bn_stats(self.st[:, t, :], x_sb[:, t, :]).then_inc(self.stats, 1)
        dve.wait_ge(self.stats, n * g + n)
        for t in range(NT)[tiles]:
            dve.bn_aggr(self.mv[:, t, :], self.st[:, t, :]).then_inc(self.aggr, 1)
        dve.wait_ge(self.aggr, n * g + n)
        ve, y, z = self.ve[:, tiles], self.y[:, tiles], self.z[:, tiles]
        dve.tensor_scalar(ve, self.mv[:, tiles, 1], EPS, None, ALU.add).then_inc(self.steps, 1)
        dve.wait_ge(self.rooted, g + 1)
        dve.reciprocal(y, self.root_sb[:, tiles]).then_inc(self.steps, 1)
        dve.wait_ge(self.steps, STEPS * g + 2)
        dve.tensor_tensor(z, y, y, ALU.mult).then_inc(self.steps, 1)
        dve.wait_ge(self.steps, STEPS * g + 3)
        dve.tensor_tensor(z, z, ve, ALU.mult).then_inc(self.steps, 1)
        dve.wait_ge(self.steps, STEPS * g + 4)
        dve.tensor_scalar(z, z, -0.5, 1.5, ALU.mult, ALU.add).then_inc(self.steps, 1)
        dve.wait_ge(self.steps, STEPS * g + 5)
        dve.tensor_tensor(self.rstd[:, tiles], z, y, ALU.mult).then_inc(self.steps, 1)
        dve.wait_ge(self.steps, STEPS * g + 6)
        dve.scalar_tensor_tensor(out=self.shift[:, tiles], in0=self.mv[:, tiles, 0], scalar=-1.0, in1=self.rstd[:, tiles],
                                 op0=ALU.mult, op1=ALU.mult).then_inc(self.steps, 1)

    def normalise(self, act, out, x_sb, tile, g):
        act.wait_ge(self.steps, STEPS * (g + 1))
        return act.activation(out, x_sb[:, tile, :], ACT.Identity, bias=self.shift[:, tile:tile + 1],
                              scale=self.rstd[:, tile:tile + 1])

    def root(self, act, g):
        tiles = slice(NT // GROUPS * g, NT // GROUPS * (g + 1))
        act.wait_ge(self.steps, STEPS * g + 1)
        act.activation(self.root_sb[:, tiles], self.ve[:, tiles], ACT.Sqrt).then_inc(self.rooted, 1)


def identity(pool, ident, zeroed):
    pool.memset(ident[:], 0.0).then_inc(zeroed, 1)
    pool.wait_ge(zeroed, 1)
    return pool.affine_select(out=ident[:], in_=ident[:], compare_op=ALU.not_equal, fill=1.0, base=0,
                              pattern=[[-1, P]], channel_multiplier=1)


class Operands:

    def __init__(self, m, parts):
        self.parts = parts
        self.qs = [m.sb(f"qs{n}", [P, NP, S], F32R) for n in range(NBUF)]
        self.ks = [m.sb(f"ks{n}", [P, NP, S], F32R) for n in range(NBUF)]
        self.q_in, self.k_in = m.sems("q_in", NBUF), m.sems("k_in", NBUF)

    def kinds(self, n):
        return (self.qs, (0, 0, 1)) if n == 0 else (self.ks, (0, 1, 0))

    def stack(self, sp, n, b, part, j, src, done):
        bufs, kinds = self.kinds(n)
        for r, kind in enumerate(kinds):
            if kind == part:
                row = 64 * j + HD * r
                sp.dma_start(bufs[b % NBUF][row:row + HD, :, :].bitcast(F32), src).then_inc(done, 16)

    def load(self, sp, b):
        for n, done in enumerate((self.q_in, self.k_in)):
            for j in range(2):
                for part in range(2):
                    src = self.parts[2 * n + part][b, j].rearrange("(d p) s -> d p s", p=NP)
                    self.stack(sp, n, b, part, j, src, done[b % NBUF])

    def load_ones(self, sp, ones, done):
        for n in range(NBUF):
            for j in range(2):
                row = 64 * j + KR
                sp.dma_start(self.ks[n][row:row + 1, :, :].bitcast(F32), ones[:]).then_inc(done, 16)

    def wait(self, eng, b):
        loads = b // NBUF + (b % NBUF >= DIRECT)
        if loads:
            eng.wait_ge(self.q_in[b % NBUF], 96 * loads)
            eng.wait_ge(self.k_in[b % NBUF], 96 * loads)


def three_products(pe, out, lhs, rhs, terms, start, stop):
    n = len(terms)
    for a, t in enumerate(terms):
        lh, ll = lhs[0](t), lhs[1](t)
        rh, rl = rhs[0](t), rhs[1](t)
        pe.matmul(out, lh, rh, start=start and a == 0, stop=False)
        pe.matmul(out, ll, rh, start=False, stop=False)
        last = pe.matmul(out, lh, rl, start=False, stop=stop and a == n - 1)
    return last


def project(nc, tag, x_sb, c_sb, ctx_sb, va, ident, his, los, srcs, bqk, bv, operands, first=None, acc=None):
    H = B // 2
    GT = NT // GROUPS
    nw = len(srcs)
    with Mem(nc, tag) as m:
        (wkh, wvh, wqh), (wkl, wvl, wql) = his[:3], los[:3]
        parts = operands.parts
        halves = [ctx_sb[:, GT * n:GT * (n + 1), :] for n in range(GROUPS)]
        raw = m.sb("raw", [P, FC * nw, D]) if acc is not None else ctx_sb
        raws = [raw[:, FC * n:FC * (n + 1), :] for n in range(nw)]
        bvb = m.sb("bvb", [P, D])
        bqk_sb = m.sb("bqk", [P, 4])
        ones = m.sb("ones", [NP, S])
        xn = [m.sb(f"xn{u}", [P, TB, D]) for u in range(2)]
        norm = Norm(m)
        xh = [m.sb(f"xh{u}", [P, FC, S], F32R) for u in range(2)]
        xl = [m.sb(f"xl{u}", [P, FC, S], F32R) for u in range(2)]
        ch = [m.sb(f"ch{u}", [P, FC, S], F32R) for u in range(2)]
        cl = [m.sb(f"cl{u}", [P, FC, S], F32R) for u in range(2)]
        qkh = [[m.sb(f"{n}h{u}", [P, 2, S], F32R) for u in range(2)] for n in "qk"]
        qkl = [[m.sb(f"{n}l{u}", [P, 2, S], F32R) for u in range(2)] for n in "qk"]
        pt = [m.ps(f"pt{u}", [P, FC, S]) for u in range(2)]
        pq = [[m.ps(f"p{n}{u}", [P, 2, S]) for u in range(2)] for n in "qk"]
        pv = [m.ps(f"pv{u}", [P, TB, D]) for u in range(2)]

        biases, ones_made, zeroed, ident_made = (m.sem(n) for n in ("biases", "ones_made", "zeroed", "ident_made"))
        w_in, w_hi, w_lo = m.sems("w_in", nw), m.sem("w_hi"), m.sem("w_lo")
        c_in, x_in, summed = m.sems("c_in", H), m.sems("x_in", GROUPS), m.sem("summed")
        va_ones = m.sem("va_ones")
        ones_in = m.sem("ones_in")
        xn_ready, xt_ready = m.sems("xn_ready"), m.sems("xt_ready")
        xh_ready, xl_ready = m.sems("xh_ready"), m.sems("xl_ready")
        ch_ready, cl_ready = m.sems("ch_ready"), m.sems("cl_ready")
        mm_ready = [m.sems("q_mm"), m.sems("k_mm")]
        v_mm = m.sems("v_mm")
        hi_ready = [m.sems("qh_ready"), m.sems("kh_ready")]
        lo_ready = [m.sems("ql_ready"), m.sems("kl_ready")]
        v_ready = m.sems("v_ready")
        stored = [m.sems("q_stored"), m.sems("k_stored")]

        def stored_by(i):
            return 16 * (6 * min(i, DIRECT // 2) + 2 * max(i - DIRECT // 2, 0))

        def rounds(body):
            for i in range(H):
                body(i, i == H - 1)

        def after(i, u):
            return i + (u + 1) // 2, (u + 1) % 2

        with nc.Block() as block:
            @block.sync
            def _(sp):
                def weight(n):
                    sp.dma_start(raws[n], srcs[n].rearrange("(c p) n -> p c n", p=P)).then_inc(w_in[n], 16)

                def rows(ap, g):
                    return ap[g * GT * P:(g + 1) * GT * P, :].rearrange("(n p) d -> p n d", p=P)

                def context(i):
                    cols = slice(2 * S * i, 2 * S * (i + 1))
                    sp.dma_start(c_sb[:, :, cols], first[1][:, cols].rearrange("(c p) t -> p c t", p=P)).then_inc(c_in[i], 16)

                def tokens(g):
                    x = x_sb[:, GT * g:GT * (g + 1), :]
                    if first is not None:
                        sp.dma_start(x, rows(first[0], g)).then_inc(x_in[g], 16)
                    else:
                        sp.dma_start(x, rows(acc[0], g)).then_inc(x_in[g], 16)
                        sp.dma_start(halves[g], rows(acc[1], g)).then_inc(x_in[g], 16)

                weight(0)
                if first is not None:
                    context(0)
                weight(1)
                tokens(0)
                sp.dma_start(bqk_sb[:], bqk).then_inc(biases, 16)
                sp.dma_start(bvb[:], bv.partition_broadcast(P)).then_inc(biases, 16)
                weight(2)
                for g in range(1, GROUPS):
                    tokens(g)
                    if first is not None:
                        context(g)
                for n in range(3, nw):
                    weight(n)
                def store(n, b):
                    u, i = b % 2, b // 2
                    for part, (src, ready) in enumerate(((qkh[n][u], hi_ready[n][u]), (qkl[n][u], lo_ready[n][u]))):
                        sp.wait_ge(ready, 2 * i + 2)
                        if b < DIRECT:
                            for j in range(2):
                                operands.stack(sp, n, b, part, j, src[:, j, :].bitcast(F32), stored[n][u])
                        else:
                            sp.dma_start(parts[2 * n + part][b].rearrange("j r s -> r j s"),
                                         src[:].bitcast(F32)).then_inc(stored[n][u], 16)

                store(1, 0)
                for b in range(B):
                    if b + 1 < B:
                        store(1, b + 1)
                    store(0, b)
                    if b == DIRECT:
                        sp.wait_ge(ones_made, 1)
                        operands.load_ones(sp, ones, ones_in)
                sp.wait_ge(ones_in, 16 * 2 * NBUF)
                for n in range(2):
                    for u in range(2):
                        sp.wait_ge(stored[n][u], stored_by(H))

            @block.gpsimd
            def _(pool):
                for b in range(B):
                    u, i = b % 2, b // 2
                    if first is not None:
                        pool.wait_ge(c_in[i], 16)
                    wait(pool, v_mm[u], i)
                    c = c_sb[:, :, b * S:(b + 1) * S]
                    pool.tensor_copy(ch[u][:], c).then_inc(ch_ready[u], 1)
                    pool.wait_ge(ch_ready[u], i + 1)
                    pool.tensor_tensor(cl[u][:], c, ch[u][:], ALU.subtract).then_inc(cl_ready[u], 1)
                    if b == 0:
                        if first is not None:
                            identity(pool, ident, zeroed).then_inc(ident_made, 1)
                        pool.memset(ones[:], 1.0).then_inc(ones_made, 1)

            @block.vector
            def _(dve):
                def split(n):
                    dve.wait_ge(w_hi, n + 1)
                    dve.tensor_tensor(los[n][:], raws[n], his[n][:], ALU.subtract).then_inc(w_lo, 1)

                def total(g):
                    dve.wait_ge(x_in[g], 16 if first is not None else 32)
                    if first is None:
                        x = x_sb[:, GT * g:GT * (g + 1), :]
                        dve.tensor_tensor(x, x, halves[g], ALU.add).then_inc(summed, 1)
                        dve.wait_ge(summed, g + 1)

                def low(n, i, u):
                    for j in range(2):
                        dve.wait_ge(hi_ready[n][u], 2 * i + 2)
                        if j == 0:
                            wait(dve, stored[n][u], stored_by(i))
                        dve.scalar_tensor_tensor(out=qkl[n][u][:, j, :], in0=pq[n][u][:, j, :],
                                                 scalar=bqk_sb[:, 2 * n + j:2 * n + j + 1], in1=qkh[n][u][:, j, :],
                                                 op0=ALU.add, op1=ALU.subtract).then_inc(lo_ready[n][u], 1)

                def values(i, u):
                    dve.wait_ge(v_mm[u], i + 1)
                    for t in range(TB):
                        dve.tensor_tensor(
                            va[:, 2 * (2 * i + u) + t, :, 0:HD],
                            pv[u][:, t, :].rearrange("p (h d) -> p h d", h=NH),
                            bvb[:].rearrange("p (h d) -> p h d", h=NH), ALU.add).then_inc(v_ready[u], 1)

                if first is not None:
                    dve.memset(va[:, :, :, HD:VW], 1.0).then_inc(va_ones, 1)
                split(0)
                split(1)
                total(0)
                norm.statistics(dve, x_sb, 0)
                split(2)
                dve.wait_ge(biases, 32)
                low(1, 0, 0)
                values(0, 0)

                def batches(i, last):
                    for u in range(2):
                        end = last and u == 1
                        dve.wait_ge(xh_ready[u], i + 1)
                        dve.tensor_tensor(xl[u][:], pt[u][:], xh[u][:], ALU.subtract).then_inc(xl_ready[u], 1)
                        if u == 0 and not last:
                            total(i + 1)
                            norm.statistics(dve, x_sb, i + 1)
                        if not end:
                            low(1, *after(i, u))
                            values(*after(i, u))
                        low(0, i, u)
                    for n in range(3, nw) if i == 1 else ():
                        split(n)

                rounds(batches)

            @block.scalar
            def _(act):
                def high(n, i, u):
                    act.wait_ge(mm_ready[n][u], i + 1)
                    wait(act, stored[n][u], stored_by(i))
                    for j in range(2):
                        act.activation(qkh[n][u][:, j, :], pq[n][u][:, j, :], ACT.Identity,
                                       bias=bqk_sb[:, 2 * n + j:2 * n + j + 1]).then_inc(hi_ready[n][u], 1)

                def split(n):
                    act.wait_ge(w_in[n], 16)
                    act.activation(his[n][:], raws[n], ACT.Copy).then_inc(w_hi, 1)

                def normalise(i, u):
                    wait(act, xt_ready[u], i)
                    for t in range(TB):
                        norm.normalise(act, xn[u][:, t, :], x_sb, TB * (2 * i + u) + t, i).then_inc(xn_ready[u], 1)

                split(0)
                split(1)
                norm.root(act, 0)
                normalise(0, 0)
                split(2)
                act.wait_ge(biases, 32)
                high(1, 0, 0)

                def batches(i, last):
                    for u in range(2):
                        act.wait_ge(xt_ready[u], i + 1)
                        wait(act, mm_ready[0][u], i)
                        act.activation(xh[u][:], pt[u][:], ACT.Copy).then_inc(xh_ready[u], 1)
                        if u == 0 and not last:
                            norm.root(act, i + 1)
                        if not (last and u == 1):
                            normalise(*after(i, u))
                            high(1, *after(i, u))
                        high(0, i, u)
                    for n in range(3, nw) if i == 1 else ():
                        split(n)

                rounds(batches)

            @block.tensor
            def _(pe):
                def qk(n, wh, wl, ah, al, i, u):
                    wait(pe, lo_ready[n][u], 2 * i)
                    for j in range(2):
                        last = three_products(
                            pe, pq[n][u][:, j, :],
                            (lambda c: wh[:, c, j * P:(j + 1) * P], lambda c: wl[:, c, j * P:(j + 1) * P]),
                            (lambda c: ah[:, c, :], lambda c: al[:, c, :]), range(FC), True, True)
                    last.then_inc(mm_ready[n][u], 1)

                def of_context(i, u):
                    pe.wait_ge(cl_ready[u], i + 1)
                    qk(1, wkh, wkl, ch[u], cl[u], i, u)
                    if i == 0:
                        pe.wait_ge(w_lo, 2)
                    wait(pe, v_ready[u], 2 * i)
                    for t in range(TB):
                        last = three_products(
                            pe, pv[u][:, t, :],
                            (lambda c: ch[u][:, c, t * P:(t + 1) * P], lambda c: cl[u][:, c, t * P:(t + 1) * P]),
                            (lambda c: wvh[:, c, :], lambda c: wvl[:, c, :]), range(FC), True, True)
                    last.then_inc(v_mm[u], 1)

                pe.wait_ge(w_lo, 1)
                of_context(0, 0)
                if first is not None:
                    pe.wait_ge(ident_made, 1)

                def batches(i, last):
                    for u in range(2):
                        pe.wait_ge(xn_ready[u], 2 * i + 2)
                        wait(pe, xl_ready[u], i)
                        for t in range(TB):
                            for c in range(FC):
                                done = pe.transpose(pt[u][:, c, t * P:(t + 1) * P], xn[u][:, t, c * P:(c + 1) * P], ident[:])
                        done.then_inc(xt_ready[u], 1)
                        if not (last and u == 1):
                            of_context(*after(i, u))
                        if i == 0:
                            pe.wait_ge(w_lo, 3)
                        pe.wait_ge(xl_ready[u], i + 1)
                        qk(0, wqh, wql, xh[u], xl[u], i, u)

                rounds(batches)


def attend(nc, tag, x_sb, ctx_sb, va, ident, operands, bias=None):
    SLOTS = B * NP
    with Mem(nc, tag) as m:
        qs, ks = operands.qs, operands.ks
        pT = [m.sb(f"pT{n}", [P, 2, TB, S]) for n in range(4)]
        mx = [m.sb(f"mx{n}", [P, TB, NH]) for n in range(2)]
        nm = [m.sb(f"nm{n}", [NH, S], F32R) for n in range(2)]
        oT = [m.sb(f"oT{n}", [P, 2, 2 * S]) for n in range(2)]
        rs = m.sb("rs", [P, TB, NH])
        sc = [m.ps(f"sc{n}", [P, TB, S]) for n in range(BANKS)]
        sT = [m.ps(f"sT{n}", [P, TB * S]) for n in range(BANKS)]
        po = m.ps("po", [P, 2, S])
        pf = m.ps("pf", [P, 512])

        sc_mm, sc_max = m.sem("sc_mm"), m.sem("sc_max")
        mT_mm, nm_made, m_in = m.sem("mT_mm"), m.sem("nm_made"), m.sems("m_in", NBUF)
        sT_mm, exped = m.sem("sT_mm"), m.sem("exped")
        pv_mm, o_out = m.sem("pv_mm"), m.sem("o_out")
        oT_mm, recip, normed = m.sem("oT_mm"), m.sem("recip"), m.sem("normed")
        bias_in = m.sem("bias_in")
        bias_sb = m.sb("bias", [P, D]) if bias is not None else None

        with nc.Block() as block:
            @block.sync
            def _(sp):
                if bias is not None:
                    sp.dma_start(bias_sb[:], bias.partition_broadcast(P)).then_inc(bias_in, 16)
                def maxima(b):
                    n = b % NBUF
                    sp.wait_ge(nm_made, b + 1)
                    for j in range(2):
                        row = 64 * j + KR
                        sp.dma_start(qs[n][row:row + 1, :, :].bitcast(F32), nm[b % 2][NP * j:NP * j + NP, :].bitcast(F32)).then_inc(m_in[n], 16)

                for b in range(DIRECT, NBUF):
                    operands.load(sp, b)
                for b in range(B):
                    maxima(b)
                    if b + 2 in range(NBUF, B):
                        sp.wait_ge(sT_mm, NH * (b + 2 - NBUF + 1))
                        operands.load(sp, b + 2)

            @block.gpsimd
            def _(pool):
                if bias is not None:
                    pool.wait_ge(bias_in, 16)
                for k in range(NT):
                    if bias is None:
                        pool.wait_ge(normed, k + 1)
                    pool.tensor_tensor(x_sb[:, k, :], x_sb[:, k, :],
                                       ctx_sb[:, k, :] if bias is None else bias_sb[:], ALU.add)

            @block.tensor
            def _(pe):
                def scores(n, j):
                    b, p = divmod(n, NP)
                    if p == 0 and j == 0:
                        operands.wait(pe, b)
                    rows = slice(64 * j, 64 * j + KR)
                    h = 2 * n + j
                    if h >= BANKS:
                        pe.wait_ge(sc_max, h - BANKS + 1)
                    for qt in range(TB):
                        last = pe.matmul(sc[h % BANKS][:, qt, :], qs[b % NBUF][rows, p, qt * P:(qt + 1) * P],
                                         ks[b % NBUF][rows, p, :], start=True, stop=True)
                    last.then_inc(sc_mm, 1)

                def maxima_T(b):
                    pe.wait_ge(sc_max, 2 * NP * (b + 1))
                    for qt in range(TB):
                        last = pe.transpose(pf[0:NH, qt * P:(qt + 1) * P], mx[b % 2][:, qt, :], ident[:])
                    last.then_inc(mT_mm, 1)

                def scores_T(t, j):
                    b, p = divmod(t, NP)
                    if p == 0 and j == 0:
                        pe.wait_ge(m_in[b % NBUF], 32 * (b // NBUF + 1))
                    h = 2 * t + j
                    if h >= BANKS:
                        pe.wait_ge(exped, h - BANKS + 1)
                    rows = slice(64 * j, 64 * j + KR + 1)
                    for kt in range(TB):
                        last = pe.matmul(sT[h % BANKS][:, kt * S:(kt + 1) * S],
                                         ks[b % NBUF][rows, p, kt * P:(kt + 1) * P],
                                         qs[b % NBUF][rows, p, :], start=True, stop=True)
                    last.then_inc(sT_mm, 1)

                def values(g):
                    b, gb = divmod(g, NP // 2)
                    pe.wait_ge(exped, 4 * g + 4)
                    if g % 2 == 0 and g >= 2:
                        pe.wait_ge(o_out, g // 2)
                    for kt in range(TB):
                        for c in range(4):
                            last = pe.matmul(po[32 * c:32 * c + VW, g % 2, :], va[:, TB * b + kt, 4 * gb + c, :],
                                             pT[(2 * g + c // 2) % 4][:, c % 2, kt, :],
                                             start=(kt == 0), stop=(kt == TB - 1))
                    last.then_inc(pv_mm, 1)

                def outputs_T(b, qt):
                    pe.wait_ge(o_out, 2 * b + 2)
                    for g in range(4):
                        last = pe.transpose(pf[:, g * P:(g + 1) * P],
                                            oT[b % 2][:, g // 2, (g % 2) * S + qt * P:(g % 2) * S + (qt + 1) * P], ident[:])
                    last.then_inc(oT_mm, 1)

                shared = None
                for what, k in pe_order(SLOTS):
                    if what in ("mT", "oT"):
                        if shared is not None:
                            pe.wait_ge(nm_made if shared[0] == "mT" else normed, shared[1] + 1)
                        shared = what, k
                    if what == "sT":
                        scores_T(k // 2, k % 2)
                    elif what == "sc":
                        scores(k // 2, k % 2)
                    elif what == "mT":
                        maxima_T(k)
                    elif what == "pv":
                        values(k)
                    else:
                        outputs_T(k // TB, k % TB)

            @block.vector
            def _(dve):
                for n in range(SLOTS + LEAD + 6):
                    if n < SLOTS:
                        b, p = divmod(n, NP)
                        for j in range(2):
                            dve.wait_ge(sc_mm, 2 * n + j + 1)
                            if p == 0 and j == 0 and b >= 2:
                                dve.wait_ge(mT_mm, b - 1)
                            dve.tensor_reduce(mx[b % 2][:, :, NP * j + p], sc[(2 * n + j) % BANKS][:], AXX, ALU.max).then_inc(sc_max, 1)
                    if n >= 9 and (n - 9) % NP == 0 and (n - 9) // NP < B:
                        b = (n - 9) // NP
                        dve.wait_ge(mT_mm, b + 1)
                        if b >= 2:
                            dve.wait_ge(m_in[(b - 2) % NBUF], 32 * ((b - 2) // NBUF + 1))
                        dve.tensor_scalar(nm[b % 2][:], pf[0:NH, 0:S], -1.0, None, ALU.mult).then_inc(nm_made, 1)
                    t = n - LEAD
                    for qt in range(TB):
                        if t >= NP + 3 + qt and (t - NP - 3 - qt) % NP == 0 and (t - NP - 3 - qt) // NP < B:
                            k = TB * ((t - NP - 3 - qt) // NP) + qt
                            o = pf[:].rearrange("p (h w) -> p h w", w=VW)
                            dve.wait_ge(oT_mm, k + 1)
                            if k >= 1:
                                dve.wait_ge(normed, k)
                            dve.reciprocal(rs[:, k % 2, :], o[:, :, HD]).then_inc(recip, 1)
                            dve.wait_ge(recip, k + 1)
                            dve.tensor_tensor(ctx_sb[:, k, :].rearrange("p (h d) -> p h d", h=NH), o[:, :, 0:HD],
                                              rs[:, k % 2, :].unsqueeze(2).to_broadcast([P, NH, HD]),
                                              ALU.mult).then_inc(normed, 1)

            @block.scalar
            def _(act):
                for t in range(SLOTS + 2):
                    if t < SLOTS:
                        if t >= 4:
                            act.wait_ge(pv_mm, (t - 4) // 2 + 1)
                        for j in range(2):
                            h = 2 * t + j
                            act.wait_ge(sT_mm, h + 1)
                            act.activation(pT[t % 4][:, j].rearrange("p b s -> p (b s)"), sT[h % BANKS][:], ACT.Exp,
                                           scale=SCORE_SCALE).then_inc(exped, 1)
                    if t >= 5 and (t - 5) % 4 == 0 and (t - 5) // 4 < 2 * B:
                        h = (t - 5) // 4
                        act.wait_ge(pv_mm, 2 * h + 2)
                        if h >= 4 and h % 2 == 0:
                            act.wait_ge(oT_mm, TB * (h // 2 - 1))
                        act.activation(oT[(h // 2) % 2][:, h % 2, :], po[:].rearrange("p g s -> p (g s)"),
                                       ACT.Copy).then_inc(o_out, 1)


def pe_order(slots):
    order = []
    for n in range(slots + LEAD + 6):
        t = n - LEAD
        for j in range(2):
            if 0 <= t < slots:
                order.append(("sT", 2 * t + j))
            if n < slots:
                order.append(("sc", 2 * n + j))
        if n >= 9 and (n - 9) % NP == 0 and (n - 9) // NP < B:
            order.append(("mT", (n - 9) // NP))
        if t >= 3 and (t - 3) % 2 == 0 and (t - 3) // 2 < slots // 2:
            order.append(("pv", (t - 3) // 2))
        for qt in range(TB):
            k = t - NP - 3 - qt
            if k >= 0 and k % NP == 0 and k // NP < B:
                order.append(("oT", TB * (k // NP) + qt))
    return order


def project_out(nc, tag, x_sb, ctx_sb, ident, w):
    with Mem(nc, tag) as m:
        wh, wl = w
        ch = [m.sb(f"ch{u}", [P, FC, S], F32R) for u in range(2)]
        cl = [m.sb(f"cl{u}", [P, FC, S], F32R) for u in range(2)]
        pt = [m.ps(f"pt{u}", [P, FC, S]) for u in range(2)]
        po = [m.ps(f"po{u}", [P, TB, D]) for u in range(2)]
        t_mm, h_ready, l_ready = m.sems("t_mm"), m.sems("h_ready"), m.sems("l_ready")
        o_mm, added = m.sems("o_mm"), m.sems("added")
        with nc.Block() as block:
            @block.tensor
            def _(pe):
                for b in range(B + 1):
                    if b < B:
                        u, i = b % 2, b // 2
                        wait(pe, l_ready[u], i)
                        for t in range(TB):
                            for c in range(FC):
                                last = pe.transpose(pt[u][:, c, t * P:(t + 1) * P],
                                                    ctx_sb[:, TB * b + t, c * P:(c + 1) * P], ident[:])
                        last.then_inc(t_mm[u], 1)
                    if b >= 1:
                        u, i = (b - 1) % 2, (b - 1) // 2
                        pe.wait_ge(l_ready[u], i + 1)
                        wait(pe, added[u], i)
                        for t in range(TB):
                            last = three_products(
                                pe, po[u][:, t, :],
                                (lambda c: ch[u][:, c, t * P:(t + 1) * P], lambda c: cl[u][:, c, t * P:(t + 1) * P]),
                                (lambda c: wh[:, c, :], lambda c: wl[:, c, :]), range(FC), True, True)
                        last.then_inc(o_mm[u], 1)

            @block.scalar
            def _(act):
                for b in range(B):
                    u, i = b % 2, b // 2
                    act.wait_ge(t_mm[u], i + 1)
                    wait(act, o_mm[u], i)
                    act.activation(ch[u][:], pt[u][:], ACT.Copy).then_inc(h_ready[u], 1)

            @block.vector
            def _(dve):
                for b in range(B + 1):
                    if b < B:
                        u, i = b % 2, b // 2
                        dve.wait_ge(h_ready[u], i + 1)
                        dve.tensor_tensor(cl[u][:], pt[u][:], ch[u][:], ALU.subtract).then_inc(l_ready[u], 1)
                    if b >= 1:
                        u, i = (b - 1) % 2, (b - 1) // 2
                        dve.wait_ge(o_mm[u], i + 1)
                        x = x_sb[:, TB * (b - 1):TB * b, :]
                        dve.tensor_tensor(x, po[u][:], x, ALU.add).then_inc(added[u], 1)


NE = 8
PAIR = 2 * P
HI = T // P
KINDS = 5
COLS = 2 * NE * (T // PAIR)
PAD_COLS = COLS + HI
AK = 6
I0, I1, A1 = 256, 672, 50


class Tables:

    def __init__(self, m):
        self.gather = m.sb("gather_rows", [P, PAD_COLS], I32)
        self.scatter = m.sb("scatter_rows", [P, PAD_COLS], I32)
        self.weight = m.sb("slot_weight", [P, PAD_COLS])
        self.pairs = m.sb("pairs", [P, 3, NE], I32)


def route(nc, tag, x_sb, ident, tables, weights, rows, acc, router, actor=None):
    A = actor["w1n"] if actor else 0
    R = NE + A
    with Mem(nc, tag) as m:
        norm = Norm(m)
        xn = m.sb("xn", [P, NT, D])
        xt = [m.sb(f"xt{u}", [P, FC, P]) for u in range(2)]
        rw = m.sb("rw", [P, FC, R])
        lg = m.sb("lg", [P, NT, R])
        ahead = m.sb("ahead", [P, NT, NE, NE])
        V = m.sb("value", [P, NT, NE])
        W = m.sb("w", [P, NT, NE])
        M = m.sb("mask", [P, NT, NE])
        rank = m.sb("rank", [P, NT, NE])
        top = m.sb("top", [P, NT])
        tot = m.sb("tot", [P, NT])
        cum = [m.sb(f"cum{n}", [P, NT, NE]) for n in range(2)]
        slot = m.sb("slot", [P, NT, NE])
        sloti = m.sb("sloti", [P, NT, NE], I32)
        parti = m.sb("parti", [P, 2, NT, NE], I32)
        part = m.sb("part", [P, 2, NT, NE])
        cnt = m.sb("cnt", [P, NE])
        before = m.sb("before", [P, NE, NE])
        tril = m.sb("tril", [P, P])
        allone = m.sb("allone", [P, P])
        lanes = m.sb("lanes", [P, P])
        lane1 = m.sb("lane1", [P, 1])
        spare = m.sb("spare", [P, 1])
        hot_lo = [m.sb(f"hot_lo{u}", [P, NE, P], BF16) for u in range(3)]
        hot_hi = m.sb("hot_hi", [P, NT, NE, HI], BF16)
        rest = [m.sb(f"rest{n}", [P, NT, NE]) for n in range(2)]
        piece = [m.sb(f"piece{n}", [P, NT, NE], BF16) for n in range(3)]
        kind = m.sb("kind", [P, NT, NE, KINDS, HI], BF16)
        packed = m.sb("packed", [P, KINDS, PAD_COLS])
        found = m.sb("found", [P, PAD_COLS])
        rowf = m.sb("rowf", [P, PAD_COLS])
        pt = [m.ps(f"pt{u}", [P, 512]) for u in range(2)]
        pl = [m.ps(f"pl{u}", [P, 512]) for u in range(2)]
        pcount = m.ps("pcount", [P, 2, NT, NE])
        ptab = m.ps("ptab", [P, NE, P])
        if actor:
            b1 = m.sb("b1", [P, A])
            b2 = m.sb("b2", [P, AK])
            w2 = m.sb("w2", [A, AK])
            ah = m.sb("ah", [P, NT, A])
            ag = m.sb("ag", [P, NT, A])
            at = m.sb("at", [A, NT, P])
            al = m.sb("al", [P, NT, AK])
            number = m.sb("number", [P, AK])
            pa = [x[:].rearrange("p (t c) -> p t c", t=4) for x in pt]

        zeros = m.sb("zeros", [P, 1, D])
        zeroed = m.sem("zeroed")
        w_in = m.sem("w_in")
        consts, lanes_made = m.sem("consts"), m.sem("lanes_made")
        xn_made, rows_out, acc_out = m.sem("xn_made"), m.sem("rows_out"), m.sem("acc_out")
        t_mm, xt_out, l_mm, lg_out = m.sems("t_mm"), m.sems("xt_out"), m.sems("l_mm"), m.sems("lg_out")
        a_in, a_act, a_mm, a_out, a2_mm = (m.sem(n) for n in ("a_in", "a_act", "a_mm", "a_out", "a2_mm"))
        step, to_exp, from_exp = m.sem("step"), m.sem("to_exp"), m.sem("from_exp")
        masked, counted = m.sem("masked"), m.sem("counted")
        parts_ready, paired, lo_made, tab_mm = m.sem("parts_ready"), m.sem("paired"), m.sem("lo_made"), m.sem("tab_mm")
        number_made, weight_made = m.sem("number_made"), m.sem("weight_made")
        packed_zero, ahead_zero, packing = m.sem("packed_zero"), m.sem("ahead_zero"), m.sem("packing")


        def bc(ap, shape):
            return ap.to_broadcast(shape)

        with nc.Block() as block:
            @block.sync
            def _(sp):
                sp.dma_start(rw[:], router.rearrange("(c p) n -> p c n", p=P)).then_inc(w_in, 16)
                n_in = 16
                if actor:
                    sp.dma_start(b1[:], actor["b1"].partition_broadcast(P)).then_inc(w_in, 16)
                    sp.dma_start(b2[:], actor["b2"].partition_broadcast(P)).then_inc(w_in, 16)
                    sp.dma_start(w2[:], actor["w2"]).then_inc(w_in, 16)
                    n_in = 64
                weights.load(sp, 0)
                sp.dma_start(acc[0][0:T, :].rearrange("(n p) d -> p n d", p=P), x_sb[:]).then_inc(acc_out, 16)
                sp.dma_start(acc[0][T:T + P, :], x_sb[:, 0, :]).then_inc(acc_out, 16)
                if len(acc) > 1:
                    sp.wait_ge(zeroed, 1)
                    sp.dma_start(acc[1].rearrange("(n p) d -> p n d", p=P),
                                 bc(zeros[:], [P, NT + 1, D])).then_inc(acc_out, 16)
                sp.wait_ge(xn_made, NT)
                sp.dma_start(rows.rearrange("(n p) d -> p n d", p=P), xn[:]).then_inc(rows_out, 16)
                weights.load(sp, 1)
                sp.wait_ge(acc_out, 16 * (1 + len(acc)))
                sp.wait_ge(rows_out, 16)
                sp.wait_ge(w_in, n_in)

            @block.gpsimd
            def _(pool):
                pool.memset(zeros[:], 0.0).then_inc(zeroed, 1)
                pool.memset(tril[:], 0.0).then_inc(consts, 1)
                pool.memset(allone[:], 1.0).then_inc(consts, 1)
                pool.memset(before[:], 0.0).then_inc(consts, 1)
                pool.iota(lanes[:], [[1, P]], base=0, channel_multiplier=0, allow_small_or_imprecise_dtypes=True).then_inc(consts, 1)
                pool.iota(lane1[:], [[0, 1]], base=1, channel_multiplier=1, allow_small_or_imprecise_dtypes=True).then_inc(consts, 1)
                pool.memset(packed[:], 0.0).then_inc(packed_zero, 1)
                pool.memset(ahead[:], 0.0).then_inc(ahead_zero, 1)
                pool.iota(spare[:], [[0, 1]], base=T + 1, channel_multiplier=1, allow_small_or_imprecise_dtypes=True).then_inc(consts, 1)
                if actor:
                    pool.iota(number[:], [[1, AK]], base=-AK, channel_multiplier=0, allow_small_or_imprecise_dtypes=True).then_inc(lanes_made, 1)
                pool.wait_ge(consts, 6)
                pool.affine_select(out=tril[:], in_=tril[:], compare_op=ALU.is_ge, fill=1.0, base=0,
                                   pattern=[[-1, P]], channel_multiplier=1).then_inc(consts, 1)
                pool.affine_select(out=before[:], in_=before[:], compare_op=ALU.is_ge, fill=1.0, base=0,
                                   pattern=[[-1, NE], [1, NE]], channel_multiplier=0).then_inc(consts, 1)
                pool.wait_ge(parts_ready, 2)
                for t in range(0, NT, 2):
                    for n in range(3):
                        pool.tensor_tensor(kind[:, t:t + 2, :, 2 + n, :], hot_hi[:, t:t + 2],
                                           bc(piece[n][:, t:t + 2].unsqueeze(3), [P, 2, NE, HI]), ALU.mult).then_inc(weight_made, 1)

            @block.scalar
            def _(act):
                norm.root(act, 0)
                for t in range(NT + 1):
                    if t < NT:
                        u, i = t % 2, t // 2
                        act.wait_ge(t_mm[u], i + 1)
                        wait(act, l_mm[u], i)
                        act.activation(xt[u][:].rearrange("p c t -> p (c t)"), pt[u][:, 0:FC * P], ACT.Copy).then_inc(xt_out[u], 1)
                    if t % 3 == 1 and (t + 2) // 3 < GROUPS:
                        norm.root(act, (t + 2) // 3)
                    if t >= NT // 2 and t - NT // 2 < weights.NC:
                        weights.high(act, 0, t - NT // 2)
                    if t >= 1:
                        u, i = (t - 1) % 2, (t - 1) // 2
                        act.wait_ge(l_mm[u], i + 1)
                        act.activation(lg[:, t - 1, :], pl[u][:, 0:R], ACT.Copy).then_inc(lg_out[u], 1)
                act.wait_ge(to_exp, 1)
                act.activation(V[:], V[:], ACT.Exp).then_inc(from_exp, 1)
                if actor:
                    act.wait_ge(a_in, 1)
                    act.activation(ag[:], ah[:], ACT.Gelu_apprx_tanh).then_inc(a_act, 1)
                    for g in range(4):
                        act.wait_ge(a_mm, g + 1)
                        act.activation(at[:, 4 * g:4 * g + 4, :], pa[g % 2][0:A], ACT.Copy).then_inc(a_out, 1)
                act.wait_ge(consts, 8)
                act.wait_ge(parts_ready, 2)
                for t in range(NT):
                    act.activation(kind[:, t, :, 0, :], hot_hi[:, t], ACT.Copy, scale=lane1[:, 0:1]).then_inc(number_made, 1)
                    act.activation(kind[:, t, :, 1, :], hot_hi[:, t], ACT.Copy, scale=float(P * t)).then_inc(number_made, 1)
                act.wait_ge(paired, 1)
                firsts = [act.value_load(tables.pairs[0:1, 1, e:e + 1], min_val=0, max_val=(T // PAIR) * NE - 8)
                          for e in range(NE)]
                act.wait_ge(packed_zero, 1)
                act.wait_ge(tab_mm, NT)
                for e, first in enumerate(firsts):
                    if e >= 1:
                        act.wait_ge(packing, e)
                    act.activation(packed[:, :, bass.ds(2 * first, HI)],
                                   ptab[:, e, 0:KINDS * HI].rearrange("p (k h) -> p k h", k=KINDS), ACT.Copy).then_inc(packing, 1)

            @block.tensor
            def _(pe):
                pe.wait_ge(w_in, 64 if actor else 16)

                for t in range(NT + 1):
                    if t < NT:
                        u, i = t % 2, t // 2
                        pe.wait_ge(xn_made, t + 1)
                        wait(pe, xt_out[u], i)
                        for c in range(FC):
                            last = pe.transpose(pt[u][:, c * P:(c + 1) * P], xn[:, t, c * P:(c + 1) * P], ident[:])
                        last.then_inc(t_mm[u], 1)
                    if t >= 1:
                        u, i = (t - 1) % 2, (t - 1) // 2
                        pe.wait_ge(xt_out[u], i + 1)
                        wait(pe, lg_out[u], i)
                        for c in range(FC):
                            last = pe.matmul(pl[u][:, 0:R], xt[u][:, c, :], rw[:, c, :], start=(c == 0), stop=(c == FC - 1))
                        last.then_inc(l_mm[u], 1)
                if actor:
                    pe.wait_ge(a_act, 1)
                    for g in range(5):
                        if g < 4:
                            if g >= 2:
                                pe.wait_ge(a_out, g - 1)
                            for t in range(4):
                                last = pe.transpose(pa[g % 2][0:A, t, :], ag[:, 4 * g + t, :], ident[:])
                            last.then_inc(a_mm, 1)
                        if g >= 1:
                            pe.wait_ge(a_out, g)
                            for t in range(4 * g - 4, 4 * g):
                                last = pe.matmul(pl[0][:, AK * t:AK * t + AK], at[:, t, :], w2[:], start=True, stop=True)
                    last.then_inc(a2_mm, 1)
                pe.wait_ge(masked, 1)
                pe.wait_ge(consts, 8)
                pe.matmul(pcount[:, 0, :, :], tril[:], M[:], start=True, stop=True)
                pe.matmul(pcount[:, 1, :, :], allone[:], M[:], start=True, stop=True).then_inc(counted, 1)
                for t in range(NT):
                    pe.wait_ge(lo_made, t + 1)
                    pe.wait_ge(number_made, 2 * t + 2)
                    if t % 2 == 0:
                        pe.wait_ge(weight_made, 3 * (t // 2 + 1))
                    for e in range(NE):
                        last = pe.matmul(ptab[:, e, 0:KINDS * HI], hot_lo[t % 3][:, e, :],
                                         kind[:, t, e].rearrange("p k h -> p (k h)"), start=(t == 0 and e % 4 == 0),
                                         stop=(t == NT - 1 and e % 4 == 3), skip_group_check=True)
                    last.then_inc(tab_mm, 1)

            @block.vector
            def _(dve):
                chain = Chain(dve, step)

                def do(ins):
                    chain.step(ins)
                    chain.wait()

                def pairs_by_expert():
                    do(dve.tensor_scalar(cnt[:], cnt[:], PAIR - 1.0, float(PAIR), ALU.add, ALU.max))
                    do(dve.tensor_copy(tables.pairs[:, 0, :], cnt[:]))
                    do(dve.tensor_scalar(tables.pairs[:, 0, :], tables.pairs[:, 0, :], 8, None, ALU.arith_shift_right))
                    do(dve.tensor_copy(cnt[:], tables.pairs[:, 0, :]))
                    do(dve.tensor_tensor(ahead[:, 0], bc(cnt[:].unsqueeze(1), [P, NE, NE]), before[:], ALU.mult))
                    do(dve.tensor_reduce(rank[:, 0, :], ahead[:, 0], AXX, ALU.add))
                    dve.tensor_copy(tables.pairs[:, 1, :], rank[:, 0, :]).then_inc(paired, 1)
                    do(dve.tensor_tensor(rank[:, 0, :], rank[:, 0, :], cnt[:], ALU.add))
                    do(dve.tensor_scalar(tables.pairs[:, 2, :], rank[:, 0, :], -1.0, None, ALU.add))


                for g in range(GROUPS):
                    norm.statistics(dve, x_sb, g)
                    for t in range(NT)[g * NT // GROUPS:(g + 1) * NT // GROUPS]:
                        dve.tensor_scalar(xn[:, t, :], x_sb[:, t, :], norm.mv[:, t, 0:1], norm.rstd[:, t:t + 1],
                                          ALU.subtract, ALU.mult).then_inc(xn_made, 1)
                for c in range(weights.NC):
                    weights.low(dve, 0, c)
                dve.wait_ge(lg_out[0], NT // 2)
                dve.wait_ge(lg_out[1], NT // 2)
                do(dve.tensor_reduce(top[:], lg[:, :, 0:NE], AXX, ALU.max))
                dve.tensor_tensor(V[:], lg[:, :, 0:NE], bc(top[:].unsqueeze(2), [P, NT, NE]), ALU.subtract).then_inc(to_exp, 1)
                if actor:
                    dve.wait_ge(w_in, 64)
                    dve.tensor_tensor(ah[:], lg[:, :, NE:R], bc(b1[:].unsqueeze(1), [P, NT, A]), ALU.add).then_inc(a_in, 1)
                dve.wait_ge(from_exp, 1)
                if actor:
                    do(dve.tensor_reduce(tot[:], V[:], AXX, ALU.add))
                    do(dve.reciprocal(top[:], tot[:]))
                    do(dve.tensor_tensor(V[:], V[:], bc(top[:].unsqueeze(2), [P, NT, NE]), ALU.mult))
                    by = V[:]
                else:
                    by = lg[:, :, 0:NE]
                dve.wait_ge(consts, 8)
                dve.wait_ge(ahead_zero, 1)
                for e in range(NE):
                    for rest_of, op in (((0, e), ALU.is_ge), ((e + 1, NE), ALU.is_gt)):
                        a, b = rest_of
                        if b > a:
                            chain.step(dve.tensor_tensor(ahead[:, :, e, a:b], by[:, :, a:b],
                                                         bc(by[:, :, e:e + 1], [P, NT, b - a]), op))
                chain.wait()
                do(dve.tensor_reduce(rank[:], ahead[:], AXX, ALU.add))
                if actor:
                    dve.wait_ge(a2_mm, 1)
                    do(dve.tensor_tensor(al[:], pl[0][:, 0:NT * AK].rearrange("p (t k) -> p t k", k=AK),
                                         bc(b2[:].unsqueeze(1), [P, NT, AK]), ALU.add))
                    do(dve.tensor_scalar(al[:], al[:], -30.0, 30.0, ALU.max, ALU.min))
                    do(dve.tensor_reduce(tot[:], al[:], AXX, ALU.max))
                    do(dve.tensor_tensor(al[:], al[:], bc(tot[:].unsqueeze(2), [P, NT, AK]), ALU.is_equal))
                    dve.wait_ge(lanes_made, 1)
                    do(dve.tensor_tensor(al[:], al[:], bc(number[:].unsqueeze(1), [P, NT, AK]), ALU.mult))
                    do(dve.tensor_reduce(tot[:], al[:], AXX, ALU.min))
                    do(dve.tensor_scalar(tot[:], tot[:], AK + 1.0, None, ALU.add))
                    dve.tensor_tensor(M[:], rank[:], bc(tot[:].unsqueeze(2), [P, NT, NE]), ALU.is_lt).then_inc(masked, 1)
                    dve.wait_ge(masked, 1)
                    do(dve.tensor_tensor(W[:], V[:], M[:], ALU.mult))
                else:
                    dve.tensor_scalar(M[:], rank[:], 2.0, None, ALU.is_lt).then_inc(masked, 1)
                    dve.wait_ge(masked, 1)
                    do(dve.tensor_tensor(W[:], V[:], M[:], ALU.mult))
                    do(dve.tensor_reduce(tot[:], W[:], AXX, ALU.add))
                    do(dve.reciprocal(top[:], tot[:]))
                    do(dve.tensor_tensor(W[:], W[:], bc(top[:].unsqueeze(2), [P, NT, NE]), ALU.mult))
                do(dve.tensor_copy(piece[0][:], W[:]))
                do(dve.tensor_tensor(rest[0][:], W[:], piece[0][:], ALU.subtract))
                do(dve.tensor_copy(piece[1][:], rest[0][:]))
                do(dve.tensor_tensor(piece[2][:], rest[0][:], piece[1][:], ALU.subtract))
                dve.wait_ge(counted, 1)
                do(dve.tensor_copy(cum[0][:], pcount[:, 1, :, :]))
                src = 0
                for d in (1, 2, 4, 8):
                    a, b = cum[src], cum[1 - src]
                    do(dve.tensor_copy(b[:, 0:d, :], a[:, 0:d, :]))
                    do(dve.tensor_tensor(b[:, d:NT, :], a[:, d:NT, :], a[:, 0:NT - d, :], ALU.add))
                    src = 1 - src
                incl = cum[src]
                do(dve.tensor_copy(cnt[:], incl[:, NT - 1, :]))
                do(dve.tensor_copy(slot[:, 0:1, :], pcount[:, 0, 0:1, :]))
                do(dve.tensor_tensor(slot[:, 1:NT, :], pcount[:, 0, 1:NT, :], incl[:, 0:NT - 1, :], ALU.add))
                do(dve.tensor_scalar(slot[:], slot[:], 1.0, None, ALU.add))
                do(dve.tensor_tensor(slot[:], slot[:], M[:], ALU.mult))
                do(dve.tensor_scalar(slot[:], slot[:], -1.0, None, ALU.add))
                do(dve.tensor_copy(sloti[:], slot[:]))
                do(dve.tensor_scalar(parti[:, 0], sloti[:], P - 1, None, ALU.bitwise_and))
                do(dve.tensor_scalar(parti[:, 1], sloti[:], 7, None, ALU.arith_shift_right))
                dve.tensor_copy(part[:], parti[:]).then_inc(parts_ready, 1)
                dve.wait_ge(parts_ready, 1)
                dve.tensor_tensor(hot_hi[:].rearrange("p t e h -> p (t e) h"),
                                  bc(lanes[:, 0:HI].unsqueeze(1), [P, NT * NE, HI]),
                                  bc(part[:, 1].rearrange("p t e -> p (t e)").unsqueeze(2), [P, NT * NE, HI]),
                                  ALU.is_equal).then_inc(parts_ready, 1)
                for t in range(NT):
                    if t >= 3:
                        dve.wait_ge(tab_mm, t - 2)
                    dve.tensor_tensor(hot_lo[t % 3][:], bc(lanes[:].unsqueeze(1), [P, NE, P]),
                                      bc(part[:, 0, t, :].unsqueeze(2), [P, NE, P]), ALU.is_equal).then_inc(lo_made, 1)
                    if t == 2:
                        pairs_by_expert()
                dve.wait_ge(packing, NE)
                do(dve.tensor_tensor(found[:], packed[:, 0, :], packed[:, 1, :], ALU.add))
                do(dve.tensor_scalar(tables.gather[:], found[:], -1.0, 0.0, ALU.add, ALU.max))
                do(dve.tensor_scalar(rowf[:], found[:], 0.0, spare[:, 0:1], ALU.is_equal, ALU.mult))
                do(dve.tensor_tensor(rowf[:], rowf[:], found[:], ALU.add))
                do(dve.tensor_scalar(tables.scatter[:], rowf[:], -1.0, None, ALU.add))
                do(dve.tensor_tensor(rowf[:], packed[:, 3, :], packed[:, 4, :], ALU.add))
                do(dve.tensor_tensor(tables.weight[:], rowf[:], packed[:, 2, :], ALU.add))


class Weights:

    def __init__(self, m, gu, dn, inner, cw):
        self.gu, self.dn, self.inner, self.cw, self.NC = gu, dn, inner, cw, inner // cw
        self.graw = m.sb("graw", [P, FC, 2 * inner])
        self.draw = m.sb("draw", [cw, self.NC, D])
        self.gh, self.gl = ([m.sb(f"g{x}{n}", [P, FC, 2 * inner], F32R) for n in range(2)] for x in "hl")
        self.dh, self.dl = ([m.sb(f"d{x}{n}", [cw, self.NC, D], F32R) for n in range(2)] for x in "hl")
        self.raw_in, self.hi_made, self.lo_made = m.sem("raw_in"), m.sem("hi_made"), m.sem("lo_made")

    def load(self, sp, e):
        if e >= 1:
            sp.wait_ge(self.lo_made, 2 * self.NC * e)
        sp.dma_start(self.graw[:], self.gu[e].rearrange("(c p) n -> p c n", p=P)).then_inc(self.raw_in, 16)
        sp.dma_start(self.draw[:], self.dn[e].rearrange("(c p) n -> p c n", p=self.cw)).then_inc(self.raw_in, 16)

    def slices(self, e, c):
        g = slice(2 * self.cw * c, 2 * self.cw * (c + 1))
        return ((self.graw[:, :, g], self.gh[e % 2][:, :, g], self.gl[e % 2][:, :, g]),
                (self.draw[:, c, :], self.dh[e % 2][:, c, :], self.dl[e % 2][:, c, :]))

    def high(self, act, e, c):
        act.wait_ge(self.raw_in, 32 * (e + 1))
        for raw, hi, lo in self.slices(e, c):
            act.activation(hi, raw, ACT.Copy).then_inc(self.hi_made, 1)

    def low(self, dve, e, c):
        dve.wait_ge(self.hi_made, 2 * (self.NC * e + c + 1))
        for raw, hi, lo in self.slices(e, c):
            dve.tensor_tensor(lo, raw, hi, ALU.subtract).then_inc(self.lo_made, 1)


def experts(nc, tag, ident, tables, rows, acc, weights):
    NC, cw, inner = weights.NC, weights.cw, weights.inner
    gh, gl, dh, dl = weights.gh, weights.gl, weights.dh, weights.dl
    with Mem(nc, tag) as m:
        gidx = m.sb("gidx", [P, 2], I32)
        sidx = m.sb("sidx", [P, 2], I32)

        xg = m.sb("xg", [P, 2, D])
        xh = m.sb("xh", [P, FC, PAIR], F32R)
        xl = m.sb("xl", [P, FC, PAIR], F32R)
        sg = [m.sb(f"sg{n}", [cw, PAIR]) for n in range(2)]
        hf = [m.sb(f"hf{n}", [cw, PAIR]) for n in range(2)]
        hh = m.sb("hh", [cw, NC, PAIR], F32R)
        hl = m.sb("hl", [cw, NC, PAIR], F32R)
        ys = m.sb("ys", [P, 2, D])
        px = m.ps("px", [P, FC, PAIR])
        NG = min(NC, 3)
        lagged = NC <= NG
        pg = [m.ps(f"pg{n}", [P, 2, PAIR]) for n in range(NG)]
        py = m.ps("py", [P, 2, D])

        index_made, gathered, scattered = m.sem("index_made"), m.sem("gathered"), m.sems("scattered")
        settled = m.sem("settled")
        x_mm, xh_made, xl_made = m.sem("x_mm"), m.sem("xh_made"), m.sem("xl_made")
        g_mm, silued, timed, hh_made, hl_made = (m.sem(n) for n in ("g_mm", "silued", "timed", "hh_made", "hl_made"))
        y_mm, y_out = m.sem("y_mm"), m.sem("y_out")

        def each(eng, body, between=None, opening=None):
            for e in range(NE):
                n = eng.value_load(tables.pairs[0:1, 0, e:e + 1], min_val=1, max_val=T // PAIR)
                first = eng.value_load(tables.pairs[0:1, 1, e:e + 1], min_val=e, max_val=e * (T // PAIR))
                if between:
                    between(e)
                if opening:
                    opening(e, first if e >= 1 else 0)
                    first, n = first + 1, n - 1
                with eng.Fori(0, n) as i:
                    body(e, first + i)

        def last_pair(eng, e):
            return eng.value_load(tables.pairs[0:1, 2, e:e + 1], min_val=e, max_val=COLS // 2)

        with nc.Block() as block:
            @block.sync
            def _(sp):
                for e in range(2, NE):
                    weights.load(sp, e)
                sp.wait_ge(weights.raw_in, 32 * NE)

            @block.gpsimd
            def _(pool):
                def settle(sem, value):
                    pool.wait_ge(sem, value)
                    pool.sem_inc(settled, 1)

                def gather(q, k):
                    pool.tensor_copy(gidx[:], tables.gather[:, bass.ds(2 * q, 2)]).then_inc(index_made, 1)
                    settle(index_made, k)
                    for t in range(2):
                        pool.indirect_dma_start(out=xg[:, t, :], out_offset=None, in_=rows,
                                                in_offset=bass.IndirectOffsetOnAxis(ap=gidx[:, t:t + 1], axis=0)
                                                ).then_inc(gathered, 16)

                def scatter(q, k):
                    settle(y_out, 2 * q + 2)
                    for t in range(2):
                        settle(scattered[t], 16 * q + 16)
                    pool.tensor_copy(sidx[:], tables.scatter[:, bass.ds(2 * q, 2)]).then_inc(index_made, 1)
                    settle(index_made, k)
                    for t in range(2):
                        if t == 1 and len(acc) == 1:
                            settle(scattered[0], 16 * q + 32)
                        pool.indirect_dma_start(out=acc[t % len(acc)], out_offset=bass.IndirectOffsetOnAxis(ap=sidx[:, t:t + 1], axis=0),
                                                in_=ys[:, t, :], in_offset=None, compute_op=ALU.add
                                                ).then_inc(scattered[t], 16)

                def pair(e, q):
                    settle(x_mm, q + 2)
                    if not lagged:
                        gather(q + 2, 2 * q + 3)
                        scatter(q, 2 * q + 4)
                    elif isinstance(q, int):
                        gather(2, 3)
                    else:
                        gather(q + 2, 2 * q + 2)
                        scatter(q - 1, 2 * q + 3)

                gather(0, 1)
                for t in range(2):
                    pool.dma_start(sidx[:, t:t + 1], tables.scatter[:, t:t + 1]).then_inc(scattered[t], 16)
                settle(x_mm, 1)
                gather(1, 2)
                each(pool, pair, opening=pair if lagged else None)
                end = last_pair(pool, NE - 1)
                if lagged:
                    scatter(end, 2 * end + 4)
                for t in range(2):
                    settle(scattered[t], 16 * end + 32)
                settle(gathered, 32 * end + 96)

            @block.tensor
            def _(pe):
                def transposes(q):
                    pe.wait_ge(gathered, 32 * q + 32)
                    for t in range(2):
                        for c in range(FC):
                            last = pe.transpose(px[:, c, t * P:(t + 1) * P], xg[:, t, c * P:(c + 1) * P], ident[:])
                    last.then_inc(x_mm, 1)

                def gate_up(e, q, before=None):
                    n = e % 2
                    pe.wait_ge(xl_made, q + 1)
                    for c in range(NC):
                        if c >= NG:
                            pe.wait_ge(timed, NC * q + c - NG + 1)
                        elif before is not None:
                            pe.wait_ge(timed, NC * before + c + 1)
                        for s in range(2):
                            cols = slice(s * inner + c * cw, s * inner + (c + 1) * cw)
                            last = three_products(pe, pg[c % NG][0:cw, s, :],
                                                  (lambda f: gh[n][:, f, cols], lambda f: gl[n][:, f, cols]),
                                                  (lambda f: xh[:, f, :], lambda f: xl[:, f, :]), range(FC), True, True)
                        last.then_inc(g_mm, 1)

                def down(e, q):
                    n = e % 2
                    for c in range(NC):
                        pe.wait_ge(hl_made, NC * q + c + 1)
                        for t in range(2):
                            cols = slice(t * P, (t + 1) * P)
                            for k, (a, b) in enumerate(((hh, dh[n]), (hl, dh[n]), (hh, dl[n]))):
                                last = pe.matmul(py[:, t, :], a[:, c, cols], b[:, c, :], start=(c == 0 and t == 0 and k == 0),
                                                 stop=(c == NC - 1 and k == 2), skip_group_check=True)
                    last.then_inc(y_mm, 1)

                def pair(e, q):
                    gate_up(e, q, q - 1 if lagged else None)
                    transposes(q + 1)
                    if lagged:
                        down(e, q - 1)
                    else:
                        down(e, q)

                def opening(e, q):
                    before = last_pair(pe, e - 1) if e >= 1 else None
                    gate_up(e, q, before)
                    transposes(q + 1)
                    if e >= 1:
                        down(e - 1, before)

                def between(e):
                    pe.wait_ge(weights.lo_made, 2 * NC * (e + 1))

                transposes(0)
                each(pe, pair, between, opening if lagged else None)
                if lagged:
                    down(NE - 1, last_pair(pe, NE - 1))

            @block.scalar
            def _(act):
                def xhigh(q):
                    act.wait_ge(x_mm, q + 1)
                    act.activation(xh[:], px[:], ACT.Copy).then_inc(xh_made, 1)

                def silu(q, c):
                    act.wait_ge(g_mm, NC * q + c + 1)
                    act.activation(sg[c % 2][:], pg[c % NG][0:cw, 0, :], ACT.Silu).then_inc(silued, 1)

                def high(q, c):
                    act.wait_ge(timed, NC * q + c + 1)
                    act.activation(hh[:, c, :], hf[c % 2][:], ACT.Copy).then_inc(hh_made, 1)

                def opening(e, q):
                    if not lagged and e >= 1:
                        act.wait_ge(y_mm, q)
                    pair(e, q, split=e + 1 < NE)

                def pair(e, q, split=False):
                    if lagged:
                        for c in range(NC):
                            silu(q, c)
                        xhigh(q + 1)
                        wait(act, y_mm, q)
                        for c in range(NC):
                            high(q, c)
                        for c in range(NC if split else 0):
                            weights.high(act, e + 1, c)
                        return
                    for c in range(NC):
                        silu(q, c)
                        if split:
                            weights.high(act, e + 1, c)
                        high(q, c)
                    xhigh(q + 1)

                xhigh(0)
                each(act, pair, opening=opening)

            @block.vector
            def _(dve):
                def xlow(q):
                    dve.wait_ge(xh_made, q + 1)
                    dve.tensor_tensor(xl[:], px[:], xh[:], ALU.subtract).then_inc(xl_made, 1)

                def times(q, c):
                    dve.wait_ge(silued, NC * q + c + 1)
                    dve.tensor_tensor(hf[c % 2][:], pg[c % NG][0:cw, 1, :], sg[c % 2][:], ALU.mult).then_inc(timed, 1)

                def low(q, c):
                    dve.wait_ge(hh_made, NC * q + c + 1)
                    dve.tensor_tensor(hl[:, c, :], hf[c % 2][:], hh[:, c, :], ALU.subtract).then_inc(hl_made, 1)

                def weigh(q):
                    dve.wait_ge(y_mm, q + 1)
                    for t in range(2):
                        dve.wait_ge(scattered[t], 16 * q + 16)
                        dve.tensor_scalar(ys[:, t, :], py[:, t, :], tables.weight[:, bass.ds(2 * q + t, 1)], None,
                                          ALU.mult).then_inc(y_out, 1)

                def opening(e, q):
                    pair(e, q, split=e + 1 < NE)

                def pair(e, q, split=False):
                    if lagged:
                        if not isinstance(q, int):
                            dve.wait_ge(hl_made, NC * q)
                        for c in range(NC):
                            times(q, c)
                        xlow(q + 1)
                        if not isinstance(q, int):
                            weigh(q - 1)
                        for c in range(NC):
                            low(q, c)
                        for c in range(NC if split else 0):
                            weights.low(dve, e + 1, c)
                        return
                    for c in range(NC):
                        times(q, c)
                        if split:
                            weights.low(dve, e + 1, c)
                        low(q, c)
                    xlow(q + 1)
                    weigh(q)

                xlow(0)
                each(dve, pair, opening=opening)
                if lagged:
                    weigh(last_pair(dve, NE - 1))


def moe(nc, tag, x_sb, ident, rows, acc, router, actor, gu, dn, inner, cw):
    with Mem(nc, tag) as m:
        tables = Tables(m)
        weights = Weights(m, gu, dn, inner, cw)
        route(nc, tag + "route", x_sb, ident, tables, weights, rows, acc, router, actor)
        experts(nc, tag + "experts", ident, tables, rows, acc, weights)


def attention(nc, tag, x_sb, c_sb, va, ident, scratch, weights, bqk, bv, bo=None, first=None, acc=None):
    with Mem(nc, tag) as m:
        ctx_sb = m.sb("ctx", [P, NT, D])
        hi = [m.sb(f"w{n}h", [P, FC, D], F32R) for n in range(len(weights))]
        lo = [m.sb(f"w{n}l", [P, FC, D], F32R) for n in range(len(weights))]
        with Mem(nc, tag + "heads") as h:
            operands = Operands(h, scratch)
            project(nc, tag + "project", x_sb, c_sb, ctx_sb, va, ident, hi, lo, weights, bqk, bv, operands, first, acc)
            attend(nc, tag + "attend", x_sb, ctx_sb, va, ident, operands, bo)
        if bo is not None:
            project_out(nc, tag + "out", x_sb, ctx_sb, ident, (hi[3], lo[3]))


def build(nc, a, out):
    Mem.held = []
    scratch = [nc.dram_tensor(n, (B, 2, P, S), F32, kind="Internal").ap() for n in ("qh", "ql", "kh", "kl")]
    rows = [nc.dram_tensor(f"rows{n}", (T, D), F32, kind="Internal").ap() for n in range(2)]
    acc = [[nc.dram_tensor(f"acc{t}", (T + P, D), F32, kind="Internal").ap() for t in range(2)], [out]]
    with Mem(nc, "all") as m:
        ident = m.sb("ident", [P, P])
        x_sb = m.sb("x", [P, NT, D])
        with Mem(nc, "attn") as t:
            c_sb = t.sb("c", [P, FC, T])
            va = t.sb("va", [P, NT, NH, VW])
            attention(nc, "a0", x_sb, c_sb, va, ident, scratch, [a[w + "0"] for w in ("wk", "wv", "wq", "wo")],
                      a["bqk0"], a["bv0"], a["bo0"], first=(a["x"], a["ctx_t"]))
            moe(nc, "m0", x_sb, ident, rows[0], acc[0], a["router0"], None, a["gu0"], a["dn0"], I0, P)
            Mem.release(nc)
            attention(nc, "a1", x_sb, c_sb, va, ident, scratch, [a[w + "1"] for w in ("wk", "wv", "wq")],
                      a["bqk1"], a["bv1"], acc=acc[0])
        moe(nc, "m1", x_sb, ident, rows[1], acc[1], a["router1"],
            {"w1n": A1, "b1": a["ab1"], "b2": a["ab2"], "w2": a["aw2"]}, a["gu1"], a["dn1"], I1, 112)


def layouts(v):
    import numpy as np

    def by_half(w):
        return w.reshape(-1, NP, 2, HD).transpose(0, 2, 3, 1).reshape(-1, D)

    a = {"x": v["x"].reshape(T, D), "ctx_t": v["ctx_1024"].reshape(T, D).T}
    for n, l in enumerate(("L0_xattn_", "L1_xattn_")):
        a[f"wq{n}"], a[f"wk{n}"], a[f"wv{n}"] = by_half(v[l + "Wq"]), by_half(v[l + "Wk"]), v[l + "Wv"]
        a[f"bqk{n}"] = np.concatenate([by_half(v[l + x][None])[0].reshape(2, P) for x in ("bq", "bk")]).T
        a[f"bv{n}"] = v[l + "bv"]
    a["wo0"], a["bo0"] = v["L0_xattn_Wo"], v["L0_xattn_bo"]
    a["router0"] = v["L0_ffn_router_weight"].T
    a["gu0"], a["dn0"] = v["L0_ffn_w1"].transpose(0, 2, 1), v["L0_ffn_w2"].transpose(0, 2, 1)
    a["router1"] = np.concatenate([v["L1_ffn_router_w"], v["L1_ffn_actor_w1"]]).T
    a["ab1"], a["ab2"], a["aw2"] = v["L1_ffn_actor_b1"], v["L1_ffn_actor_b2"], v["L1_ffn_actor_w2"].T
    a["gu1"] = np.concatenate([v["L1_ffn_gate_w"], v["L1_ffn_up_w"]], axis=1).transpose(0, 2, 1)
    a["dn1"] = v["L1_ffn_down_w"].transpose(0, 2, 1)
    return {k: np.ascontiguousarray(x) for k, x in a.items()}


def kernel(**inputs):
    import numpy as np
    import concourse.bacc as bacc
    from concourse.bass_utils import run_bass_kernel_spmd

    arrays = layouts({k: np.asarray(x) for k, x in inputs.items()})
    nc = bacc.Bacc("TRN2", target_bir_lowering=False, num_devices=1)
    aps = {k: nc.dram_tensor(f"in_{k}", x.shape, mybir.dt.from_np(x.dtype), kind="ExternalInput").ap()
           for k, x in arrays.items()}
    out = nc.dram_tensor("out", (T + P, D), F32, kind="ExternalOutput").ap()
    build(nc, aps, out)
    r = run_bass_kernel_spmd(nc, [{f"in_{k}": x for k, x in arrays.items()}], core_ids=[0])
    return r.results[0]["out"][:T].reshape(B, S, D)
```
